# Optimizing a Trainium2 kernel written in Bass

```python
import numpy as np
import jax
import jax.numpy as jnp

def _softmax(x, axis=-1):
    return jax.nn.softmax(x, axis=axis)

def _gelu(x):
    return jax.nn.gelu(x, approximate=True)

def _silu(x):
    return jax.nn.silu(x)

def _sigmoid(x):
    return jax.nn.sigmoid(x)

def _layernorm(x, axis=-1, eps=1e-05):
    m = jnp.mean(x, axis=axis, keepdims=True)
    v = jnp.var(x, axis=axis, keepdims=True)
    return (x - m) / jnp.sqrt(v + eps)

def _scatter_add(tgt, idx, src, axis=0):
    return tgt.at[idx].add(src)

def _segment_sum(src, seg, n):
    return jax.ops.segment_sum(src, seg, n)
kernel_name = 'mk_gps_d1_gnn_r8_34b063'

def setup_inputs(seed: int=0):
    np.random.seed(seed)
    _w = jnp.asarray

    def _rec_inputs():
        import jax
        import jax.numpy as jnp
        _gk = jax.random.key(seed)
        x = -0.0002117 + 1 * jax.random.normal(jax.random.fold_in(_gk, 1), (6250, 256), jnp.float32)
        _s = jax.random.randint(jax.random.fold_in(_gk, 2), (100000,), 0, 6250, jnp.int32)
        _d = jax.random.randint(jax.random.fold_in(_gk, 3), (100000,), 0, 6250, jnp.int32)
        _loop = jnp.arange(6250, dtype=jnp.int32)
        src = jnp.concatenate([_s, _d, _loop])
        dst = jnp.concatenate([_d, _s, _loop])
        _o = jnp.argsort(dst, stable=True)
        src = src[_o]
        dst = dst[_o]
        return (x, src, dst)
    x, src, dst = _rec_inputs()

    def _L0_gnn_setup():
        import jax, jax.numpy as jnp
        import numpy as np
        N_NODES = 12500
        N_EDGES = 400000
        IN_FEAT = 256
        OUT_FEAT = 256
        EPS = 1e-12
        key = jax.random.key(seed)
        k1, k2, k3, k4, k5 = jax.random.split(key, 5)
        x = jax.random.normal(k1, (N_NODES, IN_FEAT), dtype=jnp.float32)
        W = jax.random.normal(k2, (IN_FEAT, OUT_FEAT), dtype=jnp.float32) / np.sqrt(IN_FEAT)
        b = jax.random.normal(k3, (OUT_FEAT,), dtype=jnp.float32) * 0.01
        src = jax.random.randint(k4, (N_EDGES,), 0, N_NODES, dtype=jnp.int32)
        dst = jax.random.randint(k5, (N_EDGES,), 0, N_NODES, dtype=jnp.int32)
        return {'x': x, 'W': W, 'b': b, 'src': src, 'dst': dst}
    _L0_gnn_all = _L0_gnn_setup()
    _L0_gnn_in = {k: v for k, v in _L0_gnn_all.items() if k in ('W', 'b')}
    del _L0_gnn_all

    def _L0_mix_setup():
        import jax, jax.numpy as jnp
        import numpy as np
        HEADS, DIM_HEAD = (8, 64)
        EPS = 1e-05

        def instance_norm(t):
            mu = jnp.mean(t, axis=-1, keepdims=True)
            var = jnp.mean((t - mu) ** 2, axis=-1, keepdims=True)
            return (t - mu) * jax.lax.rsqrt(var + EPS)
        key = jax.random.key(seed)
        k1, k2, k3, k4 = jax.random.split(key, 4)
        B, N, D = (8, 1024, 256)
        inner = HEADS * DIM_HEAD
        x = jax.random.normal(k1, (B, N, D), jnp.float32)
        w_qkv = jax.random.normal(k2, (3 * inner, D), jnp.float32) / np.sqrt(D).astype(np.float32)
        w_out = jax.random.normal(k3, (D, inner), jnp.float32) / np.sqrt(inner).astype(np.float32)
        b_out = 0.01 * jax.random.normal(k4, (D,), jnp.float32)
        return {'x': x, 'w_qkv': w_qkv, 'w_out': w_out, 'b_out': b_out}
    _L0_mix_all = _L0_mix_setup()
    _L0_mix_in = {k: v for k, v in _L0_mix_all.items() if k in ('w_qkv', 'w_out', 'b_out')}
    del _L0_mix_all

    def _L0_ffn_setup():
        import math
        import jax, jax.numpy as jnp
        import numpy as np
        CAPACITY_FACTOR = 1.25
        key = jax.random.key(seed)
        ks = jax.random.split(key, 5)
        B, L, D, F, E = (8, 1024, 256, 1024, 8)
        h = jax.random.normal(ks[0], (B, L, D), dtype=jnp.float32)
        gate_w = jax.random.normal(ks[1], (D, E), dtype=jnp.float32) * 0.02
        gate_b = jnp.zeros((E,), dtype=jnp.float32)
        w1 = jax.random.normal(ks[2], (E, D, F), dtype=jnp.float32) * (1.0 / math.sqrt(D))
        b1 = jnp.zeros((E, F), dtype=jnp.float32)
        w2 = jax.random.normal(ks[3], (E, F, D), dtype=jnp.float32) * (1.0 / math.sqrt(F))
        b2 = jnp.zeros((E, D), dtype=jnp.float32)
        return {'h': h, 'gate_w': gate_w, 'gate_b': gate_b, 'w1': w1, 'b1': b1, 'w2': w2, 'b2': b2}
    _L0_ffn_all = _L0_ffn_setup()
    _L0_ffn_in = {k: v for k, v in _L0_ffn_all.items() if k in ('gate_w', 'gate_b', 'w1', 'b1', 'w2', 'b2')}
    del _L0_ffn_all
    return {'x': x, 'src': src, 'dst': dst, 'L0_gnn_W': _L0_gnn_in['W'], 'L0_gnn_b': _L0_gnn_in['b'], 'L0_mix_w_qkv': _L0_mix_in['w_qkv'], 'L0_mix_w_out': _L0_mix_in['w_out'], 'L0_mix_b_out': _L0_mix_in['b_out'], 'L0_ffn_gate_w': _L0_ffn_in['gate_w'], 'L0_ffn_gate_b': _L0_ffn_in['gate_b'], 'L0_ffn_w1': _L0_ffn_in['w1'], 'L0_ffn_b1': _L0_ffn_in['b1'], 'L0_ffn_w2': _L0_ffn_in['w2'], 'L0_ffn_b2': _L0_ffn_in['b2']}

def reference(x, src, dst, L0_gnn_W, L0_gnn_b, L0_mix_w_qkv, L0_mix_w_out, L0_mix_b_out, L0_ffn_gate_w, L0_ffn_gate_b, L0_ffn_w1, L0_ffn_b1, L0_ffn_w2, L0_ffn_b2):
    import jax
    import jax.numpy as jnp

    def _L0_gnn_ref(x, W, b, src, dst):
        import jax, jax.numpy as jnp
        import numpy as np
        N_NODES = 12500
        N_EDGES = 400000
        IN_FEAT = 256
        OUT_FEAT = 256
        EPS = 1e-12
        N = x.shape[0]
        ones = jnp.ones(src.shape[0], dtype=x.dtype)
        deg_out = jnp.maximum(jax.ops.segment_sum(ones, src, num_segments=N), 1.0)
        deg_in = jnp.maximum(jax.ops.segment_sum(ones, dst, num_segments=N), 1.0)
        h = x * jax.lax.rsqrt(deg_out)[:, None]
        agg = jax.ops.segment_sum(h[src], dst, num_segments=N)
        h = agg * jax.lax.rsqrt(deg_in)[:, None]
        h = h @ W + b
        h = jax.nn.relu(h)
        nrm = jnp.maximum(jnp.linalg.norm(h, axis=1, keepdims=True), EPS)
        return h / nrm

    def _L0_mix_ref(x, w_qkv, w_out, b_out):
        import jax, jax.numpy as jnp
        import numpy as np
        HEADS, DIM_HEAD = (8, 64)
        EPS = 1e-05

        def instance_norm(t):
            mu = jnp.mean(t, axis=-1, keepdims=True)
            var = jnp.mean((t - mu) ** 2, axis=-1, keepdims=True)
            return (t - mu) * jax.lax.rsqrt(var + EPS)
        B, N, _ = x.shape
        H, Dh = (HEADS, DIM_HEAD)
        qkv = jnp.einsum('bnd,ed->bne', x, w_qkv)
        q, k, v = jnp.split(qkv, 3, axis=-1)

        def to_heads(t):
            return t.reshape(B, N, H, Dh).transpose(0, 2, 1, 3)
        q, k, v = (to_heads(q), to_heads(k), to_heads(v))
        k = instance_norm(k)
        v = instance_norm(v)
        dots = jnp.einsum('bhnd,bhne->bhde', k, v)
        out = jnp.einsum('bhnd,bhde->bhne', q, dots) / N
        out = out.transpose(0, 2, 1, 3).reshape(B, N, H * Dh)
        return jnp.einsum('bne,de->bnd', out, w_out) + b_out

    def _L0_ffn_ref(h, gate_w, gate_b, w1, b1, w2, b2):
        import math
        import jax, jax.numpy as jnp
        import numpy as np
        CAPACITY_FACTOR = 1.25
        B, L, D = h.shape
        E = gate_w.shape[1]
        T = B * L
        C = max(1, math.ceil(CAPACITY_FACTOR * T / E))
        x = h.reshape(T, D)
        logits = x @ gate_w + gate_b
        probs = jax.nn.softmax(logits, axis=-1)
        idx = jnp.argmax(probs, axis=-1)
        prb = jnp.take_along_axis(probs, idx[:, None], axis=1)[:, 0]
        one_hot = jax.nn.one_hot(idx, E, dtype=jnp.float32)
        pos = (jnp.cumsum(one_hot, axis=0) * one_hot).sum(-1).astype(jnp.int32) - 1
        kept = pos < C
        pos_safe = jnp.where(kept, pos, C)
        buf = jnp.zeros((E, C, D), dtype=h.dtype).at[idx, pos_safe].set(x, mode='drop')
        hmid = jax.nn.relu(jnp.einsum('ecd,edf->ecf', buf, w1) + b1[:, None, :])
        ybuf = jnp.einsum('ecf,efd->ecd', hmid, w2) + b2[:, None, :]
        pos_g = jnp.minimum(pos, C - 1)
        y_tok = ybuf[idx, pos_g] * (prb * kept)[:, None]
        y = y_tok.reshape(B, L, D)
        y = jnp.nan_to_num(y, nan=0.0, posinf=10000.0, neginf=-10000.0)
        return y
    xn = _layernorm(x, axis=-1)
    x = x + _L0_gnn_ref(xn, L0_gnn_W, L0_gnn_b, src, dst) + _L0_mix_ref(xn[None], L0_mix_w_qkv, L0_mix_w_out, L0_mix_b_out)[0]
    x = x + _L0_ffn_ref(_layernorm(x, axis=-1)[None], L0_ffn_gate_w, L0_ffn_gate_b, L0_ffn_w1, L0_ffn_b1, L0_ffn_w2, L0_ffn_b2)[0]
    return x

_drawn_inputs = setup_inputs


def setup_inputs(seed=0):
    import zlib

    import numpy as np

    out = dict(_drawn_inputs(seed))
    spreads = {'L0_ffn_gate_b': (0.0, 0.1), 'L0_ffn_b1': (0.0, 0.691), 'L0_ffn_b2': (0.0, 0.488)}
    factors = {'L0_gnn_b': 8.0, 'L0_mix_b_out': 4.807}
    for name, (base, spread) in spreads.items():
        noise = np.random.default_rng([zlib.crc32(name.encode()), seed]).standard_normal(out[name].shape)
        drawn = base * np.exp(spread * noise) if base else spread * noise
        out[name] = jnp.asarray(drawn.astype(out[name].dtype))
    for name, factor in factors.items():
        out[name] = (out[name] * factor).astype(out[name].dtype)
    return out
```

```python
import concourse.bass as bass
import numpy as np
from concourse import mybir
from contextlib import ExitStack

F32 = mybir.dt.float32
F16 = mybir.dt.float16
I32 = mybir.dt.int32
ALU = mybir.AluOpType
ACT = mybir.ActivationFunctionType
AX = mybir.AxisListType

P = 128
N = 6250
D = 256
DC = D // P
E = 206250
NB = -(-N // P)
NPAD = NB * P
LAST = N - (NB - 1) * P
UT = 4
RING = 8
EROWS = E // P
EREST = E - EROWS * P
HT = 16
HS = -(-E // (P * HT))
NT = HS * HT
NU = NT // UT
ECH = -(-NT // P)
H = 8
DH = 64
INNER = H * DH
IC = INNER // P
NE = 8
FF = 1024
FC = FF // P
CAP = -(-5 * N // (4 * NE))
CT = -(-CAP // P)
CROWS = CT * P
CLAST = CAP - (CT - 1) * P
HSCALE = 2048.0
GW = 2 * D + 1
TOKW = 2 * D + 1
KV_A = 12
EPS = 1e-5
LN_AT = 30
FIN_STEPS = 24
Y_STEPS = 4


def build(nc, x, src, dst, gnn_w, gnn_b, w_qkv, w_out, b_out, gate_w, gate_b, w1, b1, w2, b2, out):
    ctx = ExitStack()

    def sb(name, shape, dt=F32):
        return ctx.enter_context(nc.sbuf_tensor(name, shape, dt))

    def sem(name):
        return ctx.enter_context(nc.semaphore(name))

    def dram(name, shape, dt=F32):
        return nc.dram_tensor(name, shape, dt, kind="Internal").ap()

    h_rows = dram("h_rows", (NPAD, 2 * D), F16)
    xn_rows = dram("xn_rows", (NPAD, D))
    xnT_rows = dram("xnT_rows", (NPAD, D))
    tok_rows = dram("tok_rows", (NPAD, TOKW))

    reg_a = sb("reg_a", [P, NB * (D + 1)])
    reg_b = sb("reg_b", [P, NB * D])
    reg_c = sb("reg_c", [P, 8960])
    reg_e = sb("reg_e", [P, 4416])

    xn_all = reg_a[:, 0:NB * D].rearrange("p (t d) -> p t d", t=NB)
    agg_all = reg_a[:, :].rearrange("p (t d) -> p t d", t=NB)
    hidT = reg_a[:, 0:FC * CROWS].rearrange("p (f n) -> p f n", f=FC)

    h_all = reg_b[:, :].bitcast(F16).rearrange("p (t d) -> p t d", t=NB)
    W1N = DC * FF
    w1_sb = [reg_b[:, k * W1N:(k + 1) * W1N].rearrange("p (c f) -> p c f", c=DC) for k in range(2)]
    W2N = FC * D
    w2_sb = [reg_b[:, 2 * W1N + k * W2N:2 * W1N + (k + 1) * W2N].rearrange("p (c f) -> p c f", c=FC)
             for k in range(2)]
    GXN = CT * TOKW
    gx0 = 2 * W1N + 2 * W2N
    gx = [reg_b[:, gx0:gx0 + GXN].rearrange("p (c d) -> p c d", c=CT),
          reg_c[:, 0:GXN].rearrange("p (c d) -> p c d", c=CT)]

    EN = ECH * P
    src_raw = reg_c[:, 0:EN].rearrange("p (c j) -> p c j", c=ECH)
    dst_raw = reg_c[:, EN:2 * EN].rearrange("p (c j) -> p c j", c=ECH)
    o = 2 * EN
    lo16 = reg_c[:, o:o + EN // 2].bitcast(F16)
    hi16 = reg_c[:, o + EN // 2:o + EN].bitcast(F16)
    o += EN
    iota_e = reg_c[:, o:o + P * HT // 2].bitcast(F16).rearrange("p (j t) -> p j t", t=HT)
    o += P * HT // 2
    oh_lo, oh_hi = [], []
    for _ in range(2):
        oh_lo.append(reg_c[:, o:o + P * HT // 2].bitcast(F16).rearrange("p (j t) -> p j t", t=HT))
        o += P * HT // 2
        oh_hi.append(reg_c[:, o:o + NB * HT // 2].bitcast(F16).rearrange("p (j t) -> p j t", t=HT))
        o += NB * HT // 2
    assert o <= 8960
    ring = reg_c[:, 0:RING * UT * (GW + 1) // 2].bitcast(F16).rearrange("p (t d) -> p t d", d=GW + 1)
    xT = reg_c[:, GXN:GXN + DC * CROWS].rearrange("p (c n) -> p c n", c=DC)
    o = GXN + DC * CROWS
    y_sb = reg_c[:, o:o + D]
    y_cl = reg_c[:, o + D:o + 2 * D]
    y_df = reg_c[:, o + 2 * D:o + 3 * D]
    y_mask = reg_c[:, o + 3 * D:o + 4 * D].bitcast(I32)
    y_nan = reg_c[:, o + 4 * D:o + 5 * D].bitcast(I32)
    y_out = [reg_c[:, o + (5 + k) * D:o + (6 + k) * D] for k in range(2)]
    assert o + 7 * D <= 8960

    wkv_nat = reg_e[:, 0:2048].rearrange("p (c d) -> p c d", c=8)
    wout_nat = reg_e[:, 2048:3072].rearrange("p (c d) -> p c d", c=DC)
    b1_nat = reg_e[0:NE * FC, 3072:3200]
    kv_mean = reg_e[:, 3200:3232]
    ln_junk = reg_e[:, 3584:3840]
    sq = reg_e[:, 0:1024]
    r_sb = reg_e[:, 0:1024].rearrange("p (c d) -> p c d", c=IC)
    k_sb = reg_e[:, 1024:1536]
    v_sb = reg_e[:, 1536:2048]
    bd_sb = reg_e[:, 1024:1536].rearrange("p (c d) -> p c d", c=IC)
    agg_s = reg_e[:, 2048:2304]
    aggT = reg_e[:, 2304:2560]
    relu_h = reg_e[:, 2560:2816]
    sq_junk = reg_e[:, 2816:3072]
    mixed = reg_e[:, 3072:3328]
    tok_t = reg_e[:, 3328:3328 + TOKW]
    xn2T = reg_e[:, 3844:4100]
    cl_hot = reg_e[:, 4100:4228]
    hi_tok = reg_e[:, 4228:4292]
    tiny = reg_e[:, 4292:4416]

    src_idx = sb("src_idx", [P, EN], I32)
    dst_f = sb("dst_f", [P, EN])
    idx_ring = [sb(f"idx_ring{k}", [P, RING * UT], I32) for k in range(2)]
    dst_rel = sb("dst_rel", [P, 2, UT], F16)
    S = sb("S", [P, 2, P * UT], F16)
    blk_base = sb("blk_base", [P, 1])
    iota_4 = sb("iota_4", [P, P, UT], F16)
    ident = sb("ident", [P, P])
    utri = sb("utri", [P, P])
    ones = sb("ones", [P, P])
    zeros16 = sb("zeros16", [1, 512], F16)
    zeros32 = sb("zeros32", [P, D])
    iota_128 = sb("iota_128", [P, P])
    iota_64 = sb("iota_64", [P, NE * CT])
    iota_8 = sb("iota_8", [P, NE])
    rev_8 = sb("rev_8", [P, NE])
    node_1 = sb("node_1", [P, 1])
    block_edge = sb("block_edge", [64, 1])
    valid = sb("valid", [P, 1])
    eps = sb("eps", [P, 1])
    first_u = sb("first_u", [1, 64], I32)
    t0_col = sb("t0_col", [64, 1])
    ln_sum = sb("ln_sum", [P, NB])
    ln_nm = sb("ln_nm", [P, NB])
    ln_sq = sb("ln_sq", [P, NB])
    ln_sd = sb("ln_sd", [P, NB])
    ln_rs = sb("ln_rs", [P, NB])
    ln_nb = sb("ln_nb", [P, NB])
    deg = sb("deg", [P, NB])
    deg_sd = sb("deg_sd", [P, NB])
    deg_rs = sb("deg_rs", [P, NB])
    wkvT = sb("wkvT", [P, DC, 2 * INNER])
    wq = sb("wq", [P, IC, D])
    woutT = sb("woutT", [P, IC, D])
    mix_m = sb("mix_m", [P, DC, D])
    gnn_w_sb = sb("gnn_w_sb", [P, DC, D])
    gate_w_sb = sb("gate_w_sb", [P, DC, NE])
    gnn_b_row = sb("gnn_b_row", [1, D])
    b_out_row = sb("b_out_row", [1, D])
    gate_b_row = sb("gate_b_row", [1, NE])
    b1_cols = sb("b1_cols", [P, NE * FC])
    b2_row = [sb(f"b2_row{k}", [1, D]) for k in range(2)]
    xn_t = sb("xn_t", [P, D])
    xnT_t = sb("xnT_t", [P, D])
    x_t = sb("x_t", [P, D])
    oh_sum = sb("oh_sum", [P, NE])
    inv_i = sb("inv_i", [P, NE * CT], I32)
    inv_f = sb("inv_f", [P, NE * CT])
    inv_m = sb("inv_m", [P, NE * CT])
    tok_idx = [sb(f"tok_idx{k}", [P, CT], I32) for k in range(2)]

    names = iter(range(124))

    def small(n=1):
        a = next(names)
        for _ in range(n - 1):
            next(names)
        return tiny[:, a:a + n]

    kv_var, kv_sd, kv_rs, kv_sc = small(16), small(16), small(16), small(8)
    f_deg, f_sd, f_rin, f_ss, f_nr, f_rn, f_sd2, f_rstd = (small() for _ in range(8))
    f_bn, f_mv, f_nmx, f_sum, f_m1, f_pos, f_drop, f_slot = small(6), small(2), *(small() for _ in range(6))
    f_hot, f_cum, f_exp, f_log, f_cl, f_hi = small(8), small(8), small(8), small(8), small(), small()
    f_slot_i, f_cl_i, f_hi_i = (small().bitcast(I32) for _ in range(3))

    bank = [ctx.enter_context(nc.psum_tensor(f"bank{k}", [P, 512], F32)) for k in range(8)]
    agg_ps = bank[0][:, 0:D + 1]
    kv_ps = bank[1:3]
    dots_ps = bank[3]
    tp_ps = bank[4]
    m_ps = bank[5]
    gate_ps = bank[6][:, 0:NE]
    cum_ps = bank[6][:, 64:64 + NE]
    inv_ps = bank[7][:, 0:NE * CT]
    hist_ps = bank[7][:, 0:NB]
    g_ps, mix_ps = bank[1][:, 0:D], bank[2][:, 0:D]

    src_in, dst_in, pads_set = sem("src_in"), sem("dst_in"), sem("pads_set")
    consts, x_in, w_in, pool_c = sem("consts"), [sem(f"x_in{g}") for g in range(5)], sem("w_in"), sem("pool_c")
    w_in2 = sem("w_in2")
    edges_f, edges_T, idx_set, dst_set = sem("edges_f"), sem("edges_T"), sem("idx_set"), sem("dst_set")
    bounds_b, bounds_c, bounds_T, bounds_set = (sem(n) for n in ("bounds_b", "bounds_c", "bounds_T", "bounds_set"))
    wT_ready, wT_out = sem("wT_ready"), sem("wT_out")
    hot_ready, hot_used, hist_done = sem("hot_ready"), sem("hot_used"), sem("hist_done")
    deg_set, deg_rt, deg_ok = sem("deg_set"), sem("deg_rt"), sem("deg_ok")
    ln_act, ln_var, ln_rec, ln_bias, xn_set = (sem(n) for n in ("ln_act", "ln_var", "ln_rec", "ln_bias", "xn_set"))
    xn_out, h_hi, h_lo, h_out = sem("xn_out"), sem("h_hi"), sem("h_lo"), sem("h_out")
    dve_pre, wkv_set = sem("dve_pre"), sem("wkv_set")
    ring_ones, passed = sem("ring_ones"), sem("passed")
    idx_next, base_set, kv_v = sem("idx_next"), sem("base_set"), sem("kv_v")
    rows_in = [sem(f"rows_in{k}") for k in range(RING)]
    rows_landed, units_used = sem("rows_landed"), sem("units_used")
    rel_set, hots_ready, hots_used = sem("rel_set"), sem("hots_ready"), sem("hots_used")
    agg_done, agg_out = sem("agg_done"), sem("agg_out")
    xn_ld, kvT_ready, kvT_out, xnT_st = sem("xn_ld"), sem("kvT_ready"), sem("kvT_out"), sem("xnT_st")
    kv_ready, kv_sq, k_out, kv_dve, kv_root, v_out, dots_done = (
        sem(n) for n in ("kv_ready", "kv_sq", "k_out", "kv_dve", "kv_root", "v_out", "dots_done"))
    bd_zero, bd_set, r_ready, r_out, m_ready, m_out = (
        sem(n) for n in ("bd_zero", "bd_set", "r_ready", "r_out", "m_ready", "m_out"))
    x_ld, xT_ld = sem("x_ld"), sem("xT_ld")
    fin_dve, fin_deg, fin_sd, fin_aggs, fin_aggT, fin_aggT_out = (
        sem(n) for n in ("fin_dve", "fin_deg", "fin_sd", "fin_aggs", "fin_aggT", "fin_aggT_out"))
    fin_g, fin_mix, fin_relu, fin_ss, fin_nr, fin_var, fin_sd2, fin_xn2, fin_xn2T, fin_xn2T_out = (
        sem(n) for n in ("fin_g", "fin_mix", "fin_relu", "fin_ss", "fin_nr", "fin_var", "fin_sd2", "fin_xn2",
                         "fin_xn2T", "fin_xn2T_out"))
    fin_gate, fin_nmx, fin_exp, fin_hot, fin_cum, fin_slot, fin_inv, fin_prb, tok_st, out_st = (
        sem(n) for n in ("fin_gate", "fin_nmx", "fin_exp", "fin_hot", "fin_cum", "fin_slot", "fin_inv", "fin_prb",
                         "tok_st", "out_st"))
    inv_set, inv_dve, gx_zero, ti_set = sem("inv_set"), sem("inv_dve"), sem("gx_zero"), sem("ti_set")
    gx_in = [sem(f"gx_in{k}") for k in range(2)]
    wexp_in = [sem(f"wexp_in{k}") for k in range(2)]
    xT_ready, xT_out, up_ready, up_out, down_ready, y_read, y_dve, y_ready = (
        sem(n) for n in ("xT_ready", "xT_out", "up_ready", "up_out", "down_ready", "y_read", "y_dve", "y_ready"))
    y_st = [sem(f"y_st{k}") for k in range(2)]

    ds = bass.ds
    XG = [(12 * g, 12) for g in range(4)]

    def main_phase(eng, gnn, kv, mix, fin):
        with eng.Fori(0, KV_A) as i:
            gnn(i)
            for c in range(4):
                kv(i * 4 + c)
        kv(NB - 1)
        mix()
        with eng.Fori(0, KV_A) as j:
            gnn(j + KV_A)
            fin(j * 2, False)
            fin(j * 2 + 1, False)
        with eng.Fori(2 * KV_A, NB - 2) as b:
            gnn(b)
            fin(b, False)
        gnn(NB - 2)
        fin(NB - 2, False)
        gnn(NB - 1)
        fin(NB - 1, True)

    def apart(eng):
        eng.sem_inc(passed, 1)

    def each_expert(eng, expert):
        for k in range(2):
            expert(k, k)
        with eng.Fori(1, NE // 2) as i:
            for k in range(2):
                expert(i * 2 + k, k)

    def pair(e, k):
        return e // 2 + 1 if isinstance(e, int) else (e - k + 2) // 2

    block = ctx.enter_context(nc.Block())

    @block.sync
    def _(sp):
        full = ECH - 1
        rest = EROWS - full * P
        sp.dma_start(src_raw[:, 0:full, :].bitcast(I32),
                     src[0:full * P * P].rearrange("(c p j) -> p c j", p=P, j=P)).then_inc(src_in, 16)
        sp.dma_start(dst_raw[:, 0:full, :].bitcast(I32),
                     dst[0:full * P * P].rearrange("(c p j) -> p c j", p=P, j=P)).then_inc(dst_in, 16)
        sp.wait_ge(pads_set, 3)
        for raw, edges, landed in ((src_raw, src, src_in), (dst_raw, dst, dst_in)):
            sp.dma_start(raw[0:rest, full, :].bitcast(I32),
                         edges[full * P * P:EROWS * P].rearrange("(p j) -> p j", j=P)).then_inc(landed, 16)
            sp.dma_start(raw[rest:rest + 1, full, 0:EREST].bitcast(I32),
                         edges[EROWS * P:E].rearrange("(p j) -> p j", p=1)).then_inc(landed, 16)
        wv = w_qkv.rearrange("(c p) d -> p c d", p=P)
        sp.dma_start(wkv_nat, wv[:, IC:3 * IC, :]).then_inc(w_in, 16)
        sp.dma_start(wout_nat, w_out.rearrange("(c p) d -> p c d", p=P)).then_inc(w_in, 16)
        sp.dma_start(b1_nat, b1.rearrange("e (f p) -> (e f) p", p=P)).then_inc(w_in, 16)
        for g, (t, n) in enumerate(XG):
            sp.dma_start(xn_all[:, t:t + n, :],
                         x[t * P:(t + n) * P, :].rearrange("(t p) d -> p t d", p=P)).then_inc(x_in[g], 16)
        sp.dma_start(xn_all[0:LAST, NB - 1, :], x[(NB - 1) * P:N, :]).then_inc(x_in[4], 16)
        sp.dma_start(wq[:, :, :], wv[:, 0:IC, :]).then_inc(w_in2, 16)
        sp.dma_start(gnn_w_sb[:, :, :], gnn_w.rearrange("(c p) d -> p c d", p=P)).then_inc(w_in2, 16)
        sp.dma_start(gate_w_sb[:, :, :], gate_w.rearrange("(c p) d -> p c d", p=P)).then_inc(w_in2, 16)
        sp.dma_start(gnn_b_row[:, :], gnn_b.rearrange("(a d) -> a d", a=1)).then_inc(w_in2, 16)
        sp.dma_start(b_out_row[:, :], b_out.rearrange("(a d) -> a d", a=1)).then_inc(w_in2, 16)
        sp.dma_start(gate_b_row[:, :], gate_b.rearrange("(a d) -> a d", a=1)).then_inc(w_in2, 16)
        for g, (t, n) in enumerate([*XG, (NB - 1, 1)]):
            sp.wait_ge(xn_set, t + n)
            sp.dma_start(xn_rows[t * P:(t + n) * P, :].rearrange("(t p) d -> p t d", p=P),
                         xn_all[:, t:t + n, :]).then_inc(xn_out, 16)
        for g, (t, n) in enumerate([*XG, (NB - 1, 1)]):
            sp.wait_ge(h_lo, t + n)
            sp.dma_start(h_rows[t * P:(t + n) * P, :].rearrange("(t p) d -> p t d", p=P),
                         h_all[:, t:t + n, :]).then_inc(h_out, 16)
        sp.wait_ge(h_out, 16 * 5)

        def load_expert(e, k):
            sp.dma_start(w1_sb[k], w1[ds(e, 1), :, :].rearrange("e (c p) f -> p (e c) f", p=P)).then_inc(wexp_in[k], 16)
            sp.dma_start(w2_sb[k], w2[ds(e, 1), :, :].rearrange("e (c p) f -> p (e c) f", p=P)).then_inc(wexp_in[k], 16)
            sp.dma_start(b2_row[k][:, :], b2[ds(e, 1), :]).then_inc(wexp_in[k], 16)

        load_expert(0, 0)
        load_expert(1, 1)

        def landed(i, k):
            sp.wait_ge(rows_in[k], (i + 1) * (16 * UT))
            sp.sem_inc(rows_landed, 1)

        with sp.Fori(0, NU // RING) as i:
            for k in range(RING):
                landed(i, k)
        for k in range(NU % RING):
            landed(NU // RING, k)
        with sp.Fori(0, NE // 2 - 1) as i:
            for k in range(2):
                sp.wait_ge(down_ready, (i * 2 + k + 1) * CT)
                load_expert(i * 2 + 2 + k, k)
        sp.wait_ge(xn_out, 16 * 5)
        sp.wait_ge(xnT_st, 16 * NB)
        sp.wait_ge(tok_st, 16 * NB)
        sp.wait_ge(out_st, 16 * NB)
        for k in range(2):
            sp.wait_ge(y_st[k], 16 * NE * CT // 2)

    @block.gpsimd
    def _(pool):
        g = nc.gpsimd
        g.memset(src_raw[:, ECH - 1, :].bitcast(I32), NPAD - 1).then_inc(pads_set, 1)
        g.memset(dst_raw[:, ECH - 1, :].bitcast(I32), NPAD - 1).then_inc(pads_set, 1)
        g.memset(xn_all[:, NB - 1, :], 0.0).then_inc(pads_set, 1)
        g.memset(ident[:, :], 0.0).then_inc(pool_c, 1)
        g.memset(utri[:, :], 0.0).then_inc(pool_c, 1)
        g.memset(valid[:, :], 1.0).then_inc(pool_c, 1)
        pool.wait_ge(pool_c, 3)
        g.affine_select(out=ident[:, :], in_=ident[:, :], compare_op=ALU.not_equal, fill=1.0, base=0,
                        pattern=[[-1, P]], channel_multiplier=1).then_inc(consts, 1)
        g.affine_select(out=utri[:, :], in_=utri[:, :], compare_op=ALU.is_gt, fill=1.0, base=0,
                        pattern=[[-1, P]], channel_multiplier=1).then_inc(consts, 1)
        g.affine_select(out=valid[:, :], in_=valid[:, :], compare_op=ALU.is_gt, fill=0.0, base=LAST,
                        pattern=[[0, 1]], channel_multiplier=-1).then_inc(consts, 1)
        g.iota(iota_e, pattern=[[1, P], [0, HT]], base=0, channel_multiplier=0,
               allow_small_or_imprecise_dtypes=True).then_inc(consts, 1)
        g.iota(iota_4[:, :, :], pattern=[[1, P], [0, UT]], base=0, channel_multiplier=0,
               allow_small_or_imprecise_dtypes=True).then_inc(consts, 1)
        g.iota(iota_128[:, :], pattern=[[1, P]], base=0, channel_multiplier=0,
               allow_small_or_imprecise_dtypes=True).then_inc(consts, 1)
        g.iota(iota_64[:, :], pattern=[[1, NE * CT]], base=0, channel_multiplier=0,
               allow_small_or_imprecise_dtypes=True).then_inc(consts, 1)
        g.iota(iota_8[:, :], pattern=[[1, NE]], base=0, channel_multiplier=0,
               allow_small_or_imprecise_dtypes=True).then_inc(consts, 1)
        g.iota(rev_8[:, :], pattern=[[-1, NE]], base=NE, channel_multiplier=0,
               allow_small_or_imprecise_dtypes=True).then_inc(consts, 1)
        g.iota(node_1[:, :], pattern=[[0, 1]], base=1, channel_multiplier=1,
               allow_small_or_imprecise_dtypes=True).then_inc(consts, 1)
        g.iota(block_edge[:, :], pattern=[[0, 1]], base=0, channel_multiplier=P,
               allow_small_or_imprecise_dtypes=True).then_inc(consts, 1)
        g.memset(ones[:, :], 1.0).then_inc(consts, 1)
        g.memset(zeros16[:, :], 0.0).then_inc(consts, 1)
        g.memset(zeros32[:, :], 0.0).then_inc(consts, 1)
        g.memset(eps[:, :], EPS).then_inc(consts, 1)
        g.memset(oh_sum[:, :], 0.0).then_inc(consts, 1)

        pool.wait_ge(idx_set, 1)
        g.tensor_copy(idx_ring[0][:, :], src_idx[:, 0:RING * UT]).then_inc(idx_next, 1)
        pool.wait_ge(hist_done, 1)
        g.memset(ring[:, :, 2 * D:2 * D + 1], 1.0).then_inc(ring_ones, 1)
        pool.wait_ge(h_out, 16 * 5)

        def unit(k, r, u):
            pool.wait_ge(units_used, u + 1)
            apart(pool)
            for j in range(UT):
                t = k * UT + j
                g.indirect_dma_start(out=ring[:, t, 0:2 * D], out_offset=None, in_=h_rows[:, :],
                                     in_offset=bass.IndirectOffsetOnAxis(ap=idx_ring[r][:, t:t + 1], axis=0)
                                     ).then_inc(rows_in[k], 16)

        with pool.Fori(0, NU // RING // 2) as i:
            for r in range(2):
                pool.wait_ge(idx_next, i * 2 + r + 1)
                for k in range(RING):
                    unit(k, r, i * (2 * RING) + r * RING + k)
                g.tensor_copy(idx_ring[1 - r][:, :],
                              src_idx[:, ds(i * (2 * RING * UT) + (r + 1) * RING * UT, RING * UT)]).then_inc(idx_next, 1)
        done = NU // RING // 2 * 2
        pool.wait_ge(idx_next, done + 1)
        for k in range(NU % RING):
            unit(k, 0, done * RING + k)

        pool.wait_ge(inv_set, 1)
        pool.wait_ge(gx_zero, 2)
        pool.wait_ge(tok_st, 16 * NB)
        pool.wait_ge(out_st, 16 * NB)

        def take(e, k):
            g.tensor_copy(tok_idx[k][:, :], inv_i[:, ds(e * CT, CT)]).then_inc(ti_set, 1)
            pool.wait_ge(ti_set, e + 1)
            apart(pool)
            for c in range(CT):
                g.indirect_dma_start(out=gx[k][:, c, :], out_offset=None, in_=tok_rows[:, :],
                                     in_offset=bass.IndirectOffsetOnAxis(ap=tok_idx[k][:, c:c + 1], axis=0),
                                     bounds_check=N - 1, oob_is_err=False).then_inc(gx_in[k], 16)

        def give(e, k):
            for c in range(CT):
                pool.wait_ge(y_ready, e * CT + c + 1)
                apart(pool)
                g.indirect_dma_start(out=out[:, :],
                                     out_offset=bass.IndirectOffsetOnAxis(ap=tok_idx[k][:, c:c + 1], axis=0),
                                     in_=y_out[c % 2], in_offset=None,
                                     bounds_check=N - 1, oob_is_err=False).then_inc(y_st[c % 2], 16)

        take(0, 0)
        with pool.Fori(0, NE // 2 - 1) as i:
            take(i * 2 + 1, 1)
            give(i * 2, 0)
            pool.wait_ge(y_st[0], (i * 2 + 1) * (16 * CT // 2))
            pool.wait_ge(y_st[1], (i * 2 + 1) * (16 * CT // 2))
            take(i * 2 + 2, 0)
            give(i * 2 + 1, 1)
            pool.wait_ge(y_st[0], (i * 2 + 2) * (16 * CT // 2))
            pool.wait_ge(y_st[1], (i * 2 + 2) * (16 * CT // 2))
        take(NE - 1, 1)
        give(NE - 2, 0)
        give(NE - 1, 1)

    @block.scalar
    def _(act):
        a = nc.scalar
        n_act = [0]

        def link(ins):
            n_act[0] += 1
            ins.then_inc(ln_act, 1)
            act.wait_ge(ln_act, n_act[0])

        act.sem_inc(agg_out, 1)
        for n in range(7):
            act.wait_ge(wT_ready, n + 1)
            if n < 4:
                for m in range(2):
                    for c in range(DC):
                        ins = a.activation(wkvT[:, c, (2 * n + m) * P:(2 * n + m + 1) * P],
                                           bank[n % 4][:, (2 * m + c) * P:(2 * m + c + 1) * P], ACT.Copy)
            elif n < 6:
                ins = a.activation(woutT[:, :, (n - 4) * P:(n - 3) * P],
                                   bank[n % 4][:, :].rearrange("p (c d) -> p c d", c=IC), ACT.Copy)
            else:
                ins = a.activation(b1_cols[:, :], bank[n % 4][:, 0:NE * FC], ACT.Copy)
            ins.then_inc(wT_out, 1)
        act.wait_ge(consts, 16)
        for g, (t0, n) in enumerate([*XG, (NB - 1, 1)]):
            act.wait_ge(x_in[g], 16)
            for t in range(t0, t0 + n):
                link(a.activation(ln_junk, xn_all[:, t, :], ACT.Copy, accum_out=ln_sum[:, t:t + 1]))
        link(a.mul(ln_nm[:, :], ln_sum[:, :], -1.0 / D))
        for t in range(NB):
            link(a.activation(ln_junk, xn_all[:, t, :], ACT.Square, bias=ln_nm[:, t:t + 1],
                              accum_out=ln_sq[:, t:t + 1]))
        a.activation(ln_sd[:, :], ln_sq[:, :], ACT.Sqrt, bias=eps[:, :], scale=1.0 / D).then_inc(ln_var, 1)
        act.wait_ge(ln_bias, 1)
        for t in range(NB):
            a.activation(xn_all[:, t, :], xn_all[:, t, :], ACT.Identity, bias=ln_nb[:, t:t + 1],
                         scale=ln_rs[:, t:t + 1]).then_inc(xn_set, 1)
        act.wait_ge(deg_set, 1)
        a.activation(deg_sd[:, :], deg[:, :], ACT.Sqrt, scale=HSCALE ** -2).then_inc(deg_rt, 1)
        act.wait_ge(deg_ok, 1)
        act.wait_ge(xn_set, NB)
        for t in range(NB):
            a.activation(h_all[:, t, 0:D], xn_all[:, t, :], ACT.Copy, scale=deg_rs[:, t:t + 1]).then_inc(h_hi, 1)
        act.wait_ge(xn_out, 16 * 5)
        act.wait_ge(h_lo, NB)
        act.dma_start(xn_t[:, :], xn_rows[0:P, :]).then_inc(xn_ld, 16)

        def gnn(b):
            act.wait_ge(agg_done, b + 1)
            apart(act)
            a.activation(agg_all[:, ds(b, 1), :].rearrange("p a d -> p (a d)"), agg_ps, ACT.Copy).then_inc(agg_out, 1)

        def kv(t):
            act.wait_ge(kvT_ready, t + 1)
            a.activation(xnT_t[:, :], tp_ps[:, 0:D], ACT.Copy).then_inc(kvT_out, 1)
            act.wait_ge(kvT_out, t + 1)
            act.dma_start(xnT_rows[ds(t * P, P), :], xnT_t[:, :]).then_inc(xnT_st, 16)
            if not isinstance(t, int):
                act.dma_start(xn_t[:, :], xn_rows[ds(t * P + P, P), :]).then_inc(xn_ld, 16)
            act.wait_ge(kv_ready, t + 1)
            for m in range(2):
                ins = a.activation(sq[:, m * INNER:(m + 1) * INNER], kv_ps[m][:, :], ACT.Square)
            ins.then_inc(kv_sq, 1)
            act.wait_ge(dots_done, t + 1)
            a.activation(k_sb, kv_ps[0][:, :], ACT.Copy).then_inc(k_out, 1)
            act.wait_ge(kv_dve, t + 1)
            a.activation(kv_sd, kv_var, ACT.Sqrt, bias=eps[:, :], scale=1.0 / DH).then_inc(kv_root, 1)
            act.wait_ge(xnT_st, (t + 1) * 16)

        def load_block(b, last):
            if last:
                act.dma_start(x_t[0:LAST, :], x[(NB - 1) * P:N, :]).then_inc(x_ld, 16)
            else:
                act.dma_start(x_t[:, :], x[ds(b * P, P), :]).then_inc(x_ld, 16)
            act.dma_start(xnT_t[:, :], xnT_rows[ds(b * P, P), :]).then_inc(xT_ld, 16)

        def mix():
            act.wait_ge(r_ready, 1)
            for m in range(2):
                ins = a.activation(r_sb[:, 2 * m:2 * m + 2, :].rearrange("p c d -> p (c d)"), kv_ps[m][:, :],
                                   ACT.Copy, scale=1.0 / N)
            ins.then_inc(r_out, 1)
            act.wait_ge(m_ready, 1)
            a.activation(mix_m[:, :, :].rearrange("p c d -> p (c d)"), m_ps[:, :], ACT.Copy).then_inc(m_out, 1)
            act.wait_ge(xnT_st, 16 * NB)
            load_block(0, False)

        def fin(b, last):
            act.wait_ge(fin_deg, b + 1)
            a.activation(f_sd, f_deg, ACT.Sqrt, scale=HSCALE ** 2).then_inc(fin_sd, 1)
            act.wait_ge(fin_aggT, b + 1)
            a.activation(aggT, tp_ps[:, 0:D], ACT.Copy).then_inc(fin_aggT_out, 1)
            act.wait_ge(fin_g, b + 1)
            a.activation(relu_h, g_ps, ACT.Relu).then_inc(fin_relu, 1)
            act.wait_ge(fin_relu, b + 1)
            a.activation(sq_junk, relu_h, ACT.Square, accum_out=f_ss).then_inc(fin_ss, 1)
            act.wait_ge(fin_ss, b + 1)
            a.activation(f_nr, f_ss, ACT.Sqrt).then_inc(fin_nr, 1)
            act.wait_ge(fin_var, b + 1)
            a.activation(f_sd2, f_mv[:, 1:2], ACT.Sqrt, bias=eps[:, :]).then_inc(fin_sd2, 1)
            act.wait_ge(fin_xn2T, b + 1)
            a.activation(xn2T, tp_ps[:, D:2 * D], ACT.Copy).then_inc(fin_xn2T_out, 1)
            act.wait_ge(fin_nmx, b + 1)
            a.activation(f_exp, f_log, ACT.Exp, bias=f_nmx, accum_out=f_sum).then_inc(fin_exp, 1)
            if not last:
                load_block(b + 1, isinstance(b, int) and b + 1 == NB - 1)
            act.wait_ge(fin_prb, b + 1)
            act.dma_start(tok_rows[ds(b * P, P), :], tok_t).then_inc(tok_st, 16)
            if last:
                act.dma_start(out[(NB - 1) * P:N, :], tok_t[0:LAST, D:2 * D]).then_inc(out_st, 16)
            else:
                act.dma_start(out[ds(b * P, P), :], tok_t[:, D:2 * D]).then_inc(out_st, 16)
            act.wait_ge(tok_st, (b + 1) * 16)
            act.wait_ge(out_st, (b + 1) * 16)

        main_phase(act, gnn, kv, mix, fin)

        def expert(e, k):
            if not isinstance(e, int) or e > 0:
                act.wait_ge(down_ready, e * CT)
            for m in range(2):
                w = min(512, CAP - m * 512)
                for f in range(FC):
                    act.wait_ge(up_ready, e * (2 * FC) + m * FC + f + 1)
                    apart(act)
                    a.activation(hidT[:, f, m * 512:m * 512 + w], bank[f % 4][:, 0:w], ACT.Relu,
                                 bias=b1_cols[:, ds(e * FC + f, 1)]).then_inc(up_out, 1)

        each_expert(act, expert)

    @block.tensor
    def _(pe):
        t_ = nc.tensor

        def transpose2(out_ps, rows):
            for c in range(DC):
                ins = t_.transpose(out_ps[:, c * P:(c + 1) * P], rows[:, c * P:(c + 1) * P], ident[:, :])
            return ins

        pe.wait_ge(consts, 16)
        for n, (raw, first) in enumerate(((src_raw, 0), (dst_raw, 4))):
            pe.wait_ge(edges_f, n + 1)
            for c in range(ECH):
                ins = t_.transpose(bank[first + c // 4][:, c % 4 * P:(c % 4 + 1) * P], raw[:, c, :], ident[:, :])
            ins.then_inc(edges_T, 1)
        pe.wait_ge(dst_set, 1)
        t_.matmul(bank[4][0:64, 0:NU - 1], ones[0:1, 0:64], dst_f[0:1, UT:NT:UT], start=True, stop=True
                  ).then_inc(bounds_b, 1)
        pe.wait_ge(bounds_c, 2)
        t_.matmul(bank[5][0:1, 0:64], t0_col[:, :], ident[0:64, 0:64], start=True, stop=True).then_inc(bounds_T, 1)
        pe.wait_ge(idx_set, 1)
        pe.wait_ge(w_in, 48)
        for n in range(7):
            if n >= 4:
                pe.wait_ge(wT_out, n - 3)
            if n < 4:
                for m in range(2):
                    ins = transpose2(bank[n][:, 2 * m * P:(2 * m + 2) * P], wkv_nat[:, 2 * n + m, :])
            elif n < 6:
                for c in range(IC):
                    ins = t_.transpose(bank[n % 4][:, c * P:(c + 1) * P], wout_nat[:, n - 4, c * P:(c + 1) * P], ident[:, :])
            else:
                ins = t_.transpose(bank[n % 4][:, 0:NE * FC], b1_nat, ident[0:NE * FC, 0:NE * FC])
            ins.then_inc(wT_ready, 1)
        t_.matmul(hist_ps, zeros16[:, 0:P], zeros16[:, 0:NB], start=True, stop=False).then_inc(hot_used, 2)

        def hist(s, k, last=False):
            pe.wait_ge(hot_ready, s + 1)
            for t in range(HT):
                ins = t_.matmul(hist_ps, oh_lo[k][:, :, t], oh_hi[k][:, :, t], start=False,
                                stop=last and t == HT - 1)
            ins.then_inc(hist_done if last else hot_used, 1)

        with pe.Fori(0, HS // 2) as i:
            for k in range(2):
                hist(i * 2 + k, k)
        hist(HS - 1, 0, True)

        pe.sem_inc(units_used, RING)
        pe.sem_inc(hots_used, 2)
        pe.wait_ge(ring_ones, 1)
        pe.wait_ge(w_in2, 16 * 6)
        pe.wait_ge(wkv_set, 1)
        pe.wait_ge(deg_set, 1)
        t_.matmul(inv_ps, zeros16[:, 0:P], zeros16[:, 0:NE * CT], start=True, stop=False)
        t_.matmul(dots_ps[:, :], zeros16[:, 0:P], zeros16[:, 0:512], start=True, stop=False).then_inc(dots_done, 1)

        def visit(u, v, closing):
            pe.wait_ge(rows_landed, u + 1)
            pe.wait_ge(hots_ready, v + 1)
            slot, hot = pe.snap((u % RING) * (UT * (GW + 1))), pe.snap((v % 2) * (P * UT))
            S_v = S[:, :, :].rearrange("p a b -> p (a b)")
            rows = ring.rearrange("p t d -> p (t d)")
            for j in range(UT):
                left = S_v[:, ds(hot, P * UT)].rearrange("p (n j) -> p n j", j=UT)[:, :, j]
                last = closing and j == UT - 1
                base = slot + j * (GW + 1)
                t_.matmul(agg_ps[:, 0:D], left, rows[:, ds(base, D)], start=False, stop=False)
                ins = t_.matmul(agg_ps, left, rows[:, ds(base + D, D + 1)], start=False, stop=last)
            ins.then_inc(hots_used, 1)
            return ins

        def gnn(b):
            u0 = pe.value_load(first_u[0:1, ds(b, 1)], min_val=0, max_val=NU - 1)
            u1 = pe.value_load(first_u[0:1, ds(b + 1, 1)], min_val=0, max_val=NU - 1)
            pe.wait_ge(agg_out, b + 1)
            t_.matmul(agg_ps, zeros16[:, 0:P], zeros16[:, 0:D + 1], start=True, stop=False)
            with pe.If(u0 < u1):
                with pe.Fori(u0, u1) as u:
                    visit(u, u + b, False)
                    pe.wait_ge(hots_used, u + b + 3)
                    pe.sem_inc(units_used, 1)
            visit(u1, u1 + b, True)
            pe.wait_ge(hots_used, u1 + b + 3)
            pe.sem_inc(agg_done, 1)

        def kv(t):
            pe.wait_ge(xn_ld, (t + 1) * 16)
            transpose2(tp_ps, xn_t).then_inc(kvT_ready, 1)
            pe.wait_ge(kvT_out, t + 1)
            for m in range(2):
                for c in range(DC):
                    ins = t_.matmul(kv_ps[m][:, :], xnT_t[:, c * P:(c + 1) * P],
                                    wkvT[:, c, m * INNER:(m + 1) * INNER], start=(c == 0), stop=(c == DC - 1))
            ins.then_inc(kv_ready, 1)
            pe.wait_ge(k_out, t + 1)
            pe.wait_ge(v_out, t + 1)
            last = isinstance(t, int)
            for c in range(IC):
                ins = t_.matmul(dots_ps[:, c * P:(c + 1) * P], v_sb[:, c * P:(c + 1) * P],
                                k_sb[:, c * P:(c + 1) * P], start=False, stop=last and c == IC - 1)
            ins.then_inc(dots_done, 1)

        def mix():
            pe.wait_ge(bd_set, 1)
            for c in range(IC):
                ins = t_.matmul(kv_ps[c // 2][:, c % 2 * D:(c % 2 + 1) * D], bd_sb[:, c, :], woutT[:, c, :],
                                start=True, stop=True)
            ins.then_inc(r_ready, 1)
            pe.wait_ge(r_out, 1)
            for d in range(DC):
                for c in range(IC):
                    ins = t_.matmul(m_ps[:, d * D:(d + 1) * D], wq[:, c, d * P:(d + 1) * P], r_sb[:, c, :],
                                    start=(c == 0), stop=(c == IC - 1))
            ins.then_inc(m_ready, 1)
            pe.wait_ge(m_out, 1)

        def fin(b, last):
            pe.wait_ge(xT_ld, (b + 1) * 16)
            t_.matmul(mix_ps, ones[0:1, :], b_out_row[:, :], start=True, stop=False)
            for c in range(DC):
                ins = t_.matmul(mix_ps, xnT_t[:, c * P:(c + 1) * P], mix_m[:, c, :], start=False, stop=(c == DC - 1))
            ins.then_inc(fin_mix, 1)
            pe.wait_ge(fin_aggs, b + 1)
            transpose2(tp_ps, agg_s).then_inc(fin_aggT, 1)
            t_.matmul(g_ps, ones[0:1, :], gnn_b_row[:, :], start=True, stop=False)
            pe.wait_ge(fin_aggT_out, b + 1)
            for c in range(DC):
                ins = t_.matmul(g_ps, aggT[:, c * P:(c + 1) * P], gnn_w_sb[:, c, :], start=False, stop=(c == DC - 1))
            ins.then_inc(fin_g, 1)
            pe.wait_ge(fin_xn2, b + 1)
            transpose2(tp_ps[:, D:2 * D], tok_t).then_inc(fin_xn2T, 1)
            t_.matmul(gate_ps, ones[0:1, :], gate_b_row[:, :], start=True, stop=False)
            pe.wait_ge(fin_xn2T_out, b + 1)
            for c in range(DC):
                ins = t_.matmul(gate_ps, xn2T[:, c * P:(c + 1) * P], gate_w_sb[:, c, :], start=False, stop=(c == DC - 1))
            ins.then_inc(fin_gate, 1)
            pe.wait_ge(fin_hot, b + 1)
            t_.matmul(cum_ps, utri[:, :], f_hot, start=True, stop=False)
            t_.matmul(cum_ps, ones[:, :], oh_sum[:, :], start=False, stop=True).then_inc(fin_cum, 1)
            pe.wait_ge(fin_slot, b + 1)
            t_.matmul(inv_ps, cl_hot, hi_tok, start=False, stop=last).then_inc(fin_inv, 1)

        main_phase(pe, gnn, kv, mix, fin)

        def expert(e, k):
            for c in range(CT):
                n = e * CT + c
                if c == 0:
                    pe.wait_ge(gx_in[k], pair(e, k) * (16 * CT))
                if not isinstance(n, int) or n >= 2:
                    pe.wait_ge(xT_out, n - 1)
                transpose2(bank[6 + c % 2], gx[k][:, c, 0:D]).then_inc(xT_ready, 1)
            pe.wait_ge(xT_out, e * CT + CT)
            pe.wait_ge(wexp_in[k], pair(e, k) * 48)
            for m in range(2):
                w = min(512, CAP - m * 512)
                for f in range(FC):
                    n = e * (2 * FC) + m * FC + f
                    if not isinstance(n, int) or n >= 4:
                        pe.wait_ge(up_out, n - 3)
                    for c in range(DC):
                        ins = t_.matmul(bank[f % 4][:, 0:w], w1_sb[k][:, c, f * P:(f + 1) * P],
                                        xT[:, c, m * 512:m * 512 + w], start=(c == 0), stop=(c == DC - 1))
                    ins.then_inc(up_ready, 1)
            for c in range(CT):
                w = min(P, CAP - c * P)
                pe.wait_ge(up_out, e * (2 * FC) + ((c * P + w - 1) // 512 + 1) * FC)
                n = e * CT + c
                if not isinstance(n, int) or n >= 2:
                    pe.wait_ge(y_read, n - 1)
                y_ps = bank[4 + c % 2][0:w, 0:D]
                t_.matmul(y_ps, ones[0:1, 0:w], b2_row[k][:, :], start=True, stop=False)
                for f in range(FC):
                    ins = t_.matmul(y_ps, hidT[:, f, c * P:c * P + w], w2_sb[k][:, f, :], start=False, stop=(f == FC - 1))
                ins.then_inc(down_ready, 1)

        each_expert(pe, expert)

    @block.vector
    def _(dve):
        v_ = nc.vector
        n_pre = [0]

        def link(ins):
            n_pre[0] += 1
            ins.then_inc(dve_pre, 1)
            dve.wait_ge(dve_pre, n_pre[0])

        v_.memset(blk_base[:, :], 0.0).then_inc(base_set, 1)
        dve.wait_ge(src_in, 48)
        v_.tensor_copy(src_raw, src_raw.bitcast(I32)).then_inc(edges_f, 1)
        dve.wait_ge(dst_in, 48)
        v_.tensor_copy(dst_raw, dst_raw.bitcast(I32)).then_inc(edges_f, 1)
        for n, (to, first, landed) in enumerate(((src_idx, 0, idx_set), (dst_f, 4, dst_set))):
            dve.wait_ge(edges_T, n + 1)
            for q in range(4):
                w = min(512, EN - q * 512)
                ins = v_.tensor_copy(to[:, q * 512:q * 512 + w], bank[first + q][:, 0:w])
            ins.then_inc(landed, 1)
        dve.wait_ge(consts, 16)
        dve.wait_ge(bounds_b, 1)
        before = reg_e[0:64, 3840:3840 + NU - 1]
        v_.tensor_scalar(before, bank[4][0:64, 0:NU - 1], block_edge[:, :], None, ALU.is_lt).then_inc(bounds_c, 1)
        dve.wait_ge(bounds_c, 1)
        v_.tensor_reduce(out=t0_col[:, :], in_=before, op=ALU.add, axis=AX.X).then_inc(bounds_c, 1)
        dve.wait_ge(idx_set, 1)
        lo_i, hi_i = (raw.rearrange("p c j -> p (c j)").bitcast(I32) for raw in (src_raw, dst_raw))
        v_.tensor_scalar(lo_i, src_idx[:, :], P - 1, None, ALU.bitwise_and)
        link(v_.tensor_scalar(hi_i, src_idx[:, :], 7, None, ALU.logical_shift_right))
        v_.tensor_copy(lo16, lo_i)
        link(v_.tensor_copy(hi16, hi_i))
        dve.wait_ge(bounds_T, 1)
        v_.tensor_copy(first_u[:, :], bank[5][0:1, 0:64]).then_inc(bounds_set, 1)

        def hot(s, k):
            dve.wait_ge(hot_used, s + 1)
            v_.tensor_tensor(oh_lo[k], iota_e, lo16[:, ds(s * HT, HT)].unsqueeze(1).to_broadcast([P, P, HT]), ALU.is_equal)
            v_.tensor_tensor(oh_hi[k], iota_e[:, 0:NB, :], hi16[:, ds(s * HT, HT)].unsqueeze(1).to_broadcast([P, NB, HT]),
                             ALU.is_equal).then_inc(hot_ready, 1)

        with dve.Fori(0, LN_AT) as i:
            for k in range(2):
                hot(i * 2 + k, k)
        dve.wait_ge(ln_var, 1)
        link(v_.reciprocal(ln_rs[:, :], ln_sd[:, :]))
        v_.tensor_tensor(ln_nb[:, :], ln_nm[:, :], ln_rs[:, :], ALU.mult).then_inc(ln_bias, 1)
        with dve.Fori(LN_AT, HS // 2) as i:
            for k in range(2):
                hot(i * 2 + k, k)
        hot(HS - 1, 0)
        dve.wait_ge(hist_done, 1)
        v_.tensor_scalar(deg[:, :], hist_ps, 1.0, None, ALU.max).then_inc(deg_set, 1)
        dve.wait_ge(deg_rt, 1)
        v_.reciprocal(deg_rs[:, :], deg_sd[:, :]).then_inc(deg_ok, 1)
        dve.wait_ge(deg_ok, 1)
        for t in range(NB):
            dve.wait_ge(h_hi, t + 1)
            v_.scalar_tensor_tensor(h_all[:, t, D:2 * D], xn_all[:, t, :], deg_rs[:, t:t + 1], h_all[:, t, 0:D],
                                    ALU.mult, ALU.subtract).then_inc(h_lo, 1)
        dve.wait_ge(wT_out, 4)
        groups = wkvT[:, :, :].rearrange("p c (h d) -> p (c h) d", d=DH)
        link(v_.tensor_reduce(out=kv_mean, in_=groups, op=ALU.add, axis=AX.X))
        link(v_.tensor_scalar(kv_mean, kv_mean, 1.0 / DH, None, ALU.mult))
        v_.tensor_tensor(groups, groups, kv_mean.unsqueeze(2).to_broadcast([P, 2 * DC * H, DH]), ALU.subtract
                         ).then_inc(wkv_set, 1)
        dve.wait_ge(bounds_set, 1)

        def visit(u, v):
            slot = dve.snap(v % 2)
            dve.wait_ge(hots_used, v + 1)
            rel = dst_rel[:, ds(slot, 1), :].rearrange("p a t -> p (a t)")
            v_.tensor_scalar(rel, dst_f[:, ds(u * UT, UT)], blk_base[:, :], None, ALU.subtract).then_inc(rel_set, 1)
            dve.wait_ge(rel_set, v + 1)
            v_.tensor_tensor(S[:, ds(slot, 1), :].rearrange("p a (n j) -> p (a n) j", j=UT), iota_4[:, :, :],
                             rel.unsqueeze(1).to_broadcast([P, P, UT]), ALU.is_equal).then_inc(hots_ready, 1)

        def gnn(b):
            u0 = dve.value_load(first_u[0:1, ds(b, 1)], min_val=0, max_val=NU - 1)
            u1 = dve.value_load(first_u[0:1, ds(b + 1, 1)], min_val=0, max_val=NU - 1)
            dve.wait_ge(base_set, b + 1)
            apart(dve)
            with dve.If(u0 < u1):
                with dve.Fori(u0, u1) as u:
                    visit(u, u + b)
            visit(u1, u1 + b)
            v_.tensor_scalar(blk_base[:, :], blk_base[:, :], float(P), None, ALU.add).then_inc(base_set, 1)

        def kv(t):
            dve.wait_ge(kv_sq, t + 1)
            v_.tensor_reduce(out=kv_var, in_=sq.rearrange("p (g d) -> p g d", d=DH), op=ALU.add, axis=AX.X
                             ).then_inc(kv_dve, 1)
            dve.wait_ge(kv_root, t + 1)
            v_.reciprocal(kv_rs, kv_sd).then_inc(kv_v, 1)
            dve.wait_ge(kv_v, t * 2 + 1)
            v_.tensor_tensor(kv_sc, kv_rs[:, 0:H], kv_rs[:, H:2 * H], ALU.mult).then_inc(kv_v, 1)
            dve.wait_ge(kv_v, t * 2 + 2)
            dve.wait_ge(dots_done, t + 1)
            v_.tensor_tensor(v_sb.rearrange("p (h d) -> p h d", d=DH), kv_ps[1][:, :].rearrange("p (h d) -> p h d", d=DH),
                             kv_sc.unsqueeze(2).to_broadcast([P, H, DH]), ALU.mult).then_inc(v_out, 1)

        def mix():
            dve.wait_ge(dots_done, NB + 1)
            v_.memset(bd_sb, 0.0).then_inc(bd_zero, 1)
            dve.wait_ge(bd_zero, 1)
            for half in range(2):
                r = slice(half * DH, (half + 1) * DH)
                ins = v_.tensor_copy(bd_sb[r, :, r], dots_ps[r, :].rearrange("p (c d) -> p c d", c=IC)[:, :, r])
            ins.then_inc(bd_set, 1)

        def fin(b, last):
            n = [0]

            def step(ins):
                n[0] += 1
                ins.then_inc(fin_dve, 1)
                dve.wait_ge(fin_dve, b * FIN_STEPS + n[0])

            def then(ins, signal):
                ins.then_inc(signal, 1)
                dve.wait_ge(signal, b + 1)

            agg = agg_all[:, ds(b, 1), :].rearrange("p a d -> p (a d)")
            dve.wait_ge(agg_out, b + 2)
            v_.tensor_scalar(f_deg, agg[:, D:D + 1], 1.0, None, ALU.max).then_inc(fin_deg, 1)
            dve.wait_ge(fin_sd, b + 1)
            step(v_.reciprocal(f_rin, f_sd))
            v_.tensor_scalar(agg_s, agg[:, 0:D], f_rin, None, ALU.mult).then_inc(fin_aggs, 1)
            dve.wait_ge(x_ld, (b + 1) * 16)
            dve.wait_ge(fin_mix, b + 1)
            step(v_.tensor_tensor(mixed, x_t[:, :], mix_ps, ALU.add))
            dve.wait_ge(fin_nr, b + 1)
            step(v_.tensor_scalar(f_nr, f_nr, 1e-12, None, ALU.max))
            step(v_.reciprocal(f_rn, f_nr))
            step(v_.scalar_tensor_tensor(tok_t[:, D:2 * D], relu_h, f_rn, mixed, ALU.mult, ALU.add))
            step(v_.bn_stats(f_bn, tok_t[:, D:2 * D]))
            apart(dve)
            then(v_.bn_aggr(f_mv, f_bn), fin_var)
            dve.wait_ge(fin_sd2, b + 1)
            step(v_.reciprocal(f_rstd, f_sd2))
            v_.tensor_scalar(tok_t[:, 0:D], tok_t[:, D:2 * D], f_mv[:, 0:1], f_rstd, ALU.subtract, ALU.mult
                             ).then_inc(fin_xn2, 1)
            dve.wait_ge(fin_gate, b + 1)
            step(v_.tensor_copy(f_log, gate_ps))
            then(v_.tensor_reduce(out=f_nmx, in_=f_log, op=ALU.max, axis=AX.X, negate=True), fin_nmx)
            step(v_.tensor_scalar(f_cum, f_log, f_nmx, 0.0, ALU.add, ALU.is_equal))
            step(v_.tensor_tensor(f_cum, f_cum, rev_8[:, :], ALU.mult))
            step(v_.tensor_reduce(out=f_m1, in_=f_cum, op=ALU.max, axis=AX.X))
            if last:
                step(v_.tensor_scalar(f_hot, rev_8[:, :], f_m1, valid[:, :], ALU.is_equal, ALU.mult))
                ins = v_.tensor_copy(f_drop, valid[:, :])
            else:
                ins = v_.tensor_scalar(f_hot, rev_8[:, :], f_m1, None, ALU.is_equal)
            ins.then_inc(fin_hot, 1)
            dve.wait_ge(fin_cum, b + 1)
            step(v_.tensor_tensor(f_cum, cum_ps, f_hot, ALU.mult))
            step(v_.tensor_tensor(oh_sum[:, :], oh_sum[:, :], f_hot, ALU.add))
            step(v_.tensor_reduce(out=f_pos, in_=f_cum, op=ALU.add, axis=AX.X))
            step(v_.tensor_scalar(f_drop, f_pos, float(CAP), float(2 * NE * CROWS), ALU.is_gt, ALU.mult))
            step(v_.tensor_scalar(f_slot, f_m1, -float(CROWS), float(NE * CROWS - 1), ALU.mult, ALU.add))
            step(v_.tensor_tensor(f_slot, f_slot, f_pos, ALU.add))
            step(v_.tensor_tensor(f_slot_i, f_slot, f_drop, ALU.add))
            step(v_.tensor_scalar(f_cl_i, f_slot_i, P - 1, None, ALU.bitwise_and))
            step(v_.tensor_scalar(f_hi_i, f_slot_i, 7, None, ALU.arith_shift_right))
            step(v_.tensor_copy(f_cl, f_cl_i))
            step(v_.tensor_copy(f_hi, f_hi_i))
            step(v_.tensor_scalar(cl_hot, iota_128[:, :], f_cl, None, ALU.is_equal))
            if last:
                step(v_.tensor_tensor(node_1[:, :], node_1[:, :], valid[:, :], ALU.mult))
            v_.tensor_scalar(hi_tok, iota_64[:, :], f_hi, node_1[:, :], ALU.is_equal, ALU.mult).then_inc(fin_slot, 1)
            dve.wait_ge(fin_exp, b + 1)
            then(v_.reciprocal(tok_t[:, 2 * D:2 * D + 1], f_sum), fin_prb)
            dve.wait_ge(fin_inv, b + 1)
            step(v_.tensor_scalar(node_1[:, :], node_1[:, :], float(P), None, ALU.add))
            apart(dve)
            assert last or n[0] == FIN_STEPS, n

        main_phase(dve, gnn, kv, mix, fin)

        dve.wait_ge(fin_inv, NB)
        n = [0]

        def chain(ins):
            n[0] += 1
            ins.then_inc(inv_dve, 1)
            dve.wait_ge(inv_dve, n[0])

        chain(v_.tensor_scalar(inv_m[:, :], inv_ps, 0.0, float(2 * N), ALU.is_equal, ALU.mult))
        chain(v_.tensor_scalar(inv_f[:, :], inv_ps, -1.0, None, ALU.add))
        v_.tensor_tensor(inv_i[:, :], inv_f[:, :], inv_m[:, :], ALU.add).then_inc(inv_set, 1)
        dve.wait_ge(hots_used, NU - 1 + NB + 2)
        for k in range(2):
            v_.memset(gx[k], 0.0).then_inc(gx_zero, 1)
        for k in range(2):
            chain(v_.memset(y_out[k], 0.0))

        def expert(e, k):
            for c in range(CT):
                dve.wait_ge(xT_ready, e * CT + c + 1)
                v_.tensor_copy(xT[:, :, c * P:(c + 1) * P], bank[6 + c % 2][:, 0:D].rearrange("p (c n) -> p c n", c=DC)
                               ).then_inc(xT_out, 1)
            for c in range(CT):
                t = e * CT + c
                w = min(P, CAP - c * P)
                m = [0]

                def step(ins):
                    m[0] += 1
                    ins.then_inc(y_dve, 1)
                    dve.wait_ge(y_dve, t * Y_STEPS + m[0])

                row = gx[k][0:w, c, :]
                y, z, d, fine, nan = (b_[0:w, :] for b_ in (y_sb, y_cl, y_df, y_mask, y_nan))
                dve.wait_ge(down_ready, t + 1)
                v_.tensor_scalar(y, bank[4 + c % 2][0:w, 0:D], row[:, 2 * D:2 * D + 1], None, ALU.mult).then_inc(y_read, 1)
                dve.wait_ge(y_read, t + 1)
                v_.tensor_scalar(z, y, 1e4, -1e4, ALU.min, ALU.max)
                step(v_.tensor_tensor(d, y, y, ALU.subtract))
                v_.tensor_scalar(fine, d, 0.0, None, ALU.is_equal)
                step(v_.tensor_tensor(nan, y, y, ALU.not_equal))
                apart(dve)
                step(v_.copy_predicated(z, fine, y))
                apart(dve)
                step(v_.copy_predicated(z, nan, zeros32[0:w, :]))
                if c >= 2 or not isinstance(e, int) or e > 0:
                    dve.wait_ge(y_st[c % 2], t // 2 * 16 if isinstance(t, int) else e * (16 * CT // 2) + c // 2 * 16)
                v_.tensor_tensor(y_out[c % 2][0:w, :], z, row[:, D:2 * D], ALU.add).then_inc(y_ready, 1)

        each_expert(dve, expert)


_INS = ['x', 'src', 'dst', 'L0_gnn_W', 'L0_gnn_b', 'L0_mix_w_qkv', 'L0_mix_w_out', 'L0_mix_b_out',
        'L0_ffn_gate_w', 'L0_ffn_gate_b', 'L0_ffn_w1', 'L0_ffn_b1', 'L0_ffn_w2', 'L0_ffn_b2']


def kernel(**inputs):
    import numpy as _np
    import concourse.bacc as _bacc
    from concourse.bass_utils import run_bass_kernel_spmd as _run

    nc = _bacc.Bacc("TRN2", target_bir_lowering=False, num_devices=1)
    arrays, args = {}, []
    for name in _INS:
        a = _np.ascontiguousarray(inputs[name])
        arrays[f"in_{name}"] = a
        args.append(nc.dram_tensor(f"in_{name}", a.shape, mybir.dt.from_np(a.dtype), kind="ExternalInput").ap())
    args.append(nc.dram_tensor("out_0", (N, D), F32, kind="ExternalOutput").ap())
    build(nc, *args)
    r = _run(nc, [arrays], core_ids=[0])
    return r.results[0]["out_0"]
```

```python
import concourse.bass as bass
import numpy as np
from concourse import mybir
from contextlib import ExitStack

F32 = mybir.dt.float32
F16 = mybir.dt.float16
I32 = mybir.dt.int32
ALU = mybir.AluOpType
ACT = mybir.ActivationFunctionType
AX = mybir.AxisListType

P = 128
N = 6250
D = 256
DC = D // P
E = 206250
NB = -(-N // P)
NPAD = NB * P
LAST = N - (NB - 1) * P
UT = 4
RING = 8
EROWS = E // P
EREST = E - EROWS * P
HT = 16
HS = -(-E // (P * HT))
NT = HS * HT
NU = NT // UT
ECH = -(-NT // P)
H = 8
DH = 64
INNER = H * DH
IC = INNER // P
NE = 8
FF = 1024
FC = FF // P
CAP = -(-5 * N // (4 * NE))
CT = -(-CAP // P)
CROWS = CT * P
CLAST = CAP - (CT - 1) * P
HSCALE = 2048.0
GW = 2 * D + 1
TOKW = 2 * D
NQ = NB // 2
ROUTED = NB - 3
EPS = 1e-5
LN_AT = 30
FIN_STEPS = 7
Y_STEPS = 4


def build(nc, x, src, dst, gnn_w, gnn_b, w_qkv, w_out, b_out, gate_w, gate_b, w1, b1, w2, b2, out):
    ctx = ExitStack()

    def sb(name, shape, dt=F32):
        return ctx.enter_context(nc.sbuf_tensor(name, shape, dt))

    def sem(name):
        return ctx.enter_context(nc.semaphore(name))

    def dram(name, shape, dt=F32):
        return nc.dram_tensor(name, shape, dt, kind="Internal").ap()

    h_rows = dram("h_rows", (NPAD, 2 * D), F16)
    xn_rows = dram("xn_rows", (NPAD, D))
    xnT_rows = dram("xnT_rows", (NPAD, D))
    tok_rows = dram("tok_rows", (NPAD, TOKW))

    reg_a = sb("reg_a", [P, NB * (D + 1)])
    reg_b = sb("reg_b", [P, NB * D])
    reg_c = sb("reg_c", [P, 8960])
    reg_e = sb("reg_e", [P, 4416])

    xn_all = reg_a[:, 0:NB * D].rearrange("p (t d) -> p t d", t=NB)
    agg_all = reg_a[:, :].rearrange("p (t d) -> p t d", t=NB)
    hidT = reg_a[:, 0:FC * CROWS].rearrange("p (f n) -> p f n", f=FC)

    h_all = reg_b[:, :].bitcast(F16).rearrange("p (t d) -> p t d", t=NB)
    W1N = DC * FF
    w1_sb = [reg_b[:, k * W1N:(k + 1) * W1N].rearrange("p (c f) -> p c f", c=DC) for k in range(2)]
    W2N = FC * D
    w2_sb = [reg_b[:, 2 * W1N + k * W2N:2 * W1N + (k + 1) * W2N].rearrange("p (c f) -> p c f", c=FC)
             for k in range(2)]
    GXN = CT * TOKW
    gx0 = 2 * W1N + 2 * W2N
    gx = [reg_b[:, gx0:gx0 + GXN].rearrange("p (c d) -> p c d", c=CT),
          reg_c[:, 0:GXN].rearrange("p (c d) -> p c d", c=CT)]

    EN = ECH * P
    src_raw = reg_c[:, 0:EN].rearrange("p (c j) -> p c j", c=ECH)
    dst_raw = reg_c[:, EN:2 * EN].rearrange("p (c j) -> p c j", c=ECH)
    o = 2 * EN
    lo16 = reg_c[:, o:o + EN // 2].bitcast(F16)
    hi16 = reg_c[:, o + EN // 2:o + EN].bitcast(F16)
    o += EN
    iota_e = reg_c[:, o:o + P * HT // 2].bitcast(F16).rearrange("p (j t) -> p j t", t=HT)
    o += P * HT // 2
    oh_lo, oh_hi = [], []
    for _ in range(2):
        oh_lo.append(reg_c[:, o:o + P * HT // 2].bitcast(F16).rearrange("p (j t) -> p j t", t=HT))
        o += P * HT // 2
        oh_hi.append(reg_c[:, o:o + NB * HT // 2].bitcast(F16).rearrange("p (j t) -> p j t", t=HT))
        o += NB * HT // 2
    assert o <= 8960
    ring = reg_c[:, 0:RING * UT * (GW + 1) // 2].bitcast(F16).rearrange("p (t d) -> p t d", d=GW + 1)
    xT = reg_c[:, GXN:GXN + DC * CROWS].rearrange("p (c n) -> p c n", c=DC)
    o = GXN + DC * CROWS
    y_sb = reg_c[:, o:o + D]
    y_cl = reg_c[:, o + D:o + 2 * D]
    y_df = reg_c[:, o + 2 * D:o + 3 * D]
    y_mask = reg_c[:, o + 3 * D:o + 4 * D].bitcast(I32)
    y_nan = reg_c[:, o + 4 * D:o + 5 * D].bitcast(I32)
    y_out = [reg_c[:, o + (5 + k) * D:o + (6 + k) * D] for k in range(2)]
    assert o + 7 * D <= 8960

    wkv_nat = reg_e[:, 0:2048].rearrange("p (c d) -> p c d", c=8)
    wout_nat = reg_e[:, 2048:3072].rearrange("p (c d) -> p c d", c=DC)
    b1_nat = reg_e[0:NE * FC, 3072:3200]
    kv_mean = reg_e[:, 3200:3232]
    ln_junk = reg_e[:, 3584:3840]
    sq = reg_e[:, 0:2048].rearrange("p (m d) -> p m d", m=2)
    k_sb = reg_e[:, 2048:3072].rearrange("p (m d) -> p m d", m=2)
    v_sb = reg_e[:, 3072:4096].rearrange("p (m d) -> p m d", m=2)
    r_sb = reg_e[:, 0:1024].rearrange("p (c d) -> p c d", c=IC)
    bd_sb = reg_e[:, 2048:2560].rearrange("p (c d) -> p c d", c=IC)
    agg_s, aggT, relu_h, mixed = (reg_e[:, k * 2 * D:(k + 1) * 2 * D].rearrange("p (m d) -> p m d", m=2)
                                  for k in range(4))
    tok_t = reg_e[:, 2048:2048 + 2 * TOKW].rearrange("p (m d) -> p m d", m=2)
    xn2T = reg_e[:, 3072:3584].rearrange("p (m d) -> p m d", m=2)
    sq_junk = [reg_e[:, 3584 + k * D:3584 + (k + 1) * D] for k in range(2)]
    tiny = reg_e[:, 4096:4416]

    src_idx = sb("src_idx", [P, EN], I32)
    dst_f = sb("dst_f", [P, EN])
    idx_ring = [sb(f"idx_ring{k}", [P, RING * UT], I32) for k in range(2)]
    dst_rel = sb("dst_rel", [P, 2, UT], F16)
    S = sb("S", [P, 2, P * UT], F16)
    blk_base = sb("blk_base", [P, 1])
    iota_4 = sb("iota_4", [P, P, UT], F16)
    ident = sb("ident", [P, P])
    utri = sb("utri", [P, P])
    ones = sb("ones", [P, P])
    zeros16 = sb("zeros16", [1, 512], F16)
    zeros32 = sb("zeros32", [P, D])
    iota_128 = sb("iota_128", [P, P])
    iota_64 = sb("iota_64", [P, NE * CT])
    rev_8 = sb("rev_8", [P, NE])
    node_1 = sb("node_1", [P, NB])
    block_edge = sb("block_edge", [64, 1])
    valid = sb("valid", [P, 1])
    eps = sb("eps", [P, 1])
    first_u = sb("first_u", [1, 64], I32)
    t0_col = sb("t0_col", [64, 1])
    ln_sum = sb("ln_sum", [P, NB])
    ln_nm = sb("ln_nm", [P, NB])
    ln_sq = sb("ln_sq", [P, NB])
    ln_sd = sb("ln_sd", [P, NB])
    ln_rs = sb("ln_rs", [P, NB])
    ln_nb = sb("ln_nb", [P, NB])
    deg = sb("deg", [P, NB])
    deg_sd = sb("deg_sd", [P, NB])
    deg_rs = sb("deg_rs", [P, NB])
    wkvT = sb("wkvT", [P, DC, 2 * INNER])
    wq = sb("wq", [P, IC, D])
    woutT = sb("woutT", [P, IC, D])
    mix_m = sb("mix_m", [P, DC, D])
    gnn_w_sb = sb("gnn_w_sb", [P, DC, D])
    gate_w_sb = sb("gate_w_sb", [P, DC, NE])
    gnn_b_row = sb("gnn_b_row", [1, D])
    b_out_row = sb("b_out_row", [1, D])
    gate_b_row = sb("gate_b_row", [1, NE])
    b1_cols = sb("b1_cols", [P, NE * FC])
    b2_row = [sb(f"b2_row{k}", [1, D]) for k in range(2)]
    xn_t = sb("xn_t", [P, 2, D])
    xnT_t = sb("xnT_t", [P, 2, D])
    x_t = sb("x_t", [P, 2, D])
    logits = sb("logits", [P, NB, NE])
    routed = sb("routed", [P, NE])
    slot_prb = sb("slot_prb", [P, NE * CT])
    inv_i = sb("inv_i", [P, NE * CT], I32)
    inv_f = sb("inv_f", [P, NE * CT])
    inv_m = sb("inv_m", [P, NE * CT])
    tok_idx = [sb(f"tok_idx{k}", [P, CT], I32) for k in range(2)]

    names = iter(range(320))

    def small(n=1):
        a = next(names)
        for _ in range(n - 1):
            next(names)
        return tiny[:, a:a + n]

    kv_var, kv_sd, kv_rs, kv_sc = small(32), small(32), small(32), small(16)
    f_deg, f_sd, f_rin, f_ss, f_nr, f_nc, f_rn, f_sd2, f_rstd = (small(2) for _ in range(9))
    f_bn = [small(6) for _ in range(2)]
    f_mv = small(4).rearrange("p (m s) -> p m s", s=2)

    per_e = [wkvT[:, :, :].rearrange("p c e -> p (c e)")[:, k * NB * NE:(k + 1) * NB * NE].rearrange(
        "p (t e) -> p t e", e=NE) for k in range(5)]
    per_t = [woutT[:, :, :].rearrange("p c e -> p (c e)")[:, k * NB:(k + 1) * NB] for k in range(13)]
    hots = wq[:, :, :].rearrange("p c e -> p (c e)")
    low_hot = [hots[:, k * P:(k + 1) * P] for k in range(2)]
    high_val = [hots[:, (2 + k) * P:(3 + k) * P] for k in range(2)]

    bank = [ctx.enter_context(nc.psum_tensor(f"bank{k}", [P, 512], F32)) for k in range(8)]
    agg_ps = bank[0][:, 0:D + 1]
    kv_ps = (bank[1:3], bank[5:7])
    dots_ps = bank[3]
    tp_ps = bank[4]
    m_ps = bank[5]
    xn2T_ps = bank[5]
    gate_ps = bank[6][:, 0:2 * NE].rearrange("p (m e) -> p m e", m=2)
    inv_ps = bank[7][:, 0:2 * NE * CT]
    hist_ps = bank[7][:, 0:NB]
    g_ps, mix_ps = (bank[k][:, :].rearrange("p (m d) -> p m d", m=2) for k in (1, 2))
    cum_ps, tot_ps = bank[1], bank[2]

    src_in, dst_in, pads_set = sem("src_in"), sem("dst_in"), sem("pads_set")
    consts, x_in, w_in, pool_c = sem("consts"), [sem(f"x_in{g}") for g in range(5)], sem("w_in"), sem("pool_c")
    w_in2 = sem("w_in2")
    edges_f, edges_T, idx_set, dst_set = sem("edges_f"), sem("edges_T"), sem("idx_set"), sem("dst_set")
    bounds_b, bounds_c, bounds_T, bounds_set = (sem(n) for n in ("bounds_b", "bounds_c", "bounds_T", "bounds_set"))
    wT_ready, wT_out = sem("wT_ready"), sem("wT_out")
    hot_ready, hot_used, hist_done = sem("hot_ready"), sem("hot_used"), sem("hist_done")
    deg_set, deg_rt, deg_ok = sem("deg_set"), sem("deg_rt"), sem("deg_ok")
    ln_act, ln_var, ln_rec, ln_bias, xn_set = (sem(n) for n in ("ln_act", "ln_var", "ln_rec", "ln_bias", "xn_set"))
    xn_out, h_hi, h_lo, h_out = sem("xn_out"), sem("h_hi"), sem("h_lo"), sem("h_out")
    dve_pre, wkv_set = sem("dve_pre"), sem("wkv_set")
    ring_ones, passed = sem("ring_ones"), sem("passed")
    idx_next, base_set, kv_v = sem("idx_next"), sem("base_set"), sem("kv_v")
    rows_in = [sem(f"rows_in{k}") for k in range(RING)]
    rows_landed, units_used = sem("rows_landed"), sem("units_used")
    rel_set, hots_ready, hots_used = sem("rel_set"), sem("hots_ready"), sem("hots_used")
    agg_done, agg_out = sem("agg_done"), sem("agg_out")
    xn_ld, kvT_ready, kvT_out, xnT_st = sem("xn_ld"), sem("kvT_ready"), sem("kvT_out"), sem("xnT_st")
    kv_ready, kv_sq, k_out, kv_dve, kv_root, v_out, dots_done = (
        sem(n) for n in ("kv_ready", "kv_sq", "k_out", "kv_dve", "kv_root", "v_out", "dots_done"))
    bd_zero, bd_set, r_ready, r_out, m_ready, m_out = (
        sem(n) for n in ("bd_zero", "bd_set", "r_ready", "r_out", "m_ready", "m_out"))
    x_ld, xT_ld = sem("x_ld"), sem("xT_ld")
    fin_dve, fin_deg, fin_sd, fin_aggs, fin_aggT, fin_aggT_out = (
        sem(n) for n in ("fin_dve", "fin_deg", "fin_sd", "fin_aggs", "fin_aggT", "fin_aggT_out"))
    fin_g, fin_mix, fin_relu, fin_ss, fin_nr, fin_var, fin_sd2, fin_xn2, fin_xn2T, fin_xn2T_out = (
        sem(n) for n in ("fin_g", "fin_mix", "fin_relu", "fin_ss", "fin_nr", "fin_var", "fin_sd2", "fin_xn2",
                         "fin_xn2T", "fin_xn2T_out"))
    fin_gate, fin_log, tok_st, out_st = sem("fin_gate"), sem("fin_log"), sem("tok_st"), sem("out_st")
    route_dve, route_d, route_exp, route_hot, route_cum, slot_hot, slot_used = (
        sem(n) for n in ("route_dve", "route_d", "route_exp", "route_hot", "route_cum", "slot_hot", "slot_used"))
    inv_set, inv_dve, gx_zero, ti_set = sem("inv_set"), sem("inv_dve"), sem("gx_zero"), sem("ti_set")
    gx_in = [sem(f"gx_in{k}") for k in range(2)]
    wexp_in = [sem(f"wexp_in{k}") for k in range(2)]
    xT_ready, xT_out, up_ready, up_out, down_ready, y_read, y_dve, y_ready = (
        sem(n) for n in ("xT_ready", "xT_out", "up_ready", "up_out", "down_ready", "y_read", "y_dve", "y_ready"))
    y_st = [sem(f"y_st{k}") for k in range(2)]

    ds = bass.ds
    XG = [(12 * g, 12) for g in range(4)]

    def main_phase(eng, gnn, kv_rows, kv_sums, mix, fin, route):
        with eng.Fori(0, NQ - 1) as i:
            kv_rows(i)
            gnn(i)
            kv_sums(i)
        kv_rows(NQ - 1)
        gnn(NQ - 1)
        kv_sums(NQ - 1)
        kv_rows(NQ)
        kv_sums(NQ)
        mix()
        with eng.Fori(0, NQ - 1) as q:
            gnn(q + NQ)
            fin(q)
        gnn(NB - 2)
        route(0)
        fin(NQ - 1)
        gnn(NB - 1)
        fin(NQ)
        route(1)

    def blocks_of(q):
        return 1 if isinstance(q, int) and q == NQ else 2

    ROUTES = ((0, ROUTED), (ROUTED, NB - ROUTED))

    def each_token_block(eng, r, place):
        if r == 0:
            with eng.Fori(0, ROUTED // 2) as i:
                for k in range(2):
                    place(i * 2 + k, k)
        else:
            for t in range(ROUTED, NB):
                place(t, t % 2, t == NB - 1)

    def apart(eng):
        eng.sem_inc(passed, 1)

    def each_expert(eng, expert):
        for k in range(2):
            expert(k, k)
        with eng.Fori(1, NE // 2) as i:
            for k in range(2):
                expert(i * 2 + k, k)

    def pair(e, k):
        return e // 2 + 1 if isinstance(e, int) else (e - k + 2) // 2

    block = ctx.enter_context(nc.Block())

    @block.sync
    def _(sp):
        full = ECH - 1
        rest = EROWS - full * P
        sp.dma_start(src_raw[:, 0:full, :].bitcast(I32),
                     src[0:full * P * P].rearrange("(c p j) -> p c j", p=P, j=P)).then_inc(src_in, 16)
        sp.dma_start(dst_raw[:, 0:full, :].bitcast(I32),
                     dst[0:full * P * P].rearrange("(c p j) -> p c j", p=P, j=P)).then_inc(dst_in, 16)
        sp.wait_ge(pads_set, 3)
        for raw, edges, landed in ((src_raw, src, src_in), (dst_raw, dst, dst_in)):
            sp.dma_start(raw[0:rest, full, :].bitcast(I32),
                         edges[full * P * P:EROWS * P].rearrange("(p j) -> p j", j=P)).then_inc(landed, 16)
            sp.dma_start(raw[rest:rest + 1, full, 0:EREST].bitcast(I32),
                         edges[EROWS * P:E].rearrange("(p j) -> p j", p=1)).then_inc(landed, 16)
        wv = w_qkv.rearrange("(c p) d -> p c d", p=P)
        sp.dma_start(wkv_nat, wv[:, IC:3 * IC, :]).then_inc(w_in, 16)
        sp.dma_start(wout_nat, w_out.rearrange("(c p) d -> p c d", p=P)).then_inc(w_in, 16)
        sp.dma_start(b1_nat, b1.rearrange("e (f p) -> (e f) p", p=P)).then_inc(w_in, 16)
        for g, (t, n) in enumerate(XG):
            sp.dma_start(xn_all[:, t:t + n, :],
                         x[t * P:(t + n) * P, :].rearrange("(t p) d -> p t d", p=P)).then_inc(x_in[g], 16)
        sp.dma_start(xn_all[0:LAST, NB - 1, :], x[(NB - 1) * P:N, :]).then_inc(x_in[4], 16)
        sp.dma_start(wq[:, :, :], wv[:, 0:IC, :]).then_inc(w_in2, 16)
        sp.dma_start(gnn_w_sb[:, :, :], gnn_w.rearrange("(c p) d -> p c d", p=P)).then_inc(w_in2, 16)
        sp.dma_start(gate_w_sb[:, :, :], gate_w.rearrange("(c p) d -> p c d", p=P)).then_inc(w_in2, 16)
        sp.dma_start(gnn_b_row[:, :], gnn_b.rearrange("(a d) -> a d", a=1)).then_inc(w_in2, 16)
        sp.dma_start(b_out_row[:, :], b_out.rearrange("(a d) -> a d", a=1)).then_inc(w_in2, 16)
        sp.dma_start(gate_b_row[:, :], gate_b.rearrange("(a d) -> a d", a=1)).then_inc(w_in2, 16)
        for g, (t, n) in enumerate([*XG, (NB - 1, 1)]):
            sp.wait_ge(xn_set, t + n)
            sp.dma_start(xn_rows[t * P:(t + n) * P, :].rearrange("(t p) d -> p t d", p=P),
                         xn_all[:, t:t + n, :]).then_inc(xn_out, 16)
        for g, (t, n) in enumerate([*XG, (NB - 1, 1)]):
            sp.wait_ge(h_lo, t + n)
            sp.dma_start(h_rows[t * P:(t + n) * P, :].rearrange("(t p) d -> p t d", p=P),
                         h_all[:, t:t + n, :]).then_inc(h_out, 16)
        sp.wait_ge(h_out, 16 * 5)

        def load_expert(e, k):
            sp.dma_start(w1_sb[k], w1[ds(e, 1), :, :].rearrange("e (c p) f -> p (e c) f", p=P)).then_inc(wexp_in[k], 16)
            sp.dma_start(w2_sb[k], w2[ds(e, 1), :, :].rearrange("e (c p) f -> p (e c) f", p=P)).then_inc(wexp_in[k], 16)
            sp.dma_start(b2_row[k][:, :], b2[ds(e, 1), :]).then_inc(wexp_in[k], 16)

        load_expert(0, 0)
        load_expert(1, 1)

        def landed(i, k):
            sp.wait_ge(rows_in[k], (i + 1) * (16 * UT))
            sp.sem_inc(rows_landed, 1)

        with sp.Fori(0, NU // RING) as i:
            for k in range(RING):
                landed(i, k)
        for k in range(NU % RING):
            landed(NU // RING, k)
        with sp.Fori(0, NE // 2 - 1) as i:
            for k in range(2):
                sp.wait_ge(down_ready, (i * 2 + k + 1) * CT)
                load_expert(i * 2 + 2 + k, k)
        sp.wait_ge(xn_out, 16 * 5)
        sp.wait_ge(xnT_st, 16 * (NQ + 2))
        sp.wait_ge(tok_st, 16 * (NQ + 2))
        sp.wait_ge(out_st, 16 * (NQ + 2))
        for k in range(2):
            sp.wait_ge(y_st[k], 16 * NE * CT // 2)

    @block.gpsimd
    def _(pool):
        g = nc.gpsimd
        g.memset(src_raw[:, ECH - 1, :].bitcast(I32), NPAD - 1).then_inc(pads_set, 1)
        g.memset(dst_raw[:, ECH - 1, :].bitcast(I32), NPAD - 1).then_inc(pads_set, 1)
        g.memset(xn_all[:, NB - 1, :], 0.0).then_inc(pads_set, 1)
        g.memset(ident[:, :], 0.0).then_inc(pool_c, 1)
        g.memset(utri[:, :], 0.0).then_inc(pool_c, 1)
        g.memset(valid[:, :], 1.0).then_inc(pool_c, 1)
        pool.wait_ge(pool_c, 3)
        g.affine_select(out=ident[:, :], in_=ident[:, :], compare_op=ALU.not_equal, fill=1.0, base=0,
                        pattern=[[-1, P]], channel_multiplier=1).then_inc(consts, 1)
        g.affine_select(out=utri[:, :], in_=utri[:, :], compare_op=ALU.is_gt, fill=1.0, base=0,
                        pattern=[[-1, P]], channel_multiplier=1).then_inc(consts, 1)
        g.affine_select(out=valid[:, :], in_=valid[:, :], compare_op=ALU.is_gt, fill=0.0, base=LAST,
                        pattern=[[0, 1]], channel_multiplier=-1).then_inc(consts, 1)
        g.iota(iota_e, pattern=[[1, P], [0, HT]], base=0, channel_multiplier=0,
               allow_small_or_imprecise_dtypes=True).then_inc(consts, 1)
        g.iota(iota_4[:, :, :], pattern=[[1, P], [0, UT]], base=0, channel_multiplier=0,
               allow_small_or_imprecise_dtypes=True).then_inc(consts, 1)
        g.iota(iota_128[:, :], pattern=[[1, P]], base=0, channel_multiplier=0,
               allow_small_or_imprecise_dtypes=True).then_inc(consts, 1)
        g.iota(iota_64[:, :], pattern=[[1, NE * CT]], base=0, channel_multiplier=0,
               allow_small_or_imprecise_dtypes=True).then_inc(consts, 1)
        g.iota(rev_8[:, :], pattern=[[-1, NE]], base=NE, channel_multiplier=0,
               allow_small_or_imprecise_dtypes=True).then_inc(consts, 1)
        g.iota(node_1[:, :], pattern=[[P, NB]], base=1, channel_multiplier=1,
               allow_small_or_imprecise_dtypes=True).then_inc(consts, 1)
        g.iota(block_edge[:, :], pattern=[[0, 1]], base=0, channel_multiplier=P,
               allow_small_or_imprecise_dtypes=True).then_inc(consts, 1)
        g.memset(ones[:, :], 1.0).then_inc(consts, 1)
        g.memset(zeros16[:, :], 0.0).then_inc(consts, 1)
        g.memset(zeros32[:, :], 0.0).then_inc(consts, 1)
        g.memset(eps[:, :], EPS).then_inc(consts, 1)

        pool.wait_ge(idx_set, 1)
        g.tensor_copy(idx_ring[0][:, :], src_idx[:, 0:RING * UT]).then_inc(idx_next, 1)
        pool.wait_ge(hist_done, 1)
        g.memset(ring[:, :, 2 * D:2 * D + 1], 1.0).then_inc(ring_ones, 1)
        pool.wait_ge(h_out, 16 * 5)

        def unit(k, r, u):
            pool.wait_ge(units_used, u + 1)
            apart(pool)
            for j in range(UT):
                t = k * UT + j
                g.indirect_dma_start(out=ring[:, t, 0:2 * D], out_offset=None, in_=h_rows[:, :],
                                     in_offset=bass.IndirectOffsetOnAxis(ap=idx_ring[r][:, t:t + 1], axis=0)
                                     ).then_inc(rows_in[k], 16)

        with pool.Fori(0, NU // RING // 2) as i:
            for r in range(2):
                pool.wait_ge(idx_next, i * 2 + r + 1)
                for k in range(RING):
                    unit(k, r, i * (2 * RING) + r * RING + k)
                g.tensor_copy(idx_ring[1 - r][:, :],
                              src_idx[:, ds(i * (2 * RING * UT) + (r + 1) * RING * UT, RING * UT)]).then_inc(idx_next, 1)
        done = NU // RING // 2 * 2
        pool.wait_ge(idx_next, done + 1)
        for k in range(NU % RING):
            unit(k, 0, done * RING + k)

        pool.wait_ge(inv_set, 1)
        pool.wait_ge(gx_zero, 2)
        pool.wait_ge(tok_st, 16 * (NQ + 2))
        pool.wait_ge(out_st, 16 * (NQ + 2))

        def take(e, k):
            g.tensor_copy(tok_idx[k][:, :], inv_i[:, ds(e * CT, CT)]).then_inc(ti_set, 1)
            pool.wait_ge(ti_set, e + 1)
            apart(pool)
            for c in range(CT):
                g.indirect_dma_start(out=gx[k][:, c, :], out_offset=None, in_=tok_rows[:, :],
                                     in_offset=bass.IndirectOffsetOnAxis(ap=tok_idx[k][:, c:c + 1], axis=0),
                                     bounds_check=N - 1, oob_is_err=False).then_inc(gx_in[k], 16)

        def give(e, k):
            for c in range(CT):
                pool.wait_ge(y_ready, e * CT + c + 1)
                apart(pool)
                g.indirect_dma_start(out=out[:, :],
                                     out_offset=bass.IndirectOffsetOnAxis(ap=tok_idx[k][:, c:c + 1], axis=0),
                                     in_=y_out[c % 2], in_offset=None,
                                     bounds_check=N - 1, oob_is_err=False).then_inc(y_st[c % 2], 16)

        take(0, 0)
        with pool.Fori(0, NE // 2 - 1) as i:
            take(i * 2 + 1, 1)
            give(i * 2, 0)
            pool.wait_ge(y_st[0], (i * 2 + 1) * (16 * CT // 2))
            pool.wait_ge(y_st[1], (i * 2 + 1) * (16 * CT // 2))
            take(i * 2 + 2, 0)
            give(i * 2 + 1, 1)
            pool.wait_ge(y_st[0], (i * 2 + 2) * (16 * CT // 2))
            pool.wait_ge(y_st[1], (i * 2 + 2) * (16 * CT // 2))
        take(NE - 1, 1)
        give(NE - 2, 0)
        give(NE - 1, 1)

    @block.scalar
    def _(act):
        a = nc.scalar
        n_act = [0]

        def link(ins):
            n_act[0] += 1
            ins.then_inc(ln_act, 1)
            act.wait_ge(ln_act, n_act[0])

        act.sem_inc(agg_out, 1)
        for n in range(7):
            act.wait_ge(wT_ready, n + 1)
            if n < 4:
                for m in range(2):
                    for c in range(DC):
                        ins = a.activation(wkvT[:, c, (2 * n + m) * P:(2 * n + m + 1) * P],
                                           bank[n % 4][:, (2 * m + c) * P:(2 * m + c + 1) * P], ACT.Copy)
            elif n < 6:
                ins = a.activation(woutT[:, :, (n - 4) * P:(n - 3) * P],
                                   bank[n % 4][:, :].rearrange("p (c d) -> p c d", c=IC), ACT.Copy)
            else:
                ins = a.activation(b1_cols[:, :], bank[n % 4][:, 0:NE * FC], ACT.Copy)
            ins.then_inc(wT_out, 1)
        act.wait_ge(consts, 14)
        for g, (t0, n) in enumerate([*XG, (NB - 1, 1)]):
            act.wait_ge(x_in[g], 16)
            for t in range(t0, t0 + n):
                link(a.activation(ln_junk, xn_all[:, t, :], ACT.Copy, accum_out=ln_sum[:, t:t + 1]))
        link(a.mul(ln_nm[:, :], ln_sum[:, :], -1.0 / D))
        for t in range(NB):
            link(a.activation(ln_junk, xn_all[:, t, :], ACT.Square, bias=ln_nm[:, t:t + 1],
                              accum_out=ln_sq[:, t:t + 1]))
        a.activation(ln_sd[:, :], ln_sq[:, :], ACT.Sqrt, bias=eps[:, :], scale=1.0 / D).then_inc(ln_var, 1)
        act.wait_ge(ln_bias, 1)
        for t in range(NB):
            a.activation(xn_all[:, t, :], xn_all[:, t, :], ACT.Identity, bias=ln_nb[:, t:t + 1],
                         scale=ln_rs[:, t:t + 1]).then_inc(xn_set, 1)
        act.wait_ge(deg_set, 1)
        a.activation(deg_sd[:, :], deg[:, :], ACT.Sqrt, scale=HSCALE ** -2).then_inc(deg_rt, 1)
        act.wait_ge(deg_ok, 1)
        act.wait_ge(xn_set, NB)
        for t in range(NB):
            a.activation(h_all[:, t, 0:D], xn_all[:, t, :], ACT.Copy, scale=deg_rs[:, t:t + 1]).then_inc(h_hi, 1)
        act.wait_ge(xn_out, 16 * 5)
        act.wait_ge(h_lo, NB)
        act.sem_inc(xnT_st, 16)
        act.sem_inc(tok_st, 16)
        act.sem_inc(out_st, 16)

        def pair_rows(rows, q):
            first, n = q * (2 * P), 2 * P
            if blocks_of(q) == 1:
                n = LAST if rows is x or rows is out else P
            rows = rows[ds(first, n), :]
            return rows if blocks_of(q) == 1 else rows.rearrange("(m p) d -> p m d", m=2)

        def load_kv(q):
            to = xn_t[:, 0, :] if blocks_of(q) == 1 else xn_t[:, :, :]
            act.dma_start(to, pair_rows(xn_rows, q)).then_inc(xn_ld, 16)

        load_kv(0)

        def gnn(b):
            act.wait_ge(agg_done, b + 1)
            apart(act)
            a.activation(agg_all[:, ds(b, 1), :].rearrange("p a d -> p (a d)"), agg_ps, ACT.Copy).then_inc(agg_out, 1)

        def kv_rows(q):
            w = blocks_of(q)
            act.wait_ge(xnT_st, (q + 1) * 16)
            act.wait_ge(kvT_ready, q + 1)
            a.activation(xnT_t[:, 0:w, :], tp_ps[:, 0:w * D].rearrange("p (m d) -> p m d", m=w), ACT.Copy
                         ).then_inc(kvT_out, 1)
            act.wait_ge(kvT_out, q + 1)
            to = xnT_t[:, 0, :] if w == 1 else xnT_t[:, :, :]
            act.dma_start(pair_rows(xnT_rows, q), to).then_inc(xnT_st, 16)
            if w == 2:
                load_kv(q + 1)
            for m in range(w):
                act.wait_ge(kv_ready, q * 2 + m + 1)
                a.activation(sq[:, m, 0:INNER], kv_ps[m][0][:, :], ACT.Square)
                a.activation(sq[:, m, INNER:2 * INNER], kv_ps[m][1][:, :], ACT.Square).then_inc(kv_sq, 1)
                a.activation(k_sb[:, m, :], kv_ps[m][0][:, :], ACT.Copy).then_inc(k_out, 1)

        def kv_sums(q):
            n = blocks_of(q) * 2 * H
            act.wait_ge(kv_dve, q + 1)
            a.activation(kv_sd[:, 0:n], kv_var[:, 0:n], ACT.Sqrt, bias=eps[:, :], scale=1.0 / DH).then_inc(kv_root, 1)

        def load_pair(q):
            w = blocks_of(q)
            xt, xT_ = (x_t[0:LAST, 0, :], xnT_t[:, 0, :]) if w == 1 else (x_t[:, :, :], xnT_t[:, :, :])
            act.dma_start(xt, pair_rows(x, q)).then_inc(x_ld, 16)
            act.dma_start(xT_, pair_rows(xnT_rows, q)).then_inc(xT_ld, 16)

        def mix():
            act.wait_ge(r_ready, 1)
            for m in range(2):
                ins = a.activation(r_sb[:, 2 * m:2 * m + 2, :].rearrange("p c d -> p (c d)"), kv_ps[0][m][:, :],
                                   ACT.Copy, scale=1.0 / N)
            ins.then_inc(r_out, 1)
            act.wait_ge(m_ready, 1)
            a.activation(mix_m[:, :, :].rearrange("p c d -> p (c d)"), m_ps[:, :], ACT.Copy).then_inc(m_out, 1)
            act.wait_ge(xnT_st, 16 * (NQ + 2))
            load_pair(0)

        def fin(q):
            w = blocks_of(q)
            act.wait_ge(tok_st, (q + 1) * 16)
            act.wait_ge(out_st, (q + 1) * 16)
            act.wait_ge(fin_deg, q + 1)
            a.activation(f_sd[:, 0:w], f_deg[:, 0:w], ACT.Sqrt, scale=HSCALE ** 2).then_inc(fin_sd, 1)
            act.wait_ge(fin_aggT, q + 1)
            a.activation(aggT[:, 0:w, :], tp_ps[:, 0:w * D].rearrange("p (m d) -> p m d", m=w), ACT.Copy
                         ).then_inc(fin_aggT_out, 1)
            act.wait_ge(fin_g, q + 1)
            a.activation(relu_h[:, 0:w, :], g_ps[:, 0:w, :], ACT.Relu).then_inc(fin_relu, 1)
            act.wait_ge(fin_relu, q + 1)
            for m in range(w):
                ins = a.activation(sq_junk[m], relu_h[:, m, :], ACT.Square, accum_out=f_ss[:, m:m + 1])
            ins.then_inc(fin_ss, 1)
            act.wait_ge(fin_ss, q + 1)
            a.activation(f_nr[:, 0:w], f_ss[:, 0:w], ACT.Sqrt).then_inc(fin_nr, 1)
            act.wait_ge(fin_var, q + 1)
            a.activation(f_sd2[:, 0:w], f_mv[:, 0:w, 1], ACT.Sqrt, bias=eps[:, :]).then_inc(fin_sd2, 1)
            act.wait_ge(fin_xn2T, q + 1)
            a.activation(xn2T[:, 0:w, :], xn2T_ps[:, 0:w * D].rearrange("p (m d) -> p m d", m=w), ACT.Copy
                         ).then_inc(fin_xn2T_out, 1)
            act.wait_ge(fin_xn2, q + 1)
            if w == 2:
                load_pair(q + 1)
                act.dma_start(pair_rows(tok_rows, q), tok_t).then_inc(tok_st, 16)
                act.dma_start(pair_rows(out, q), tok_t[:, :, D:2 * D]).then_inc(out_st, 16)
            else:
                act.dma_start(pair_rows(tok_rows, q), tok_t[:, 0, :]).then_inc(tok_st, 16)
                act.dma_start(pair_rows(out, q), tok_t[0:LAST, 0, D:2 * D]).then_inc(out_st, 16)

        def route(r):
            n = ROUTES[r][1]
            act.wait_ge(route_d, r + 1)
            a.activation(per_e[1][:, 0:n, :], per_e[0][:, 0:n, :], ACT.Exp).then_inc(route_exp, 1)

        main_phase(act, gnn, kv_rows, kv_sums, mix, fin, route)

        def expert(e, k):
            if not isinstance(e, int) or e > 0:
                act.wait_ge(down_ready, e * CT)
            for m in range(2):
                w = min(512, CAP - m * 512)
                for f in range(FC):
                    act.wait_ge(up_ready, e * (2 * FC) + m * FC + f + 1)
                    apart(act)
                    a.activation(hidT[:, f, m * 512:m * 512 + w], bank[f % 4][:, 0:w], ACT.Relu,
                                 bias=b1_cols[:, ds(e * FC + f, 1)]).then_inc(up_out, 1)

        each_expert(act, expert)

    @block.tensor
    def _(pe):
        t_ = nc.tensor

        def transpose2(out_ps, rows):
            for c in range(DC):
                ins = t_.transpose(out_ps[:, c * P:(c + 1) * P], rows[:, c * P:(c + 1) * P], ident[:, :])
            return ins

        pe.wait_ge(consts, 14)
        for n, (raw, first) in enumerate(((src_raw, 0), (dst_raw, 4))):
            pe.wait_ge(edges_f, n + 1)
            for c in range(ECH):
                ins = t_.transpose(bank[first + c // 4][:, c % 4 * P:(c % 4 + 1) * P], raw[:, c, :], ident[:, :])
            ins.then_inc(edges_T, 1)
        pe.wait_ge(dst_set, 1)
        t_.matmul(bank[4][0:64, 0:NU - 1], ones[0:1, 0:64], dst_f[0:1, UT:NT:UT], start=True, stop=True
                  ).then_inc(bounds_b, 1)
        pe.wait_ge(bounds_c, 2)
        t_.matmul(bank[5][0:1, 0:64], t0_col[:, :], ident[0:64, 0:64], start=True, stop=True).then_inc(bounds_T, 1)
        pe.wait_ge(idx_set, 1)
        pe.wait_ge(w_in, 48)
        for n in range(7):
            if n >= 4:
                pe.wait_ge(wT_out, n - 3)
            if n < 4:
                for m in range(2):
                    ins = transpose2(bank[n][:, 2 * m * P:(2 * m + 2) * P], wkv_nat[:, 2 * n + m, :])
            elif n < 6:
                for c in range(IC):
                    ins = t_.transpose(bank[n % 4][:, c * P:(c + 1) * P], wout_nat[:, n - 4, c * P:(c + 1) * P], ident[:, :])
            else:
                ins = t_.transpose(bank[n % 4][:, 0:NE * FC], b1_nat, ident[0:NE * FC, 0:NE * FC])
            ins.then_inc(wT_ready, 1)
        t_.matmul(hist_ps, zeros16[:, 0:P], zeros16[:, 0:NB], start=True, stop=False).then_inc(hot_used, 2)

        def hist(s, k, last=False):
            pe.wait_ge(hot_ready, s + 1)
            for t in range(HT):
                ins = t_.matmul(hist_ps, oh_lo[k][:, :, t], oh_hi[k][:, :, t], start=False,
                                stop=last and t == HT - 1)
            ins.then_inc(hist_done if last else hot_used, 1)

        with pe.Fori(0, HS // 2) as i:
            for k in range(2):
                hist(i * 2 + k, k)
        hist(HS - 1, 0, True)

        pe.sem_inc(units_used, RING)
        pe.sem_inc(hots_used, 2)
        pe.sem_inc(slot_used, 2)
        pe.wait_ge(ring_ones, 1)
        pe.wait_ge(w_in2, 16 * 6)
        pe.wait_ge(wkv_set, 1)
        pe.wait_ge(deg_set, 1)
        t_.matmul(inv_ps, zeros16[:, 0:P], zeros16[:, 0:2 * NE * CT], start=True, stop=False)
        t_.matmul(dots_ps[:, :], zeros16[:, 0:P], zeros16[:, 0:512], start=True, stop=False).then_inc(dots_done, 1)

        def visit(u, v):
            pe.wait_ge(rows_landed, u + 1)
            pe.wait_ge(hots_ready, v + 1)
            slot, hot = pe.snap((u % RING) * (UT * (GW + 1))), pe.snap((v % 2) * (P * UT))
            S_v = S[:, :, :].rearrange("p a b -> p (a b)")
            rows = ring.rearrange("p t d -> p (t d)")
            for j in range(UT):
                left = S_v[:, ds(hot, P * UT)].rearrange("p (n j) -> p n j", j=UT)[:, :, j]
                base = slot + j * (GW + 1)
                t_.matmul(agg_ps[:, 0:D], left, rows[:, ds(base, D)], start=False, stop=False)
                ins = t_.matmul(agg_ps, left, rows[:, ds(base + D, D + 1)], start=False, stop=False)
            ins.then_inc(hots_used, 1)

        def add_zero(stop):
            return t_.matmul(agg_ps[:, 0:2], zeros16[:, 0:P], zeros16[:, 0:2], start=False, stop=stop)

        def gnn(b):
            u0 = pe.value_load(first_u[0:1, ds(b, 1)], min_val=0, max_val=NU - 1)
            u1 = pe.value_load(first_u[0:1, ds(b + 1, 1)], min_val=0, max_val=NU - 1)
            pe.wait_ge(agg_out, b + 1)
            t_.matmul(agg_ps, zeros16[:, 0:P], zeros16[:, 0:D + 1], start=True, stop=False)
            with pe.If(u0 < u1):
                with pe.Fori(u0, u1) as u:
                    visit(u, u + b)
                    add_zero(False).then_inc(units_used, 1)
            visit(u1, u1 + b)
            add_zero(True).then_inc(agg_done, 1)

        def kv_rows(q):
            w = blocks_of(q)
            pe.wait_ge(xn_ld, (q + 1) * 16)
            for m in range(w):
                ins = transpose2(tp_ps[:, m * D:(m + 1) * D], xn_t[:, m, :])
            ins.then_inc(kvT_ready, 1)
            pe.wait_ge(kvT_out, q + 1)
            for m in range(w):
                for h in range(2):
                    for c in range(DC):
                        ins = t_.matmul(kv_ps[m][h][:, :], xnT_t[:, m, c * P:(c + 1) * P],
                                        wkvT[:, c, h * INNER:(h + 1) * INNER], start=(c == 0), stop=(c == DC - 1))
                ins.then_inc(kv_ready, 1)

        def kv_sums(q):
            w = blocks_of(q)
            pe.wait_ge(k_out, q * 2 + w)
            for m in range(w):
                pe.wait_ge(v_out, q * 2 + m + 1)
                for c in range(IC):
                    ins = t_.matmul(dots_ps[:, c * P:(c + 1) * P], v_sb[:, m, c * P:(c + 1) * P],
                                    k_sb[:, m, c * P:(c + 1) * P], start=False, stop=(w == 1 and c == IC - 1))
            ins.then_inc(dots_done, 1)

        def mix():
            pe.wait_ge(bd_set, 1)
            for c in range(IC):
                ins = t_.matmul(kv_ps[0][c // 2][:, c % 2 * D:(c % 2 + 1) * D], bd_sb[:, c, :], woutT[:, c, :],
                                start=True, stop=True)
            ins.then_inc(r_ready, 1)
            pe.wait_ge(r_out, 1)
            for d in range(DC):
                for c in range(IC):
                    ins = t_.matmul(m_ps[:, d * D:(d + 1) * D], wq[:, c, d * P:(d + 1) * P], r_sb[:, c, :],
                                    start=(c == 0), stop=(c == IC - 1))
            ins.then_inc(m_ready, 1)
            pe.wait_ge(m_out, 1)

        def fin(q):
            w = blocks_of(q)
            pe.wait_ge(xT_ld, (q + 1) * 16)
            for m in range(w):
                t_.matmul(mix_ps[:, m, :], ones[0:1, :], b_out_row[:, :], start=True, stop=False)
                for c in range(DC):
                    ins = t_.matmul(mix_ps[:, m, :], xnT_t[:, m, c * P:(c + 1) * P], mix_m[:, c, :], start=False,
                                    stop=(c == DC - 1))
            ins.then_inc(fin_mix, 1)
            pe.wait_ge(fin_aggs, q + 1)
            for m in range(w):
                ins = transpose2(tp_ps[:, m * D:(m + 1) * D], agg_s[:, m, :])
            ins.then_inc(fin_aggT, 1)
            for m in range(w):
                t_.matmul(g_ps[:, m, :], ones[0:1, :], gnn_b_row[:, :], start=True, stop=False)
                if m == 0:
                    pe.wait_ge(fin_aggT_out, q + 1)
                for c in range(DC):
                    ins = t_.matmul(g_ps[:, m, :], aggT[:, m, c * P:(c + 1) * P], gnn_w_sb[:, c, :], start=False,
                                    stop=(c == DC - 1))
            ins.then_inc(fin_g, 1)
            pe.wait_ge(fin_xn2, q + 1)
            for m in range(w):
                ins = transpose2(xn2T_ps[:, m * D:(m + 1) * D], tok_t[:, m, :])
            ins.then_inc(fin_xn2T, 1)
            for m in range(w):
                t_.matmul(gate_ps[:, m, :], ones[0:1, :], gate_b_row[:, :], start=True, stop=False)
                if m == 0:
                    pe.wait_ge(fin_xn2T_out, q + 1)
                for c in range(DC):
                    ins = t_.matmul(gate_ps[:, m, :], xn2T[:, m, c * P:(c + 1) * P], gate_w_sb[:, c, :], start=False,
                                    stop=(c == DC - 1))
            ins.then_inc(fin_gate, 1)

        def route(r):
            t0, n = ROUTES[r]
            hot = per_e[2][:, 0:n, :].rearrange("p t e -> p (t e)")
            pe.wait_ge(fin_log, NQ + 1 if r else NQ - 1)
            pe.wait_ge(route_hot, r + 1)
            t_.matmul(cum_ps[:, 0:n * NE], utri[:, :], hot, start=True, stop=True)
            t_.matmul(tot_ps[:, 0:n * NE], ones[:, :], hot, start=True, stop=True).then_inc(route_cum, 1)

            def place(t, k, last=False):
                pe.wait_ge(slot_hot, t + 1)
                t_.matmul(inv_ps, low_hot[k], high_val[k], start=False, stop=last).then_inc(slot_used, 1)

            each_token_block(pe, r, place)

        main_phase(pe, gnn, kv_rows, kv_sums, mix, fin, route)

        def expert(e, k):
            for c in range(CT):
                n = e * CT + c
                if c == 0:
                    pe.wait_ge(gx_in[k], pair(e, k) * (16 * CT))
                if not isinstance(n, int) or n >= 2:
                    pe.wait_ge(xT_out, n - 1)
                transpose2(bank[6 + c % 2], gx[k][:, c, 0:D]).then_inc(xT_ready, 1)
            pe.wait_ge(xT_out, e * CT + CT)
            pe.wait_ge(wexp_in[k], pair(e, k) * 48)
            for m in range(2):
                w = min(512, CAP - m * 512)
                for f in range(FC):
                    n = e * (2 * FC) + m * FC + f
                    if not isinstance(n, int) or n >= 4:
                        pe.wait_ge(up_out, n - 3)
                    for c in range(DC):
                        ins = t_.matmul(bank[f % 4][:, 0:w], w1_sb[k][:, c, f * P:(f + 1) * P],
                                        xT[:, c, m * 512:m * 512 + w], start=(c == 0), stop=(c == DC - 1))
                    ins.then_inc(up_ready, 1)
            for c in range(CT):
                w = min(P, CAP - c * P)
                pe.wait_ge(up_out, e * (2 * FC) + ((c * P + w - 1) // 512 + 1) * FC)
                n = e * CT + c
                if not isinstance(n, int) or n >= 2:
                    pe.wait_ge(y_read, n - 1)
                y_ps = bank[4 + c % 2][0:w, 0:D]
                t_.matmul(y_ps, ones[0:1, 0:w], b2_row[k][:, :], start=True, stop=False)
                for f in range(FC):
                    ins = t_.matmul(y_ps, hidT[:, f, c * P:c * P + w], w2_sb[k][:, f, :], start=False, stop=(f == FC - 1))
                ins.then_inc(down_ready, 1)

        each_expert(pe, expert)

    @block.vector
    def _(dve):
        v_ = nc.vector
        n_pre = [0]

        def link(ins):
            n_pre[0] += 1
            ins.then_inc(dve_pre, 1)
            dve.wait_ge(dve_pre, n_pre[0])

        v_.memset(blk_base[:, :], 0.0).then_inc(base_set, 1)
        dve.wait_ge(src_in, 48)
        v_.tensor_copy(src_raw, src_raw.bitcast(I32)).then_inc(edges_f, 1)
        dve.wait_ge(dst_in, 48)
        v_.tensor_copy(dst_raw, dst_raw.bitcast(I32)).then_inc(edges_f, 1)
        for n, (to, first, landed) in enumerate(((src_idx, 0, idx_set), (dst_f, 4, dst_set))):
            dve.wait_ge(edges_T, n + 1)
            for q in range(4):
                w = min(512, EN - q * 512)
                ins = v_.tensor_copy(to[:, q * 512:q * 512 + w], bank[first + q][:, 0:w])
            ins.then_inc(landed, 1)
        dve.wait_ge(consts, 14)
        dve.wait_ge(bounds_b, 1)
        before = reg_e[0:64, 3840:3840 + NU - 1]
        v_.tensor_scalar(before, bank[4][0:64, 0:NU - 1], block_edge[:, :], None, ALU.is_lt).then_inc(bounds_c, 1)
        dve.wait_ge(bounds_c, 1)
        v_.tensor_reduce(out=t0_col[:, :], in_=before, op=ALU.add, axis=AX.X).then_inc(bounds_c, 1)
        dve.wait_ge(idx_set, 1)
        lo_i, hi_i = (raw.rearrange("p c j -> p (c j)").bitcast(I32) for raw in (src_raw, dst_raw))
        v_.tensor_scalar(lo_i, src_idx[:, :], P - 1, None, ALU.bitwise_and)
        link(v_.tensor_scalar(hi_i, src_idx[:, :], 7, None, ALU.logical_shift_right))
        v_.tensor_copy(lo16, lo_i)
        link(v_.tensor_copy(hi16, hi_i))
        dve.wait_ge(bounds_T, 1)
        v_.tensor_copy(first_u[:, :], bank[5][0:1, 0:64]).then_inc(bounds_set, 1)

        def hot(s, k):
            dve.wait_ge(hot_used, s + 1)
            v_.tensor_tensor(oh_lo[k], iota_e, lo16[:, ds(s * HT, HT)].unsqueeze(1).to_broadcast([P, P, HT]), ALU.is_equal)
            v_.tensor_tensor(oh_hi[k], iota_e[:, 0:NB, :], hi16[:, ds(s * HT, HT)].unsqueeze(1).to_broadcast([P, NB, HT]),
                             ALU.is_equal).then_inc(hot_ready, 1)

        with dve.Fori(0, LN_AT) as i:
            for k in range(2):
                hot(i * 2 + k, k)
        dve.wait_ge(ln_var, 1)
        link(v_.reciprocal(ln_rs[:, :], ln_sd[:, :]))
        v_.tensor_tensor(ln_nb[:, :], ln_nm[:, :], ln_rs[:, :], ALU.mult).then_inc(ln_bias, 1)
        with dve.Fori(LN_AT, HS // 2) as i:
            for k in range(2):
                hot(i * 2 + k, k)
        hot(HS - 1, 0)
        dve.wait_ge(hist_done, 1)
        v_.tensor_scalar(deg[:, :], hist_ps, 1.0, None, ALU.max).then_inc(deg_set, 1)
        dve.wait_ge(deg_rt, 1)
        v_.reciprocal(deg_rs[:, :], deg_sd[:, :]).then_inc(deg_ok, 1)
        dve.wait_ge(deg_ok, 1)
        for t in range(NB):
            dve.wait_ge(h_hi, t + 1)
            v_.scalar_tensor_tensor(h_all[:, t, D:2 * D], xn_all[:, t, :], deg_rs[:, t:t + 1], h_all[:, t, 0:D],
                                    ALU.mult, ALU.subtract).then_inc(h_lo, 1)
        dve.wait_ge(wT_out, 4)
        groups = wkvT[:, :, :].rearrange("p c (h d) -> p (c h) d", d=DH)
        link(v_.tensor_reduce(out=kv_mean, in_=groups, op=ALU.add, axis=AX.X))
        link(v_.tensor_scalar(kv_mean, kv_mean, 1.0 / DH, None, ALU.mult))
        v_.tensor_tensor(groups, groups, kv_mean.unsqueeze(2).to_broadcast([P, 2 * DC * H, DH]), ALU.subtract
                         ).then_inc(wkv_set, 1)
        dve.wait_ge(bounds_set, 1)

        def visit(u, v):
            slot = dve.snap(v % 2)
            dve.wait_ge(hots_used, v + 1)
            rel = dst_rel[:, ds(slot, 1), :].rearrange("p a t -> p (a t)")
            v_.tensor_scalar(rel, dst_f[:, ds(u * UT, UT)], blk_base[:, :], None, ALU.subtract).then_inc(rel_set, 1)
            dve.wait_ge(rel_set, v + 1)
            v_.tensor_tensor(S[:, ds(slot, 1), :].rearrange("p a (n j) -> p (a n) j", j=UT), iota_4[:, :, :],
                             rel.unsqueeze(1).to_broadcast([P, P, UT]), ALU.is_equal).then_inc(hots_ready, 1)

        def gnn(b):
            u0 = dve.value_load(first_u[0:1, ds(b, 1)], min_val=0, max_val=NU - 1)
            u1 = dve.value_load(first_u[0:1, ds(b + 1, 1)], min_val=0, max_val=NU - 1)
            dve.wait_ge(base_set, b + 1)
            apart(dve)
            with dve.If(u0 < u1):
                with dve.Fori(u0, u1) as u:
                    visit(u, u + b)
            visit(u1, u1 + b)
            v_.tensor_scalar(blk_base[:, :], blk_base[:, :], float(P), None, ALU.add).then_inc(base_set, 1)

        def kv_rows(q):
            pass

        def kv_sums(q):
            w = blocks_of(q)
            for m in range(w):
                dve.wait_ge(kv_sq, q * 2 + m + 1)
                ins = v_.tensor_reduce(out=kv_var[:, m * 2 * H:(m + 1) * 2 * H],
                                       in_=sq[:, m, :].rearrange("p (g d) -> p g d", d=DH), op=ALU.add, axis=AX.X)
            ins.then_inc(kv_dve, 1)
            dve.wait_ge(kv_root, q + 1)
            v_.reciprocal(kv_rs[:, 0:w * 2 * H], kv_sd[:, 0:w * 2 * H]).then_inc(kv_v, 1)
            dve.wait_ge(kv_v, q * 2 + 1)
            rs = kv_rs.rearrange("p (m g h) -> p m g h", m=2, g=2)
            v_.tensor_tensor(kv_sc.rearrange("p (m h) -> p m h", m=2)[:, 0:w, :], rs[:, 0:w, 0, :], rs[:, 0:w, 1, :],
                             ALU.mult).then_inc(kv_v, 1)
            dve.wait_ge(kv_v, q * 2 + 2)
            dve.wait_ge(dots_done, q + 1)
            for m in range(w):
                v_.tensor_tensor(v_sb[:, m, :].rearrange("p (h d) -> p h d", d=DH),
                                 kv_ps[m][1][:, :].rearrange("p (h d) -> p h d", d=DH),
                                 kv_sc[:, m * H:(m + 1) * H].unsqueeze(2).to_broadcast([P, H, DH]), ALU.mult
                                 ).then_inc(v_out, 1)

        def mix():
            dve.wait_ge(dots_done, NQ + 2)
            v_.memset(bd_sb, 0.0).then_inc(bd_zero, 1)
            dve.wait_ge(bd_zero, 1)
            for half in range(2):
                r = slice(half * DH, (half + 1) * DH)
                ins = v_.tensor_copy(bd_sb[r, :, r], dots_ps[r, :].rearrange("p (c d) -> p c d", c=IC)[:, :, r])
            ins.then_inc(bd_set, 1)

        def fin(q):
            w = blocks_of(q)
            n = [0]

            def step(ins):
                n[0] += 1
                ins.then_inc(fin_dve, 1)
                dve.wait_ge(fin_dve, q * FIN_STEPS + n[0])

            agg = agg_all[:, ds(q * 2, w), :]
            dve.wait_ge(agg_out, q * 2 + w + 1)
            v_.tensor_scalar(f_deg[:, 0:w], agg[:, :, D], 1.0, None, ALU.max).then_inc(fin_deg, 1)
            dve.wait_ge(fin_sd, q + 1)
            step(v_.reciprocal(f_rin[:, 0:w], f_sd[:, 0:w]))
            for m in range(w):
                ins = v_.tensor_scalar(agg_s[:, m, :], agg[:, m, 0:D], f_rin[:, m:m + 1], None, ALU.mult)
            ins.then_inc(fin_aggs, 1)
            dve.wait_ge(x_ld, (q + 1) * 16)
            dve.wait_ge(fin_mix, q + 1)
            step(v_.tensor_tensor(mixed[:, 0:w, :], x_t[:, 0:w, :], mix_ps[:, 0:w, :], ALU.add))
            dve.wait_ge(fin_nr, q + 1)
            step(v_.tensor_scalar(f_nc[:, 0:w], f_nr[:, 0:w], 1e-12, None, ALU.max))
            step(v_.reciprocal(f_rn[:, 0:w], f_nc[:, 0:w]))
            for m in range(w):
                ins = v_.scalar_tensor_tensor(tok_t[:, m, D:2 * D], relu_h[:, m, :], f_rn[:, m:m + 1], mixed[:, m, :],
                                              ALU.mult, ALU.add)
            step(ins)
            for m in range(w):
                ins = v_.bn_stats(f_bn[m], tok_t[:, m, D:2 * D])
            step(ins)
            apart(dve)
            for m in range(w):
                ins = v_.bn_aggr(f_mv[:, m, :], f_bn[m])
            ins.then_inc(fin_var, 1)
            dve.wait_ge(fin_sd2, q + 1)
            step(v_.reciprocal(f_rstd[:, 0:w], f_sd2[:, 0:w]))
            for m in range(w):
                ins = v_.tensor_scalar(tok_t[:, m, 0:D], tok_t[:, m, D:2 * D], f_mv[:, m, 0:1], f_rstd[:, m:m + 1],
                                       ALU.subtract, ALU.mult)
            ins.then_inc(fin_xn2, 1)
            dve.wait_ge(fin_gate, q + 1)
            v_.tensor_copy(logits[:, ds(q * 2, w), :], gate_ps[:, 0:w, :]).then_inc(fin_log, 1)
            assert n[0] == FIN_STEPS, n

        n_route = [0]

        def chain(ins):
            n_route[0] += 1
            ins.then_inc(route_dve, 1)
            dve.wait_ge(route_dve, n_route[0])

        def route(r):
            t0, n = ROUTES[r]
            diff, exps, hot, tot, acc = (b_[:, 0:n, :] for b_ in per_e)
            top, first, prb, sums, pos, drop, slot, low, high, low_f, high_f = (b_[:, 0:n] for b_ in per_t[0:11])
            slot, low, high = (b_.bitcast(I32) for b_ in (slot, low, high))
            rev = rev_8[:, :].unsqueeze(1).to_broadcast([P, n, NE])

            def wide(col):
                return col.unsqueeze(2).to_broadcast([P, n, NE])

            dve.wait_ge(fin_log, NQ + 1 if r else NQ - 1)
            chain(v_.tensor_reduce(out=top, in_=logits[:, t0:t0 + n, :], op=ALU.max, axis=AX.X))
            v_.tensor_tensor(diff, logits[:, t0:t0 + n, :], wide(top), ALU.subtract).then_inc(route_d, 1)
            dve.wait_ge(route_d, r + 1)
            chain(v_.tensor_scalar(acc, diff, 0.0, None, ALU.is_equal))
            chain(v_.tensor_tensor(acc, acc, rev, ALU.mult))
            chain(v_.tensor_reduce(out=first, in_=acc, op=ALU.max, axis=AX.X))
            ins = v_.tensor_tensor(hot, rev, wide(first), ALU.is_equal)
            if r:
                chain(ins)
                ins = v_.tensor_scalar(hot[:, n - 1, :], hot[:, n - 1, :], valid[:, :], None, ALU.mult)
            ins.then_inc(route_hot, 1)
            dve.wait_ge(route_exp, r + 1)
            chain(v_.tensor_reduce(out=sums, in_=exps, op=ALU.add, axis=AX.X))
            chain(v_.reciprocal(prb, sums))
            if r:
                chain(v_.tensor_scalar(prb[:, n - 1:n], prb[:, n - 1:n], valid[:, :], None, ALU.mult))
                chain(v_.tensor_scalar(node_1[:, NB - 1:NB], node_1[:, NB - 1:NB], valid[:, :], None, ALU.mult))
            dve.wait_ge(route_cum, r + 1)
            tot_in = tot_ps[:, 0:n * NE].rearrange("p (t e) -> p t e", e=NE)
            chain(v_.tensor_copy(tot, tot_in))
            now, nxt, s = tot, acc, 1
            while s < n:
                v_.tensor_copy(nxt[:, 0:s, :], now[:, 0:s, :])
                chain(v_.tensor_tensor(nxt[:, s:n, :], now[:, s:n, :], now[:, 0:n - s, :], ALU.add))
                now, nxt, s = nxt, now, s * 2
            chain(v_.tensor_tensor(nxt, now, tot_in, ALU.subtract))
            if r:
                chain(v_.tensor_tensor(nxt, nxt, routed[:, :].unsqueeze(1).to_broadcast([P, n, NE]), ALU.add))
            else:
                chain(v_.tensor_copy(routed[:, :], now[:, n - 1, :]))
            chain(v_.tensor_tensor(nxt, nxt, cum_ps[:, 0:n * NE].rearrange("p (t e) -> p t e", e=NE), ALU.add))
            chain(v_.tensor_tensor(nxt, nxt, hot, ALU.mult))
            chain(v_.tensor_reduce(out=pos, in_=nxt, op=ALU.add, axis=AX.X))
            chain(v_.tensor_scalar(drop, pos, float(CAP), float(2 * NE * CROWS), ALU.is_gt, ALU.mult))
            chain(v_.tensor_scalar(first, first, -float(CROWS), float(NE * CROWS - 1), ALU.mult, ALU.add))
            chain(v_.tensor_tensor(first, first, pos, ALU.add))
            chain(v_.tensor_tensor(slot, first, drop, ALU.add))
            chain(v_.tensor_scalar(low, slot, P - 1, None, ALU.bitwise_and))
            chain(v_.tensor_scalar(high, slot, 7, None, ALU.arith_shift_right))
            chain(v_.tensor_copy(low_f, low))
            chain(v_.tensor_copy(high_f, high))

            def place(t, k, last=False):
                dve.wait_ge(slot_used, t + 1)
                col = ds(t - t0, 1)
                v_.tensor_scalar(low_hot[k], iota_128[:, :], low_f[:, col], None, ALU.is_equal)
                v_.tensor_scalar(high_val[k][:, 0:NE * CT], iota_64[:, :], high_f[:, col], node_1[:, ds(t, 1)],
                                 ALU.is_equal, ALU.mult)
                v_.tensor_scalar(high_val[k][:, NE * CT:2 * NE * CT], iota_64[:, :], high_f[:, col], prb[:, col],
                                 ALU.is_equal, ALU.mult).then_inc(slot_hot, 1)

            each_token_block(dve, r, place)

        main_phase(dve, gnn, kv_rows, kv_sums, mix, fin, route)

        dve.wait_ge(slot_used, NB + 2)
        in_slot = inv_ps[:, 0:NE * CT]
        chain(v_.tensor_copy(slot_prb[:, :], inv_ps[:, NE * CT:2 * NE * CT]))
        chain(v_.tensor_scalar(inv_m[:, :], in_slot, 0.0, float(2 * N), ALU.is_equal, ALU.mult))
        chain(v_.tensor_scalar(inv_f[:, :], in_slot, -1.0, None, ALU.add))
        v_.tensor_tensor(inv_i[:, :], inv_f[:, :], inv_m[:, :], ALU.add).then_inc(inv_set, 1)
        dve.wait_ge(hots_used, NU - 1 + NB + 2)
        for k in range(2):
            v_.memset(gx[k], 0.0).then_inc(gx_zero, 1)
        for k in range(2):
            chain(v_.memset(y_out[k], 0.0))

        def expert(e, k):
            for c in range(CT):
                dve.wait_ge(xT_ready, e * CT + c + 1)
                v_.tensor_copy(xT[:, :, c * P:(c + 1) * P], bank[6 + c % 2][:, 0:D].rearrange("p (c n) -> p c n", c=DC)
                               ).then_inc(xT_out, 1)
            for c in range(CT):
                t = e * CT + c
                w = min(P, CAP - c * P)
                m = [0]

                def step(ins):
                    m[0] += 1
                    ins.then_inc(y_dve, 1)
                    dve.wait_ge(y_dve, t * Y_STEPS + m[0])

                row = gx[k][0:w, c, :]
                y, z, d, fine, nan = (b_[0:w, :] for b_ in (y_sb, y_cl, y_df, y_mask, y_nan))
                dve.wait_ge(down_ready, t + 1)
                v_.tensor_scalar(y, bank[4 + c % 2][0:w, 0:D], slot_prb[0:w, ds(t, 1)], None, ALU.mult).then_inc(y_read, 1)
                dve.wait_ge(y_read, t + 1)
                v_.tensor_scalar(z, y, 1e4, -1e4, ALU.min, ALU.max)
                step(v_.tensor_tensor(d, y, y, ALU.subtract))
                v_.tensor_scalar(fine, d, 0.0, None, ALU.is_equal)
                step(v_.tensor_tensor(nan, y, y, ALU.not_equal))
                apart(dve)
                step(v_.copy_predicated(z, fine, y))
                apart(dve)
                step(v_.copy_predicated(z, nan, zeros32[0:w, :]))
                if c >= 2 or not isinstance(e, int) or e > 0:
                    dve.wait_ge(y_st[c % 2], t // 2 * 16 if isinstance(t, int) else e * (16 * CT // 2) + c // 2 * 16)
                v_.tensor_tensor(y_out[c % 2][0:w, :], z, row[:, D:2 * D], ALU.add).then_inc(y_ready, 1)

        each_expert(dve, expert)


_INS = ['x', 'src', 'dst', 'L0_gnn_W', 'L0_gnn_b', 'L0_mix_w_qkv', 'L0_mix_w_out', 'L0_mix_b_out',
        'L0_ffn_gate_w', 'L0_ffn_gate_b', 'L0_ffn_w1', 'L0_ffn_b1', 'L0_ffn_w2', 'L0_ffn_b2']


def kernel(**inputs):
    import numpy as _np
    import concourse.bacc as _bacc
    from concourse.bass_utils import run_bass_kernel_spmd as _run

    nc = _bacc.Bacc("TRN2", target_bir_lowering=False, num_devices=1)
    arrays, args = {}, []
    for name in _INS:
        a = _np.ascontiguousarray(inputs[name])
        arrays[f"in_{name}"] = a
        args.append(nc.dram_tensor(f"in_{name}", a.shape, mybir.dt.from_np(a.dtype), kind="ExternalInput").ap())
    args.append(nc.dram_tensor("out_0", (N, D), F32, kind="ExternalOutput").ap())
    build(nc, *args)
    r = _run(nc, [arrays], core_ids=[0])
    return r.results[0]["out_0"]
```

```python
import concourse.bass as bass
import numpy as np
from concourse import mybir
from contextlib import ExitStack

F32 = mybir.dt.float32
F32R = mybir.dt.float32r
F16 = mybir.dt.float16
I32 = mybir.dt.int32
ALU = mybir.AluOpType
ACT = mybir.ActivationFunctionType
AX = mybir.AxisListType

P = 128
N = 6250
D = 256
DC = D // P
E = 206250
NB = -(-N // P)
NPAD = NB * P
LAST = N - (NB - 1) * P
UT = 4
RING = 8
HOTS = 8
EROWS = E // P
EREST = E - EROWS * P
HT = 16
LOW = 64
HIGH = NPAD // LOW
HS = -(-E // (P * HT))
NT = HS * HT
NU = NT // UT
ECH = -(-NT // P)
H = 8
DH = 64
INNER = H * DH
IC = INNER // P
NE = 8
FF = 1024
FC = FF // P
CAP = -(-5 * N // (4 * NE))
CT = -(-CAP // P)
CROWS = CT * P
CLAST = CAP - (CT - 1) * P
CEVEN = -(-CAP // 2) * 2
HSCALE = 2048.0
GW = 2 * D + 1
TOKW = 2 * D
NQ = NB // 2
EPS = 1e-5
LN_AT = 30
ROUTE_STEPS = 11
FIN_STEPS = 23
GROUPS = ((0, CT // 2), (CT // 2, CT // 4), (CT // 2 + CT // 4, CT - CT // 2 - CT // 4))
UPS = len(GROUPS) * FC
Y_STEPS = 2


def build(nc, x, src, dst, gnn_w, gnn_b, w_qkv, w_out, b_out, gate_w, gate_b, w1, b1, w2, b2, out):
    ctx = ExitStack()

    def sb(name, shape, dt=F32):
        return ctx.enter_context(nc.sbuf_tensor(name, shape, dt))

    def sem(name):
        return ctx.enter_context(nc.semaphore(name))

    def dram(name, shape, dt=F32):
        return nc.dram_tensor(name, shape, dt, kind="Internal").ap()

    h_rows = dram("h_rows", (NPAD, 2 * D), F16)
    xn_rows = dram("xn_rows", (NPAD, D))
    xnT_rows = dram("xnT_rows", (NPAD, D))
    tok_rows = dram("tok_rows", (NPAD, TOKW))

    EN = ECH * P
    early = ExitStack()

    def room(stack, name, shape, dt=F32):
        return stack.enter_context(nc.sbuf_tensor(name, shape, dt, side="right"))

    reg_a = room(early, "reg_a", [P, NB * (D + 1)])
    reg_c = room(early, "reg_c", [P, 8960])
    reg_e = room(early, "reg_e", [P, 4416])
    reg_w = room(early, "reg_w", [P, 4096])
    early.close()
    hid_hi, hid_lo = (room(ctx, f"hid_{n}", [P, FC, CROWS], F32R) for n in ("hi", "lo"))
    w1_hi, w1_lo = (room(ctx, f"w1_{n}", [P, DC, FF], F32R) for n in ("hi", "lo"))
    w2_hi, w2_lo = (room(ctx, f"w2_{n}", [P, FC, D], F32R) for n in ("hi", "lo"))
    xT_hi, xT_lo = (room(ctx, f"xT_{n}", [P, DC, CROWS], F32R) for n in ("hi", "lo"))
    y_fine, y_nan = (room(ctx, f"y_{n}", [P, D], I32) for n in ("fine", "nan"))
    reg_b = sb("reg_b", [P, NB * D])
    reg_d = sb("reg_d", [P, 2 * EN])

    xn_all = reg_a[:, 0:NB * D].rearrange("p (t d) -> p t d", t=NB)
    agg_all = reg_a[:, :].rearrange("p (t d) -> p t d", t=NB)
    WN = DC * FF
    h_all = reg_b[:, :].bitcast(F16).rearrange("p (t d) -> p t d", t=NB)
    w1_raw = reg_b[:, 0:WN].rearrange("p (c f) -> p c f", c=DC)
    w2_raw = reg_b[:, WN:2 * WN].rearrange("p (f d) -> p f d", f=FC)
    GXN = CT * TOKW
    gx = [reg_b[:, 2 * WN + k * GXN:2 * WN + (k + 1) * GXN].rearrange("p (c d) -> p c d", c=CT) for k in range(2)]
    S = reg_b[:, 2 * WN + GXN:2 * WN + GXN + HOTS * P * UT // 2].bitcast(F16)

    src_raw = reg_c[:, 0:EN].rearrange("p (c j) -> p c j", c=ECH)
    dst_raw = reg_c[:, EN:2 * EN].rearrange("p (c j) -> p c j", c=ECH)
    o = 2 * EN
    lo16 = reg_c[:, o:o + EN // 2].bitcast(F16)
    hi16 = reg_c[:, o + EN // 2:o + EN].bitcast(F16)
    o += EN
    iota_e = reg_c[:, o:o + HIGH * HT // 2].bitcast(F16).rearrange("p (j t) -> p j t", t=HT)
    o += HIGH * HT // 2
    hi_i = reg_c[:, o:o + EN].bitcast(I32)
    oh_lo, oh_hi = [], []
    for _ in range(2):
        oh_lo.append(reg_c[:, o:o + LOW * HT // 2].bitcast(F16).rearrange("p (j t) -> p j t", t=HT))
        o += LOW * HT // 2
        oh_hi.append(reg_c[:, o:o + HIGH * HT // 2].bitcast(F16).rearrange("p (j t) -> p j t", t=HT))
        o += HIGH * HT // 2
    assert o <= 8960
    ring = reg_c[:, 0:RING * UT * (GW + 1) // 2].bitcast(F16).rearrange("p (t d) -> p t d", d=GW + 1)
    y_sum, y_sb, y_zero, y_out = ([reg_d[:, (2 * j + k) * D:(2 * j + k + 1) * D] for k in range(2)] for j in range(4))
    hid_full = [reg_d[:, 8 * D + k * 512:8 * D + (k + 1) * 512] for k in range(2)]

    wkv_nat = reg_e[:, 0:2048].rearrange("p (c d) -> p c d", c=8)
    wout_nat = reg_e[:, 2048:3072].rearrange("p (c d) -> p c d", c=DC)
    b1_nat = reg_e[0:NE * FC, 3072:3200]
    kv_mean = reg_e[:, 3200:3232]
    ln_junk = reg_e[:, 3584:3840]
    sq = reg_e[:, 0:2048].rearrange("p (m d) -> p m d", m=2)
    k_sb = reg_e[:, 2048:3072].rearrange("p (m d) -> p m d", m=2)
    v_sb = reg_e[:, 3072:4096].rearrange("p (m d) -> p m d", m=2)
    r_sb = reg_e[:, 0:1024].rearrange("p (c d) -> p c d", c=IC)
    bd_sb = reg_e[:, 2048:2560].rearrange("p (c d) -> p c d", c=IC)
    agg_s, aggT, relu_h, mixed = (reg_e[:, k * 2 * D:(k + 1) * 2 * D].rearrange("p (m d) -> p m d", m=2)
                                  for k in range(4))
    tok_t = reg_e[:, 2048:2048 + 2 * TOKW].rearrange("p (m d) -> p m d", m=2)
    xn2T = reg_e[:, 3072:3584].rearrange("p (m d) -> p m d", m=2)
    sq_junk = [reg_e[:, 3584 + k * D:3584 + (k + 1) * D] for k in range(2)]
    tiny = reg_e[:, 4096:4416]

    src_idx, dst_f = reg_d[:, 0:EN].bitcast(I32), reg_d[:, EN:2 * EN]
    idx_ring = [sb(f"idx_ring{k}", [P, RING * UT], I32) for k in range(2)]
    dst_rel = sb("dst_rel", [P, HOTS, UT], F16)
    blk_base = sb("blk_base", [P, 1])
    iota_4 = sb("iota_4", [P, P, UT], F16)
    ident = sb("ident", [P, P])
    utri = sb("utri", [P, P])
    ones = sb("ones", [P, P])
    zeros16 = sb("zeros16", [1, 512], F16)
    zeros32 = sb("zeros32", [P, D])
    iota_128 = sb("iota_128", [P, P])
    iota_64 = sb("iota_64", [P, NE * CT])
    rev_8 = sb("rev_8", [P, NE])
    node_1 = sb("node_1", [P, NB])
    block_edge = sb("block_edge", [64, 1])
    valid = sb("valid", [P, 1])
    eps = sb("eps", [P, 1])
    first_u = sb("first_u", [1, 64], I32)
    t0_col = sb("t0_col", [64, 1])
    ln_sum = sb("ln_sum", [P, NB])
    ln_nm = sb("ln_nm", [P, NB])
    ln_sq = sb("ln_sq", [P, NB])
    ln_sd = sb("ln_sd", [P, NB])
    ln_rs = sb("ln_rs", [P, NB])
    ln_nb = sb("ln_nb", [P, NB])
    hist_sb = sb("hist_sb", [LOW, HIGH])
    up_64 = sb("up_64", [LOW, P])
    deg = sb("deg", [P, NB])
    deg_sd = sb("deg_sd", [P, NB])
    deg_rs = sb("deg_rs", [P, NB])
    wkvT = reg_w[:, 0:2048].rearrange("p (c e) -> p c e", c=DC)
    wq, woutT = (reg_w[:, k:k + 1024].rearrange("p (c d) -> p c d", c=IC) for k in (2048, 3072))
    mix_m = sb("mix_m", [P, DC, D])
    gnn_w_sb = sb("gnn_w_sb", [P, DC, D])
    gate_w_sb = sb("gate_w_sb", [P, DC, NE])
    gnn_b_row = sb("gnn_b_row", [1, D])
    b_out_row = sb("b_out_row", [1, D])
    gate_b_row = sb("gate_b_row", [1, NE])
    b1_cols = sb("b1_cols", [P, NE * FC])
    b2_all = [sb(f"b2_all{k}", [P, D]) for k in range(2)]
    xn_t = sb("xn_t", [P, 2, D])
    xnT_t = sb("xnT_t", [P, 2, D])
    x_t = sb("x_t", [P, 2, D])
    routed = sb("routed", [P, NE])
    slot_prb = sb("slot_prb", [P, NE * CT])
    tokens = sb("tokens", [1, NE], I32)
    inv_i = sb("inv_i", [P, NE * CT], I32)
    inv_f = sb("inv_f", [P, NE * CT])
    inv_m = sb("inv_m", [P, NE * CT])
    take_idx, give_idx = ([sb(f"{n}_idx{k}", [P, CT], I32) for k in range(2)] for n in ("take", "give"))

    names = iter(range(320))

    def small(n=1):
        a = next(names)
        for _ in range(n - 1):
            next(names)
        return tiny[:, a:a + n]

    kv_var, kv_sd, kv_rs, kv_sc = small(32), small(32), small(32), small(16)
    f_deg, f_sd, f_rin, f_ss, f_nr, f_nc, f_rn, f_sd2, f_rstd = (small(2) for _ in range(9))
    f_bn = [small(6) for _ in range(2)]
    f_mv = small(4).rearrange("p (m s) -> p m s", s=2)

    r_log, r_diff, r_eq, r_hot, r_exp, r_cum = (small(2 * NE).rearrange("p (m e) -> p m e", m=2) for _ in range(6))
    r_top, r_first, r_sum, r_prb, r_pos, r_drop, r_base, r_place, r_low, r_high = (small(2) for _ in range(10))
    r_slot, r_low_i, r_high_i = (small(2).bitcast(I32) for _ in range(3))

    hots = wq[:, :, :].rearrange("p c e -> p (c e)")
    low_hot = [hots[:, k * P:(k + 1) * P] for k in range(2)]
    high_val = [hots[:, (2 + k) * P:(3 + k) * P] for k in range(2)]

    bank = [ctx.enter_context(nc.psum_tensor(f"bank{k}", [P, 512], F32)) for k in range(8)]
    agg_ps = bank[0][:, 0:D + 1]
    kv_ps = (bank[1:3], bank[5:7])
    dots_ps = bank[3]
    tp_ps = bank[4]
    m_ps = bank[5]
    xn2T_ps = bank[5]
    gate_ps = bank[6][:, 0:2 * NE].rearrange("p (m e) -> p m e", m=2)
    cum_ps = bank[6][:, 2 * NE:4 * NE].rearrange("p (m e) -> p m e", m=2)
    inv_ps = bank[7][:, 0:2 * NE * CT]
    hist_ps = bank[7][0:LOW, 0:HIGH]
    deg_ps = bank[6][:, 0:NB]
    g_ps, mix_ps = (bank[k][:, :].rearrange("p (m d) -> p m d", m=2) for k in (1, 2))

    src_in, dst_in, pads_set = sem("src_in"), sem("dst_in"), sem("pads_set")
    consts, x_in, w_in, pool_c = sem("consts"), [sem(f"x_in{g}") for g in range(5)], sem("w_in"), sem("pool_c")
    w_in2 = sem("w_in2")
    edges_f, edges_T, idx_set, dst_set = [sem(f"edges_f{n}") for n in ("s", "d")], sem("edges_T"), sem("idx_set"), sem("dst_set")
    hi_set, hi16_set, hist_out, deg_ready = sem("hi_set"), sem("hi16_set"), sem("hist_out"), sem("deg_ready")
    bounds_b, bounds_c, bounds_T, bounds_set = (sem(n) for n in ("bounds_b", "bounds_c", "bounds_T", "bounds_set"))
    wT_ready, wT_out = sem("wT_ready"), sem("wT_out")
    hot_ready, hot_used, hist_done = sem("hot_ready"), sem("hot_used"), sem("hist_done")
    deg_set, deg_rt, deg_ok = sem("deg_set"), sem("deg_rt"), sem("deg_ok")
    ln_act, ln_var, ln_rec, ln_bias, xn_set = (sem(n) for n in ("ln_act", "ln_var", "ln_rec", "ln_bias", "xn_set"))
    xn_out, h_hi, h_lo, h_out = sem("xn_out"), sem("h_hi"), sem("h_lo"), sem("h_out")
    dve_pre, wkv_set = sem("dve_pre"), sem("wkv_set")
    ring_ones, passed = sem("ring_ones"), sem("passed")
    idx_next, base_set, kv_v = sem("idx_next"), sem("base_set"), sem("kv_v")
    rows_in = [sem(f"rows_in{k}") for k in range(RING)]
    rows_landed, units_used = sem("rows_landed"), sem("units_used")
    rel_set, hots_ready, hots_used = sem("rel_set"), sem("hots_ready"), sem("hots_used")
    agg_done, agg_out = sem("agg_done"), sem("agg_out")
    xn_ld, kvT_ready, kvT_out, xnT_st = sem("xn_ld"), sem("kvT_ready"), sem("kvT_out"), sem("xnT_st")
    kv_ready, kv_sq, k_out, kv_dve, kv_root, v_out, dots_done = (
        sem(n) for n in ("kv_ready", "kv_sq", "k_out", "kv_dve", "kv_root", "v_out", "dots_done"))
    bd_zero, bd_set, r_ready, r_out, m_ready, m_out = (
        sem(n) for n in ("bd_zero", "bd_set", "r_ready", "r_out", "m_ready", "m_out"))
    x_ld, xT_ld = sem("x_ld"), sem("xT_ld")
    fin_dve, fin_deg, fin_sd, fin_aggs, fin_aggT, fin_aggT_out = (
        sem(n) for n in ("fin_dve", "fin_deg", "fin_sd", "fin_aggs", "fin_aggT", "fin_aggT_out"))
    fin_g, fin_mix, fin_relu, fin_ss, fin_nr, fin_var, fin_sd2, fin_xn2, fin_xn2T, fin_xn2T_out = (
        sem(n) for n in ("fin_g", "fin_mix", "fin_relu", "fin_ss", "fin_nr", "fin_var", "fin_sd2", "fin_xn2",
                         "fin_xn2T", "fin_xn2T_out"))
    fin_gate, fin_log, tok_st, out_st = sem("fin_gate"), sem("fin_log"), sem("tok_st"), sem("out_st")
    route_d, route_exp, route_hot, route_cum, slot_hot, slot_used = (
        sem(n) for n in ("route_d", "route_exp", "route_hot", "route_cum", "slot_hot", "slot_used"))
    inv_set, inv_dve, gx_zero = sem("inv_set"), sem("inv_dve"), sem("gx_zero")
    take_set, give_set = sem("take_set"), sem("give_set")
    gx_in = [sem(f"gx_in{k}") for k in range(2)]
    w1_in, w2_in, b2_in = sem("w1_in"), sem("w2_in"), [sem(f"b2_in{k}") for k in range(2)]
    w1_hi_set, w1_lo_set, w2_hi_set, w2_lo_set = (sem(n) for n in ("w1_hi_set", "w1_lo_set", "w2_hi_set", "w2_lo_set"))
    xT_ready, xT_hi_set, xT_lo_set, up_ready, hid_full_set, hid_hi_set, hid_lo_set = (
        sem(n) for n in ("xT_ready", "xT_hi_set", "xT_lo_set", "up_ready", "hid_full_set", "hid_hi_set", "hid_lo_set"))
    down_ready, y_read, y_act, y_scaled, y_dve, y_fixed, y_ready = (
        sem(n) for n in ("down_ready", "y_read", "y_act", "y_scaled", "y_dve", "y_fixed", "y_ready"))
    y_st = [sem(f"y_st{k}") for k in range(2)]

    ds = bass.ds
    XG = [(12 * g, 12) for g in range(4)]

    def main_phase(eng, gnn, kv_rows, kv_sums, mix, fin_rows, fin_norm, route):
        with eng.Fori(0, NQ - 1) as i:
            kv_rows(i)
            gnn(i)
            kv_sums(i)
        for i in range(NQ - 1, NQ + 1):
            kv_rows(i)
            gnn(i)
            kv_sums(i)
        mix()
        fin_rows(0)
        gnn(NQ + 1)
        fin_norm(0)
        with eng.Fori(1, NQ - 1) as q:
            fin_rows(q)
            gnn(q + (NQ + 1))
            fin_norm(q)
        fin_rows(NQ - 1)
        gnn(NB - 1)
        fin_norm(NQ - 1)
        fin_rows(NQ)
        fin_norm(NQ)
        route(NQ)

    def first_pair(q):
        return isinstance(q, int) and q == 0

    def blocks_of(q):
        return 1 if isinstance(q, int) and q == NQ else 2

    def apart(eng):
        eng.sem_inc(passed, 1)

    def each_expert(eng, expert):
        for k in range(2):
            expert(k, k, True)
        with eng.Fori(1, NE // 2 - 1) as i:
            for k in range(2):
                expert(i * 2 + k, k, True)
        expert(NE - 2, 0, True)
        expert(NE - 1, 1, False)

    def filled(e, eng):
        return eng.value_load(tokens[0:1, ds(e, 1)], min_val=0, max_val=N)

    def if_filled(eng, count, g, work, signals, also=None):
        if g == 0:
            work()
            return
        with eng.If(count > GROUPS[g][0] * P):
            work()
        with eng.Else():
            for signal, before, n in signals:
                eng.wait_ge(signal, before)
                eng.sem_inc(signal, n)
            if also:
                also()

    def columns(g):
        t0, n = GROUPS[g]
        return slice(t0 * P, min((t0 + n) * P, CEVEN))

    XG2 = CROWS // (2 * P)

    block = ctx.enter_context(nc.Block())

    @block.sync
    def _(sp):
        full = ECH - 1
        rest = EROWS - full * P
        sp.dma_start(src_raw[:, 0:full, :].bitcast(I32),
                     src[0:full * P * P].rearrange("(c p j) -> p c j", p=P, j=P)).then_inc(src_in, 16)
        sp.dma_start(dst_raw[:, 0:full, :].bitcast(I32),
                     dst[0:full * P * P].rearrange("(c p j) -> p c j", p=P, j=P)).then_inc(dst_in, 16)
        sp.wait_ge(pads_set, 3)
        for raw, edges, landed in ((src_raw, src, src_in), (dst_raw, dst, dst_in)):
            sp.dma_start(raw[0:rest, full, :].bitcast(I32),
                         edges[full * P * P:EROWS * P].rearrange("(p j) -> p j", j=P)).then_inc(landed, 16)
            sp.dma_start(raw[rest:rest + 1, full, 0:EREST].bitcast(I32),
                         edges[EROWS * P:E].rearrange("(p j) -> p j", p=1)).then_inc(landed, 16)
        wv = w_qkv.rearrange("(c p) d -> p c d", p=P)
        sp.dma_start(wkv_nat, wv[:, IC:3 * IC, :]).then_inc(w_in, 16)
        sp.dma_start(wout_nat, w_out.rearrange("(c p) d -> p c d", p=P)).then_inc(w_in, 16)
        sp.dma_start(b1_nat, b1.rearrange("e (f p) -> (e f) p", p=P)).then_inc(w_in, 16)
        for g, (t, n) in enumerate(XG):
            sp.dma_start(xn_all[:, t:t + n, :],
                         x[t * P:(t + n) * P, :].rearrange("(t p) d -> p t d", p=P)).then_inc(x_in[g], 16)
        sp.dma_start(xn_all[0:LAST, NB - 1, :], x[(NB - 1) * P:N, :]).then_inc(x_in[4], 16)
        sp.dma_start(wq[:, :, :], wv[:, 0:IC, :]).then_inc(w_in2, 16)
        sp.dma_start(gnn_w_sb[:, :, :], gnn_w.rearrange("(c p) d -> p c d", p=P)).then_inc(w_in2, 16)
        sp.dma_start(gate_w_sb[:, :, :], gate_w.rearrange("(c p) d -> p c d", p=P)).then_inc(w_in2, 16)
        sp.dma_start(gnn_b_row[:, :], gnn_b.rearrange("(a d) -> a d", a=1)).then_inc(w_in2, 16)
        sp.dma_start(b_out_row[:, :], b_out.rearrange("(a d) -> a d", a=1)).then_inc(w_in2, 16)
        sp.dma_start(gate_b_row[:, :], gate_b.rearrange("(a d) -> a d", a=1)).then_inc(w_in2, 16)
        for g, (t, n) in enumerate([*XG, (NB - 1, 1)]):
            sp.wait_ge(xn_set, t + n)
            sp.dma_start(xn_rows[t * P:(t + n) * P, :].rearrange("(t p) d -> p t d", p=P),
                         xn_all[:, t:t + n, :]).then_inc(xn_out, 16)
        for g, (t, n) in enumerate([*XG, (NB - 1, 1)]):
            sp.wait_ge(h_lo, t + n)
            sp.dma_start(h_rows[t * P:(t + n) * P, :].rearrange("(t p) d -> p t d", p=P),
                         h_all[:, t:t + n, :]).then_inc(h_out, 16)
        sp.wait_ge(h_out, 16 * 5)

        def load_w1(e):
            sp.dma_start(w1_raw, w1[ds(e, 1), :, :].rearrange("e (c p) f -> p (e c) f", p=P)).then_inc(w1_in, 16)

        def load_w2(e):
            sp.dma_start(w2_raw, w2[ds(e, 1), :, :].rearrange("e (c p) f -> p (e c) f", p=P)).then_inc(w2_in, 16)

        def load_b2(e, k):
            sp.dma_start(b2_all[k][:, :], b2[ds(e, 1), :].to_broadcast([P, D])).then_inc(b2_in[k], 16)

        load_w1(0)
        load_w2(0)
        load_b2(0, 0)

        def landed(i, k):
            sp.wait_ge(rows_in[k], (i + 1) * (16 * UT))
            sp.sem_inc(rows_landed, 1)

        with sp.Fori(0, NU // RING) as i:
            for k in range(RING):
                landed(i, k)
        for k in range(NU % RING):
            landed(NU // RING, k)
        def expert(e, k, more):
            if more:
                sp.wait_ge(w1_lo_set, e + 1)
                load_w1(e + 1)
                sp.wait_ge(w2_lo_set, e * 2 + 2)
                load_b2(e + 1, 1 - k)
                load_w2(e + 1)

        each_expert(sp, expert)
        sp.wait_ge(xn_out, 16 * 5)
        sp.wait_ge(xnT_st, 16 * (NQ + 2))
        sp.wait_ge(tok_st, 16 * (NQ + 2))
        sp.wait_ge(out_st, 16 * (NQ + 2))
        for k in range(2):
            sp.wait_ge(y_st[k], 16 * NE * CT // 2)

    @block.gpsimd
    def _(pool):
        g = nc.gpsimd
        g.memset(src_raw[:, ECH - 1, :].bitcast(I32), NPAD - 1).then_inc(pads_set, 1)
        g.memset(dst_raw[:, ECH - 1, :].bitcast(I32), NPAD - 1).then_inc(pads_set, 1)
        g.memset(xn_all[:, NB - 1, :], 0.0).then_inc(pads_set, 1)
        g.memset(ident[:, :], 0.0).then_inc(pool_c, 1)
        g.memset(utri[:, :], 0.0).then_inc(pool_c, 1)
        g.memset(valid[:, :], 1.0).then_inc(pool_c, 1)
        g.memset(up_64[:, :], 0.0).then_inc(pool_c, 1)
        pool.wait_ge(pool_c, 4)
        g.affine_select(out=ident[:, :], in_=ident[:, :], compare_op=ALU.not_equal, fill=1.0, base=0,
                        pattern=[[-1, P]], channel_multiplier=1).then_inc(consts, 1)
        g.affine_select(out=up_64[:, :], in_=up_64[:, :], compare_op=ALU.not_equal, fill=1.0, base=LOW,
                        pattern=[[-1, P]], channel_multiplier=1).then_inc(consts, 1)
        g.affine_select(out=utri[:, :], in_=utri[:, :], compare_op=ALU.is_gt, fill=1.0, base=0,
                        pattern=[[-1, P]], channel_multiplier=1).then_inc(consts, 1)
        g.affine_select(out=valid[:, :], in_=valid[:, :], compare_op=ALU.is_gt, fill=0.0, base=LAST,
                        pattern=[[0, 1]], channel_multiplier=-1).then_inc(consts, 1)
        g.iota(iota_e, pattern=[[1, HIGH], [0, HT]], base=0, channel_multiplier=0,
               allow_small_or_imprecise_dtypes=True).then_inc(consts, 1)
        g.iota(iota_4[:, :, :], pattern=[[1, P], [0, UT]], base=0, channel_multiplier=0,
               allow_small_or_imprecise_dtypes=True).then_inc(consts, 1)
        g.iota(iota_128[:, :], pattern=[[1, P]], base=0, channel_multiplier=0,
               allow_small_or_imprecise_dtypes=True).then_inc(consts, 1)
        g.iota(iota_64[:, :], pattern=[[1, NE * CT]], base=0, channel_multiplier=0,
               allow_small_or_imprecise_dtypes=True).then_inc(consts, 1)
        g.iota(rev_8[:, :], pattern=[[-1, NE]], base=NE, channel_multiplier=0,
               allow_small_or_imprecise_dtypes=True).then_inc(consts, 1)
        g.iota(node_1[:, :], pattern=[[P, NB]], base=1, channel_multiplier=1,
               allow_small_or_imprecise_dtypes=True).then_inc(consts, 1)
        g.iota(block_edge[:, :], pattern=[[0, 1]], base=0, channel_multiplier=P,
               allow_small_or_imprecise_dtypes=True).then_inc(consts, 1)
        g.memset(ones[:, :], 1.0).then_inc(consts, 1)
        g.memset(zeros16[:, :], 0.0).then_inc(consts, 1)
        g.memset(zeros32[:, :], 0.0).then_inc(consts, 1)
        g.memset(eps[:, :], EPS).then_inc(consts, 1)

        pool.wait_ge(idx_set, 1)
        g.tensor_copy(idx_ring[0][:, :], src_idx[:, 0:RING * UT]).then_inc(idx_next, 1)
        pool.wait_ge(hist_done, 1)
        g.memset(ring[:, :, 2 * D:2 * D + 1], 1.0).then_inc(ring_ones, 1)
        pool.wait_ge(h_out, 16 * 5)

        def unit(k, r, u):
            pool.wait_ge(units_used, u + 1)
            apart(pool)
            for j in range(UT):
                t = k * UT + j
                g.indirect_dma_start(out=ring[:, t, 0:2 * D], out_offset=None, in_=h_rows[:, :],
                                     in_offset=bass.IndirectOffsetOnAxis(ap=idx_ring[r][:, t:t + 1], axis=0)
                                     ).then_inc(rows_in[k], 16)

        with pool.Fori(0, NU // RING // 2) as i:
            for r in range(2):
                pool.wait_ge(idx_next, i * 2 + r + 1)
                for k in range(RING):
                    unit(k, r, i * (2 * RING) + r * RING + k)
                g.tensor_copy(idx_ring[1 - r][:, :],
                              src_idx[:, ds(i * (2 * RING * UT) + (r + 1) * RING * UT, RING * UT)]).then_inc(idx_next, 1)
        done = NU // RING // 2 * 2
        pool.wait_ge(idx_next, done + 1)
        for k in range(NU % RING):
            unit(k, 0, done * RING + k)

        pool.wait_ge(hots_used, NU - 1 + NB + HOTS)
        g.memset(gx[1], 0.0).then_inc(gx_zero, 1)
        pool.wait_ge(inv_set, 1)
        pool.wait_ge(gx_zero, 2)
        pool.wait_ge(tok_st, 16 * (NQ + 2))
        pool.wait_ge(out_st, 16 * (NQ + 2))

        def take_list(e, k):
            g.tensor_copy(take_idx[k][:, :], inv_i[:, ds(e * CT, CT)]).then_inc(take_set, 1)
            pool.wait_ge(take_set, e + 1)
            apart(pool)

        def take(k, c):
            nc.gpsimd.indirect_dma_start(out=gx[k][:, c, :], out_offset=None, in_=tok_rows[:, :],
                                         in_offset=bass.IndirectOffsetOnAxis(ap=take_idx[k][:, c:c + 1], axis=0),
                                         bounds_check=N - 1, oob_is_err=False).then_inc(gx_in[k], 16)

        def low_w1(e):
            pool.wait_ge(w1_hi_set, e + 1)
            apart(pool)
            g.tensor_tensor(w1_lo[:, :, :], w1_raw, w1_hi[:, :, :].bitcast(F32), ALU.subtract).then_inc(w1_lo_set, 1)

        for e in range(2):
            take_list(e, e)
            for c in range(CT):
                take(e, c)

        def expert(e, k, more):
            loop = not isinstance(e, int)
            if loop or e >= 2:
                for b_ in range(2):
                    pool.wait_ge(y_st[b_], e * (8 * CT) - 8 * CT)
                apart(pool)
            g.tensor_copy(give_idx[k][:, :], inv_i[:, ds(e * CT, CT)]).then_inc(give_set, 1)
            after = loop or e < NE - 2
            if after:
                pool.wait_ge(gx_in[k], (e - k + 2) * (8 * CT))
                take_list(e + 2, k)
            if more:
                low_w1(e + 1)
            count = filled(e, pool)
            pool.wait_ge(give_set, e + 1)
            apart(pool)
            for group, (t0, n) in enumerate(GROUPS):
                def store(c):
                    pool.wait_ge(y_ready, e * CT + c + 1)
                    apart(pool)
                    nc.gpsimd.indirect_dma_start(
                        out=out[:, :], out_offset=bass.IndirectOffsetOnAxis(ap=give_idx[k][:, c:c + 1], axis=0),
                        in_=y_out[c % 2], in_offset=None, bounds_check=N - 1, oob_is_err=False).then_inc(y_st[c % 2], 16)
                    if after:
                        take(k, c)

                def add_rows():
                    for c in range(t0, t0 + n):
                        pool.wait_ge(y_fixed, e * CT + c + 1)
                        apart(pool)
                        nc.gpsimd.tensor_tensor(y_out[c % 2], y_out[c % 2], gx[k][:, c, D:2 * D], ALU.add
                                                ).then_inc(y_ready, 1)
                        store(c)

                if_filled(pool, count, group, add_rows, ((y_ready, e * CT + t0, n),),
                          lambda: [store(c) for c in range(t0, t0 + n)])

        each_expert(pool, expert)

    @block.scalar
    def _(act):
        a = nc.scalar
        n_act = [0]

        def link(ins):
            n_act[0] += 1
            ins.then_inc(ln_act, 1)
            act.wait_ge(ln_act, n_act[0])

        act.sem_inc(agg_out, 1)
        act.wait_ge(dst_in, 48)
        a.activation(dst_raw, dst_raw.bitcast(I32), ACT.Copy).then_inc(edges_f[1], 1)
        act.wait_ge(hi_set, 1)
        a.activation(hi16, hi_i, ACT.Copy).then_inc(hi16_set, 1)
        act.wait_ge(edges_T, 2)
        for q in range(4):
            w = min(512, EN - q * 512)
            ins = a.activation(dst_f[:, q * 512:q * 512 + w], bank[4 + q][:, 0:w], ACT.Copy)
        ins.then_inc(dst_set, 1)
        for n in range(7):
            act.wait_ge(wT_ready, n + 1)
            if n < 4:
                for m in range(2):
                    for c in range(DC):
                        ins = a.activation(wkvT[:, c, (2 * n + m) * P:(2 * n + m + 1) * P],
                                           bank[n % 4][:, (2 * m + c) * P:(2 * m + c + 1) * P], ACT.Copy)
            elif n < 6:
                ins = a.activation(woutT[:, :, (n - 4) * P:(n - 3) * P],
                                   bank[n % 4][:, :].rearrange("p (c d) -> p c d", c=IC), ACT.Copy)
            else:
                ins = a.activation(b1_cols[:, :], bank[n % 4][:, 0:NE * FC], ACT.Copy)
            ins.then_inc(wT_out, 1)
        act.wait_ge(consts, 15)
        for g, (t0, n) in enumerate([*XG, (NB - 1, 1)]):
            act.wait_ge(x_in[g], 16)
            for t in range(t0, t0 + n):
                link(a.activation(ln_junk, xn_all[:, t, :], ACT.Copy, accum_out=ln_sum[:, t:t + 1]))
        link(a.mul(ln_nm[:, :], ln_sum[:, :], -1.0 / D))
        for t in range(NB):
            link(a.activation(ln_junk, xn_all[:, t, :], ACT.Square, bias=ln_nm[:, t:t + 1],
                              accum_out=ln_sq[:, t:t + 1]))
        a.activation(ln_sd[:, :], ln_sq[:, :], ACT.Sqrt, bias=eps[:, :], scale=1.0 / D).then_inc(ln_var, 1)
        act.wait_ge(ln_bias, 1)
        for t in range(NB):
            a.activation(xn_all[:, t, :], xn_all[:, t, :], ACT.Identity, bias=ln_nb[:, t:t + 1],
                         scale=ln_rs[:, t:t + 1]).then_inc(xn_set, 1)
        act.wait_ge(deg_set, 1)
        a.activation(deg_sd[:, :], deg[:, :], ACT.Sqrt, scale=HSCALE ** -2).then_inc(deg_rt, 1)
        act.wait_ge(deg_ok, 1)
        act.wait_ge(xn_set, NB)
        for t in range(NB):
            a.activation(h_all[:, t, 0:D], xn_all[:, t, :], ACT.Copy, scale=deg_rs[:, t:t + 1]).then_inc(h_hi, 1)
        act.wait_ge(xn_out, 16 * 5)
        act.wait_ge(h_lo, NB)
        act.sem_inc(xnT_st, 16)
        act.sem_inc(tok_st, 16)
        act.sem_inc(out_st, 16)

        def pair_rows(rows, q):
            first, n = q * (2 * P), 2 * P
            if blocks_of(q) == 1:
                n = LAST if rows is x or rows is out else P
            rows = rows[ds(first, n), :]
            return rows if blocks_of(q) == 1 else rows.rearrange("(m p) d -> p m d", m=2)

        def load_kv(q):
            to = xn_t[:, 0, :] if blocks_of(q) == 1 else xn_t[:, :, :]
            act.dma_start(to, pair_rows(xn_rows, q)).then_inc(xn_ld, 16)

        load_kv(0)

        def gnn(b):
            act.wait_ge(agg_done, b + 1)
            apart(act)
            a.activation(agg_all[:, ds(b, 1), :].rearrange("p a d -> p (a d)"), agg_ps, ACT.Copy).then_inc(agg_out, 1)

        def kv_rows(q):
            w = blocks_of(q)
            act.wait_ge(xnT_st, (q + 1) * 16)
            act.wait_ge(kvT_ready, q + 1)
            a.activation(xnT_t[:, 0:w, :], tp_ps[:, 0:w * D].rearrange("p (m d) -> p m d", m=w), ACT.Copy
                         ).then_inc(kvT_out, 1)
            act.wait_ge(kvT_out, q + 1)
            to = xnT_t[:, 0, :] if w == 1 else xnT_t[:, :, :]
            act.dma_start(pair_rows(xnT_rows, q), to).then_inc(xnT_st, 16)
            if w == 2:
                load_kv(q + 1)
            for m in range(w):
                act.wait_ge(kv_ready, q * 2 + m + 1)
                a.activation(sq[:, m, 0:INNER], kv_ps[m][0][:, :], ACT.Square)
                a.activation(sq[:, m, INNER:2 * INNER], kv_ps[m][1][:, :], ACT.Square).then_inc(kv_sq, 1)
                a.activation(k_sb[:, m, :], kv_ps[m][0][:, :], ACT.Copy).then_inc(k_out, 1)

        def kv_sums(q):
            n = blocks_of(q) * 2 * H
            act.wait_ge(kv_dve, q + 1)
            a.activation(kv_sd[:, 0:n], kv_var[:, 0:n], ACT.Sqrt, bias=eps[:, :], scale=1.0 / DH).then_inc(kv_root, 1)

        def load_pair(q):
            w = blocks_of(q)
            xt, xT_ = (x_t[0:LAST, 0, :], xnT_t[:, 0, :]) if w == 1 else (x_t[:, :, :], xnT_t[:, :, :])
            act.dma_start(xt, pair_rows(x, q)).then_inc(x_ld, 16)
            act.dma_start(xT_, pair_rows(xnT_rows, q)).then_inc(xT_ld, 16)

        def mix():
            act.wait_ge(r_ready, 1)
            for m in range(2):
                ins = a.activation(r_sb[:, 2 * m:2 * m + 2, :].rearrange("p c d -> p (c d)"), kv_ps[0][m][:, :],
                                   ACT.Copy, scale=1.0 / N)
            ins.then_inc(r_out, 1)
            act.wait_ge(m_ready, 1)
            a.activation(mix_m[:, :, :].rearrange("p c d -> p (c d)"), m_ps[:, :], ACT.Copy).then_inc(m_out, 1)
            act.wait_ge(xnT_st, 16 * (NQ + 2))
            load_pair(0)

        def fin_rows(q):
            w = blocks_of(q)
            act.wait_ge(tok_st, (q + 1) * 16)
            act.wait_ge(out_st, (q + 1) * 16)
            act.wait_ge(fin_deg, q + 1)
            a.activation(f_sd[:, 0:w], f_deg[:, 0:w], ACT.Sqrt, scale=HSCALE ** 2).then_inc(fin_sd, 1)
            act.wait_ge(fin_aggT, q + 1)
            a.activation(aggT[:, 0:w, :], tp_ps[:, 0:w * D].rearrange("p (m d) -> p m d", m=w), ACT.Copy
                         ).then_inc(fin_aggT_out, 1)
            act.wait_ge(fin_g, q + 1)
            a.activation(relu_h[:, 0:w, :], g_ps[:, 0:w, :], ACT.Relu).then_inc(fin_relu, 1)
            act.wait_ge(fin_relu, q + 1)
            for m in range(w):
                ins = a.activation(sq_junk[m], relu_h[:, m, :], ACT.Square, accum_out=f_ss[:, m:m + 1])
            ins.then_inc(fin_ss, 1)
            if not first_pair(q):
                route(q - 1)
            act.wait_ge(fin_ss, q + 1)
            a.activation(f_nr[:, 0:w], f_ss[:, 0:w], ACT.Sqrt).then_inc(fin_nr, 1)
            act.wait_ge(fin_var, q + 1)
            a.activation(f_sd2[:, 0:w], f_mv[:, 0:w, 1], ACT.Sqrt, bias=eps[:, :]).then_inc(fin_sd2, 1)

        def fin_norm(q):
            w = blocks_of(q)
            act.wait_ge(fin_xn2T, q + 1)
            a.activation(xn2T[:, 0:w, :], xn2T_ps[:, 0:w * D].rearrange("p (m d) -> p m d", m=w), ACT.Copy
                         ).then_inc(fin_xn2T_out, 1)
            act.wait_ge(fin_xn2, q + 1)
            if w == 2:
                load_pair(q + 1)
                act.dma_start(pair_rows(tok_rows, q), tok_t).then_inc(tok_st, 16)
                act.dma_start(pair_rows(out, q), tok_t[:, :, D:2 * D]).then_inc(out_st, 16)
            else:
                act.dma_start(pair_rows(tok_rows, q), tok_t[:, 0, :]).then_inc(tok_st, 16)
                act.dma_start(pair_rows(out, q), tok_t[0:LAST, 0, D:2 * D]).then_inc(out_st, 16)

        def route(q):
            w = blocks_of(q)
            act.wait_ge(route_d, q + 1)
            a.activation(r_exp[:, 0:w, :], r_diff[:, 0:w, :], ACT.Exp).then_inc(route_exp, 1)

        main_phase(act, gnn, kv_rows, kv_sums, mix, fin_rows, fin_norm, route)

        def high_w1(e):
            act.wait_ge(w1_in, (e + 1) * 16)
            a.activation(w1_hi[:, :, :], w1_raw, ACT.Copy).then_inc(w1_hi_set, 1)

        def high_w2(e):
            act.wait_ge(w2_in, (e + 1) * 16)
            a.activation(w2_hi[:, :, :], w2_raw, ACT.Copy).then_inc(w2_hi_set, 1)

        def high_rows(e):
            for p in range(XG2):
                act.wait_ge(xT_ready, e * XG2 + p + 1)
                a.activation(xT_hi[:, :, p * 2 * P:(p + 1) * 2 * P],
                             bank[4 + p][:, :].rearrange("p (c n) -> p c n", c=DC), ACT.Copy).then_inc(xT_hi_set, 1)

        act.sem_inc(hid_full_set, 4)
        act.wait_ge(inv_set, 1)
        act.wait_ge(tok_st, 16 * (NQ + 2))
        act.wait_ge(out_st, 16 * (NQ + 2))
        high_w1(0)
        high_w2(0)
        high_rows(0)

        def expert(e, k, more):
            count = filled(e, act)

            def hidden(g):
                at = columns(g)
                w = at.stop - at.start
                for f in range(FC):
                    n = e * UPS + g * FC + f
                    act.wait_ge(hid_lo_set, n + 1)
                    act.wait_ge(up_ready, n + 1)
                    apart(act)
                    a.activation(hid_full[f % 2][:, 0:w], bank[f % 4][:, 0:w], ACT.Relu,
                                 bias=b1_cols[:, ds(e * FC + f, 1)]).then_inc(hid_full_set, 1)
                    act.wait_ge(hid_full_set, n + 5)
                    a.activation(hid_hi[:, f, at], hid_full[f % 2][:, 0:w], ACT.Copy).then_inc(hid_hi_set, 1)

            def scale(g):
                for c in range(GROUPS[g][0], sum(GROUPS[g])):
                    t = e * CT + c
                    w = min(P, CAP - c * P)
                    act.wait_ge(y_read, t + 3)
                    apart(act)
                    a.activation(y_sb[c % 2][0:w, :], y_sum[c % 2][0:w, :], ACT.Copy, scale=slot_prb[0:w, ds(t, 1)]
                                 ).then_inc(y_act, 1)
                    act.wait_ge(y_act, t + 1)
                    a.activation(y_zero[c % 2][0:w, :], y_sb[c % 2][0:w, :], ACT.Copy, scale=0.0).then_inc(y_scaled, 1)

            for g in range(len(GROUPS)):
                if_filled(act, count, g, lambda: hidden(g),
                          ((hid_full_set, e * UPS + (g * FC + 4), FC), (hid_hi_set, e * UPS + g * FC, FC)))
            if more:
                high_rows(e + 1)
                high_w1(e + 1)
            for g, (t0, n) in enumerate(GROUPS):
                if_filled(act, count, g, lambda: scale(g), ((y_act, e * CT + t0, n), (y_scaled, e * CT + t0, n)))
            if more:
                act.wait_ge(down_ready, (e + 1) * CT)
                high_w2(e + 1)

        each_expert(act, expert)

    @block.tensor
    def _(pe):
        t_ = nc.tensor

        def transpose2(out_ps, rows):
            for c in range(DC):
                ins = t_.transpose(out_ps[:, c * P:(c + 1) * P], rows[:, c * P:(c + 1) * P], ident[:, :])
            return ins

        pe.sem_inc(hot_used, 2)
        pe.wait_ge(consts, 15)
        for n, (raw, first) in enumerate(((src_raw, 0), (dst_raw, 4))):
            pe.wait_ge(edges_f[n], 1)
            for c in range(ECH):
                ins = t_.transpose(bank[first + c // 4][:, c % 4 * P:(c % 4 + 1) * P], raw[:, c, :], ident[:, :])
            ins.then_inc(edges_T, 1)
        pe.wait_ge(dst_set, 1)
        t_.matmul(bank[4][0:64, 0:NU - 1], ones[0:1, 0:64], dst_f[0:1, UT:NT:UT], start=True, stop=True
                  ).then_inc(bounds_b, 1)
        def weights(n):
            if n >= 4:
                pe.wait_ge(wT_out, n - 3)
            if n < 4:
                for m in range(2):
                    ins = transpose2(bank[n][:, 2 * m * P:(2 * m + 2) * P], wkv_nat[:, 2 * n + m, :])
            elif n < 6:
                for c in range(IC):
                    ins = t_.transpose(bank[n % 4][:, c * P:(c + 1) * P], wout_nat[:, n - 4, c * P:(c + 1) * P], ident[:, :])
            else:
                ins = t_.transpose(bank[n % 4][:, 0:NE * FC], b1_nat, ident[0:NE * FC, 0:NE * FC])
            ins.then_inc(wT_ready, 1)

        def hist(s, k, last=False):
            pe.wait_ge(hot_ready, s + 1)
            for t in range(HT):
                ins = t_.matmul(hist_ps, oh_lo[k][:, :, t], oh_hi[k][:, :, t], start=False,
                                stop=last and t == HT - 1)
            ins.then_inc(hist_done if last else hot_used, 1)

        t_.matmul(hist_ps, zeros16[:, 0:LOW], zeros16[:, 0:HIGH], start=True, stop=False)
        pe.wait_ge(idx_set, 1)
        pe.wait_ge(w_in, 48)
        for n in range(7):
            for k in range(2):
                hist(n * 2 + k, k)
            weights(n)
        with pe.Fori(7, HS // 2) as i:
            for k in range(2):
                hist(i * 2 + k, k)
        hist(HS - 1, 0, True)
        pe.wait_ge(hist_out, 1)
        for half, move in enumerate((ident[0:LOW, :], up_64[:, :])):
            ins = t_.matmul(deg_ps, move, hist_sb[:, half:HIGH:2], start=(half == 0), stop=(half == 1))
        ins.then_inc(deg_ready, 1)
        pe.wait_ge(bounds_c, 2)
        t_.matmul(bank[5][0:1, 0:64], t0_col[:, :], ident[0:64, 0:64], start=True, stop=True).then_inc(bounds_T, 1)

        pe.sem_inc(units_used, RING)
        pe.sem_inc(hots_used, HOTS)
        pe.sem_inc(slot_used, 1)
        pe.wait_ge(ring_ones, 1)
        pe.wait_ge(w_in2, 16 * 6)
        pe.wait_ge(wkv_set, 1)
        pe.wait_ge(bounds_set, 1)
        pe.wait_ge(deg_set, 1)
        t_.matmul(inv_ps, zeros16[:, 0:P], zeros16[:, 0:2 * NE * CT], start=True, stop=False)
        t_.matmul(dots_ps[:, :], zeros16[:, 0:P], zeros16[:, 0:512], start=True, stop=False).then_inc(dots_done, 1)

        def visit(u, v):
            pe.wait_ge(rows_landed, u + 1)
            pe.wait_ge(hots_ready, v + 1)
            slot, hot = pe.snap((u % RING) * (UT * (GW + 1))), pe.snap((v % HOTS) * (P * UT))
            rows = ring.rearrange("p t d -> p (t d)")[:, ds(slot, UT * (GW + 1))].rearrange("p (t d) -> p t d", t=UT)
            left = S[:, ds(hot, P * UT)].rearrange("p (n j) -> p n j", j=UT)
            for j in range(UT):
                t_.matmul(agg_ps[:, 0:D], left[:, :, j], rows[:, j, 0:D], start=False, stop=False)
                ins = t_.matmul(agg_ps, left[:, :, j], rows[:, j, D:GW], start=False, stop=False)
            ins.then_inc(hots_used, 1)

        def add_zero(stop):
            return t_.matmul(agg_ps[:, 0:2], zeros16[:, 0:P], zeros16[:, 0:2], start=False, stop=stop)

        def gnn(b):
            u0 = pe.value_load(first_u[0:1, ds(b, 1)], min_val=0, max_val=NU - 1)
            u1 = pe.value_load(first_u[0:1, ds(b + 1, 1)], min_val=0, max_val=NU - 1)
            pe.wait_ge(agg_out, b + 1)
            t_.matmul(agg_ps, zeros16[:, 0:P], zeros16[:, 0:D + 1], start=True, stop=False)
            with pe.If(u0 < u1):
                with pe.Fori(u0, u1) as u:
                    visit(u, u + b)
                    add_zero(False).then_inc(units_used, 1)
            visit(u1, u1 + b)
            add_zero(True).then_inc(agg_done, 1)

        def kv_rows(q):
            w = blocks_of(q)
            pe.wait_ge(xn_ld, (q + 1) * 16)
            for m in range(w):
                ins = transpose2(tp_ps[:, m * D:(m + 1) * D], xn_t[:, m, :])
            ins.then_inc(kvT_ready, 1)
            pe.wait_ge(kvT_out, q + 1)
            for m in range(w):
                for h in range(2):
                    for c in range(DC):
                        ins = t_.matmul(kv_ps[m][h][:, :], xnT_t[:, m, c * P:(c + 1) * P],
                                        wkvT[:, c, h * INNER:(h + 1) * INNER], start=(c == 0), stop=(c == DC - 1))
                ins.then_inc(kv_ready, 1)

        def kv_sums(q):
            w = blocks_of(q)
            pe.wait_ge(k_out, q * 2 + w)
            for m in range(w):
                pe.wait_ge(v_out, q * 2 + m + 1)
                for c in range(IC):
                    ins = t_.matmul(dots_ps[:, c * P:(c + 1) * P], v_sb[:, m, c * P:(c + 1) * P],
                                    k_sb[:, m, c * P:(c + 1) * P], start=False, stop=(w == 1 and c == IC - 1))
            ins.then_inc(dots_done, 1)

        def mix():
            pe.wait_ge(bd_set, 1)
            for c in range(IC):
                ins = t_.matmul(kv_ps[0][c // 2][:, c % 2 * D:(c % 2 + 1) * D], bd_sb[:, c, :], woutT[:, c, :],
                                start=True, stop=True)
            ins.then_inc(r_ready, 1)
            pe.wait_ge(r_out, 1)
            for d in range(DC):
                for c in range(IC):
                    ins = t_.matmul(m_ps[:, d * D:(d + 1) * D], wq[:, c, d * P:(d + 1) * P], r_sb[:, c, :],
                                    start=(c == 0), stop=(c == IC - 1))
            ins.then_inc(m_ready, 1)
            pe.wait_ge(m_out, 1)

        def fin_rows(q):
            w = blocks_of(q)
            if not first_pair(q):
                count(q - 1)
            pe.wait_ge(xT_ld, (q + 1) * 16)
            for m in range(w):
                t_.matmul(mix_ps[:, m, :], ones[0:1, :], b_out_row[:, :], start=True, stop=False)
                for c in range(DC):
                    ins = t_.matmul(mix_ps[:, m, :], xnT_t[:, m, c * P:(c + 1) * P], mix_m[:, c, :], start=False,
                                    stop=(c == DC - 1))
            ins.then_inc(fin_mix, 1)
            pe.wait_ge(fin_aggs, q + 1)
            for m in range(w):
                ins = transpose2(tp_ps[:, m * D:(m + 1) * D], agg_s[:, m, :])
            ins.then_inc(fin_aggT, 1)
            for m in range(w):
                t_.matmul(g_ps[:, m, :], ones[0:1, :], gnn_b_row[:, :], start=True, stop=False)
                if m == 0:
                    pe.wait_ge(fin_aggT_out, q + 1)
                for c in range(DC):
                    ins = t_.matmul(g_ps[:, m, :], aggT[:, m, c * P:(c + 1) * P], gnn_w_sb[:, c, :], start=False,
                                    stop=(c == DC - 1))
            ins.then_inc(fin_g, 1)

        def fin_norm(q):
            w = blocks_of(q)
            if not first_pair(q):
                place(q - 1)
            pe.wait_ge(fin_xn2, q + 1)
            for m in range(w):
                ins = transpose2(xn2T_ps[:, m * D:(m + 1) * D], tok_t[:, m, :])
            ins.then_inc(fin_xn2T, 1)
            for m in range(w):
                t_.matmul(gate_ps[:, m, :], ones[0:1, :], gate_b_row[:, :], start=True, stop=False)
                if m == 0:
                    pe.wait_ge(fin_xn2T_out, q + 1)
                for c in range(DC):
                    ins = t_.matmul(gate_ps[:, m, :], xn2T[:, m, c * P:(c + 1) * P], gate_w_sb[:, c, :], start=False,
                                    stop=(c == DC - 1))
            ins.then_inc(fin_gate, 1)

        def count(q):
            w = blocks_of(q)
            pe.wait_ge(route_hot, q + 1)
            for m in range(w):
                t_.matmul(cum_ps[:, m, :], utri[:, :], r_hot[:, m, :], start=True, stop=False)
                if m:
                    t_.matmul(cum_ps[:, m, :], ones[:, :], r_hot[:, 0, :], start=False, stop=False)
                ins = t_.matmul(cum_ps[:, m, :], ones[:, :], routed[:, :], start=False, stop=True)
            ins.then_inc(route_cum, 1)

        def place(q):
            w = blocks_of(q)
            pe.wait_ge(slot_hot, q + 1)
            for m in range(w):
                ins = t_.matmul(inv_ps, low_hot[m], high_val[m], start=False, stop=(w == 1))
            ins.then_inc(slot_used, 1)

        def route(q):
            count(q)
            place(q)
            t_.matmul(cum_ps[:, 1, :], ones[:, :], routed[:, :], start=True, stop=True).then_inc(route_cum, 1)

        main_phase(pe, gnn, kv_rows, kv_sums, mix, fin_rows, fin_norm, route)

        def rows_T(e, k):
            pe.wait_ge(gx_in[k], (e - k + 2) // 2 * (16 * CT) if isinstance(e, int) else (e - k + 2) * (8 * CT))
            for p in range(XG2):
                for i in range(2):
                    for c in range(DC):
                        ins = t_.transpose(bank[4 + p][:, c * 2 * P + i * P:c * 2 * P + (i + 1) * P],
                                           gx[k][:, 2 * p + i, c * P:(c + 1) * P], ident[:, :])
                ins.then_inc(xT_ready, 1)

        def expert(e, k, more):
            pe.wait_ge(xT_lo_set, (e + 1) * XG2)
            pe.wait_ge(w1_lo_set, e + 1)
            count = filled(e, pe)

            def up(g):
                at = columns(g)
                w = at.stop - at.start
                for f in range(FC):
                    fs = slice(f * P, (f + 1) * P)
                    pe.wait_ge(hid_full_set, e * UPS + g * FC + f + 1)
                    for c in range(DC):
                        t_.matmul(bank[f % 4][:, 0:w], w1_hi[:, c, fs], xT_hi[:, c, at], start=(c == 0), stop=False)
                        t_.matmul(bank[f % 4][:, 0:w], w1_hi[:, c, fs], xT_lo[:, c, at], start=False, stop=False)
                        ins = t_.matmul(bank[f % 4][:, 0:w], w1_lo[:, c, fs], xT_hi[:, c, at], start=False,
                                        stop=(c == DC - 1))
                    ins.then_inc(up_ready, 1)

            def down(g):
                pe.wait_ge(hid_lo_set, e * UPS + (g + 1) * FC + 2)
                for c in range(GROUPS[g][0], sum(GROUPS[g])):
                    w = min(P, CAP - c * P)
                    at = slice(c * P, c * P + w)
                    if c < 2 and more:
                        pe.wait_ge(xT_lo_set, (e + 1) * XG2 + c + 1)
                    pe.wait_ge(y_read, e * CT + c + 1)
                    y_ps = bank[4 + c % 2][0:w, 0:D]
                    for f in range(FC):
                        t_.matmul(y_ps, hid_hi[:, f, at], w2_hi[:, f, :], start=(f == 0), stop=False)
                        t_.matmul(y_ps, hid_hi[:, f, at], w2_lo[:, f, :], start=False, stop=False)
                        ins = t_.matmul(y_ps, hid_lo[:, f, at], w2_hi[:, f, :], start=False, stop=(f == FC - 1))
                    ins.then_inc(down_ready, 1)

            for g in range(len(GROUPS)):
                if_filled(pe, count, g, lambda: up(g), ((up_ready, e * UPS + g * FC, FC),))
            if more:
                pe.wait_ge(y_read, e * CT + 2)
                rows_T(e + 1, 1 - k)
            pe.wait_ge(w2_lo_set, e * 2 + 2)
            for g, (t0, n) in enumerate(GROUPS):
                if_filled(pe, count, g, lambda: down(g), ((down_ready, e * CT + t0, n),))

        rows_T(0, 0)
        each_expert(pe, expert)

    @block.vector
    def _(dve):
        v_ = nc.vector
        n_pre = [0]

        def link(ins):
            n_pre[0] += 1
            ins.then_inc(dve_pre, 1)
            dve.wait_ge(dve_pre, n_pre[0])

        v_.memset(blk_base[:, :], 0.0).then_inc(base_set, 1)
        dve.wait_ge(src_in, 48)
        v_.tensor_copy(src_raw, src_raw.bitcast(I32)).then_inc(edges_f[0], 1)
        dve.wait_ge(edges_T, 1)
        for q in range(4):
            w = min(512, EN - q * 512)
            ins = v_.tensor_copy(src_idx[:, q * 512:q * 512 + w], bank[q][:, 0:w])
        ins.then_inc(idx_set, 1)
        dve.wait_ge(idx_set, 1)
        lo_i = src_raw.rearrange("p c j -> p (c j)").bitcast(I32)
        v_.tensor_scalar(hi_i, src_idx[:, :], LOW.bit_length() - 1, None, ALU.logical_shift_right).then_inc(hi_set, 1)
        link(v_.tensor_scalar(lo_i, src_idx[:, :], LOW - 1, None, ALU.bitwise_and))
        link(v_.tensor_copy(lo16, lo_i))
        dve.wait_ge(consts, 15)
        dve.wait_ge(hi16_set, 1)

        def hot(s, k):
            dve.wait_ge(hot_used, s + 1)
            v_.tensor_tensor(oh_lo[k], iota_e[:, 0:LOW, :], lo16[:, ds(s * HT, HT)].unsqueeze(1).to_broadcast([P, LOW, HT]),
                             ALU.is_equal)
            v_.tensor_tensor(oh_hi[k], iota_e, hi16[:, ds(s * HT, HT)].unsqueeze(1).to_broadcast([P, HIGH, HT]),
                             ALU.is_equal).then_inc(hot_ready, 1)

        with dve.Fori(0, LN_AT) as i:
            for k in range(2):
                hot(i * 2 + k, k)
        dve.wait_ge(ln_var, 1)
        link(v_.reciprocal(ln_rs[:, :], ln_sd[:, :]))
        v_.tensor_tensor(ln_nb[:, :], ln_nm[:, :], ln_rs[:, :], ALU.mult).then_inc(ln_bias, 1)
        dve.wait_ge(bounds_b, 1)
        before = reg_e[0:64, 3840:3840 + NU - 1]
        v_.tensor_scalar(before, bank[4][0:64, 0:NU - 1], block_edge[:, :], None, ALU.is_lt).then_inc(bounds_c, 1)
        dve.wait_ge(bounds_c, 1)
        v_.tensor_reduce(out=t0_col[:, :], in_=before, op=ALU.add, axis=AX.X).then_inc(bounds_c, 1)
        with dve.Fori(LN_AT, HS // 2) as i:
            for k in range(2):
                hot(i * 2 + k, k)
        hot(HS - 1, 0)
        dve.wait_ge(hist_done, 1)
        v_.tensor_copy(hist_sb[:, :], hist_ps).then_inc(hist_out, 1)
        dve.wait_ge(deg_ready, 1)
        v_.tensor_scalar(deg[:, :], deg_ps, 1.0, None, ALU.max).then_inc(deg_set, 1)
        dve.wait_ge(deg_rt, 1)
        v_.reciprocal(deg_rs[:, :], deg_sd[:, :]).then_inc(deg_ok, 1)
        dve.wait_ge(deg_ok, 1)
        dve.wait_ge(bounds_T, 1)
        v_.tensor_copy(first_u[:, :], bank[5][0:1, 0:64]).then_inc(bounds_set, 1)
        for t in range(NB):
            dve.wait_ge(h_hi, t + 1)
            v_.scalar_tensor_tensor(h_all[:, t, D:2 * D], xn_all[:, t, :], deg_rs[:, t:t + 1], h_all[:, t, 0:D],
                                    ALU.mult, ALU.subtract).then_inc(h_lo, 1)
        dve.wait_ge(wT_out, 4)
        groups = wkvT[:, :, :].rearrange("p c (h d) -> p (c h) d", d=DH)
        link(v_.tensor_reduce(out=kv_mean, in_=groups, op=ALU.add, axis=AX.X))
        link(v_.tensor_scalar(kv_mean, kv_mean, 1.0 / DH, None, ALU.mult))
        v_.tensor_tensor(groups, groups, kv_mean.unsqueeze(2).to_broadcast([P, 2 * DC * H, DH]), ALU.subtract
                         ).then_inc(wkv_set, 1)
        dve.wait_ge(bounds_set, 1)
        dve.wait_ge(h_out, 16 * 5)
        v_.memset(routed[:, :], 0.0).then_inc(base_set, 1)

        def visit(u, v):
            slot = dve.snap(v % HOTS)
            dve.wait_ge(hots_used, v + 1)
            rel = dst_rel[:, ds(slot, 1), :].rearrange("p a t -> p (a t)")
            v_.tensor_scalar(rel, dst_f[:, ds(u * UT, UT)], blk_base[:, :], None, ALU.subtract).then_inc(rel_set, 1)
            dve.wait_ge(rel_set, v + 1)
            v_.tensor_tensor(S[:, ds(slot * (P * UT), P * UT)].rearrange("p (n j) -> p n j", j=UT), iota_4[:, :, :],
                             rel.unsqueeze(1).to_broadcast([P, P, UT]), ALU.is_equal).then_inc(hots_ready, 1)

        def gnn(b):
            u0 = dve.value_load(first_u[0:1, ds(b, 1)], min_val=0, max_val=NU - 1)
            u1 = dve.value_load(first_u[0:1, ds(b + 1, 1)], min_val=0, max_val=NU - 1)
            dve.wait_ge(base_set, b + 2)
            apart(dve)
            with dve.If(u0 < u1):
                with dve.Fori(u0, u1) as u:
                    visit(u, u + b)
            visit(u1, u1 + b)
            v_.tensor_scalar(blk_base[:, :], blk_base[:, :], float(P), None, ALU.add).then_inc(base_set, 1)

        def kv_rows(q):
            pass

        def kv_sums(q):
            w = blocks_of(q)
            for m in range(w):
                dve.wait_ge(kv_sq, q * 2 + m + 1)
                ins = v_.tensor_reduce(out=kv_var[:, m * 2 * H:(m + 1) * 2 * H],
                                       in_=sq[:, m, :].rearrange("p (g d) -> p g d", d=DH), op=ALU.add, axis=AX.X)
            ins.then_inc(kv_dve, 1)
            dve.wait_ge(kv_root, q + 1)
            v_.reciprocal(kv_rs[:, 0:w * 2 * H], kv_sd[:, 0:w * 2 * H]).then_inc(kv_v, 1)
            dve.wait_ge(kv_v, q * 2 + 1)
            rs = kv_rs.rearrange("p (m g h) -> p m g h", m=2, g=2)
            v_.tensor_tensor(kv_sc.rearrange("p (m h) -> p m h", m=2)[:, 0:w, :], rs[:, 0:w, 0, :], rs[:, 0:w, 1, :],
                             ALU.mult).then_inc(kv_v, 1)
            dve.wait_ge(kv_v, q * 2 + 2)
            dve.wait_ge(dots_done, q + 1)
            for m in range(w):
                v_.tensor_tensor(v_sb[:, m, :].rearrange("p (h d) -> p h d", d=DH),
                                 kv_ps[m][1][:, :].rearrange("p (h d) -> p h d", d=DH),
                                 kv_sc[:, m * H:(m + 1) * H].unsqueeze(2).to_broadcast([P, H, DH]), ALU.mult
                                 ).then_inc(v_out, 1)

        def mix():
            dve.wait_ge(dots_done, NQ + 2)
            v_.memset(bd_sb, 0.0).then_inc(bd_zero, 1)
            dve.wait_ge(bd_zero, 1)
            for half in range(2):
                r = slice(half * DH, (half + 1) * DH)
                ins = v_.tensor_copy(bd_sb[r, :, r], dots_ps[r, :].rearrange("p (c d) -> p c d", c=IC)[:, :, r])
            ins.then_inc(bd_set, 1)
            v_.memset(gx[0], 0.0).then_inc(gx_zero, 1)

        n = [0]

        def step(ins, q):
            n[0] += 1
            ins.then_inc(fin_dve, 1)
            dve.wait_ge(fin_dve, q * FIN_STEPS + n[0])

        def fin_rows(q):
            w = blocks_of(q)
            n[0] = 0
            agg = agg_all[:, ds(q * 2, w), :]
            dve.wait_ge(agg_out, q * 2 + w + 1)
            v_.tensor_scalar(f_deg[:, 0:w], agg[:, :, D], 1.0, None, ALU.max).then_inc(fin_deg, 1)
            dve.wait_ge(fin_sd, q + 1)
            step(v_.reciprocal(f_rin[:, 0:w], f_sd[:, 0:w]), q)
            for m in range(w):
                ins = v_.tensor_scalar(agg_s[:, m, :], agg[:, m, 0:D], f_rin[:, m:m + 1], None, ALU.mult)
            ins.then_inc(fin_aggs, 1)

        def fin_norm(q):
            w = blocks_of(q)
            n[0] = 1
            if not first_pair(q):
                route(q - 1, q)
            n[0] = 1 + ROUTE_STEPS
            if first_pair(q):
                dve.sem_inc(fin_dve, ROUTE_STEPS)
            dve.wait_ge(x_ld, (q + 1) * 16)
            dve.wait_ge(fin_mix, q + 1)
            step(v_.tensor_tensor(mixed[:, 0:w, :], x_t[:, 0:w, :], mix_ps[:, 0:w, :], ALU.add), q)
            dve.wait_ge(fin_nr, q + 1)
            step(v_.tensor_scalar(f_nc[:, 0:w], f_nr[:, 0:w], 1e-12, None, ALU.max), q)
            step(v_.reciprocal(f_rn[:, 0:w], f_nc[:, 0:w]), q)
            for m in range(w):
                ins = v_.scalar_tensor_tensor(tok_t[:, m, D:2 * D], relu_h[:, m, :], f_rn[:, m:m + 1], mixed[:, m, :],
                                              ALU.mult, ALU.add)
            step(ins, q)
            for m in range(w):
                ins = v_.bn_stats(f_bn[m], tok_t[:, m, D:2 * D])
            step(ins, q)
            apart(dve)
            for m in range(w):
                ins = v_.bn_aggr(f_mv[:, m, :], f_bn[m])
            ins.then_inc(fin_var, 1)
            dve.wait_ge(fin_sd2, q + 1)
            step(v_.reciprocal(f_rstd[:, 0:w], f_sd2[:, 0:w]), q)
            for m in range(w):
                ins = v_.tensor_scalar(tok_t[:, m, 0:D], tok_t[:, m, D:2 * D], f_mv[:, m, 0:1], f_rstd[:, m:m + 1],
                                       ALU.subtract, ALU.mult)
            ins.then_inc(fin_xn2, 1)
            dve.wait_ge(fin_gate, q + 1)
            logits, diff, eq, hot = (b_[:, 0:w, :] for b_ in (r_log, r_diff, r_eq, r_hot))
            top, first = r_top[:, 0:w], r_first[:, 0:w]
            step(v_.tensor_copy(logits, gate_ps[:, 0:w, :]), q)
            step(v_.tensor_reduce(out=top, in_=logits, op=ALU.max, axis=AX.X), q)
            v_.tensor_tensor(diff, logits, top.unsqueeze(2).to_broadcast([P, w, NE]), ALU.subtract).then_inc(route_d, 1)
            dve.wait_ge(route_d, q + 1)
            step(v_.tensor_scalar(eq, diff, 0.0, None, ALU.is_equal), q)
            rev = rev_8[:, :].unsqueeze(1).to_broadcast([P, w, NE])
            step(v_.tensor_tensor(eq, eq, rev, ALU.mult), q)
            step(v_.tensor_reduce(out=first, in_=eq, op=ALU.max, axis=AX.X), q)
            ins = v_.tensor_tensor(hot, rev, first.unsqueeze(2).to_broadcast([P, w, NE]), ALU.is_equal)
            if w == 1:
                step(ins, q)
                ins = v_.tensor_scalar(hot[:, 0, :], hot[:, 0, :], valid[:, :], None, ALU.mult)
            ins.then_inc(route_hot, 1)
            assert n[0] == FIN_STEPS or w == 1, n

        def route(p, q):
            w = blocks_of(p)
            top, first, sums, prb, pos, drop, base, place, low, high, slot, low_i, high_i = (b_[:, 0:w] for b_ in (
                r_top, r_first, r_sum, r_prb, r_pos, r_drop, r_base, r_place, r_low, r_high, r_slot, r_low_i, r_high_i))
            hot, mine = r_hot[:, 0:w, :], r_cum[:, 0:w, :]
            dve.wait_ge(route_exp, p + 1)
            step(v_.tensor_reduce(out=sums, in_=r_exp[:, 0:w, :], op=ALU.add, axis=AX.X), q)
            step(v_.reciprocal(prb, sums), q)
            if w == 1:
                step(v_.tensor_scalar(prb, prb, valid[:, :], None, ALU.mult), q)
                step(v_.tensor_scalar(node_1[:, NB - 1:NB], node_1[:, NB - 1:NB], valid[:, :], None, ALU.mult), q)
            dve.wait_ge(route_cum, p + 1)
            step(v_.tensor_tensor(mine, cum_ps[:, 0:w, :], hot, ALU.mult), q)
            for m in range(w):
                step(v_.tensor_tensor(routed[:, :], routed[:, :], hot[:, m, :], ALU.add), q)
            step(v_.tensor_reduce(out=pos, in_=mine, op=ALU.add, axis=AX.X), q)
            v_.tensor_scalar(base, first, -float(CROWS), float(NE * CROWS - 1), ALU.mult, ALU.add)
            step(v_.tensor_scalar(drop, pos, float(CAP), float(2 * NE * CROWS), ALU.is_gt, ALU.mult), q)
            step(v_.tensor_tensor(place, base, pos, ALU.add), q)
            step(v_.tensor_tensor(slot, place, drop, ALU.add), q)
            v_.tensor_scalar(low_i, slot, P - 1, None, ALU.bitwise_and)
            step(v_.tensor_scalar(high_i, slot, 7, None, ALU.arith_shift_right), q)
            v_.tensor_copy(low, low_i)
            step(v_.tensor_copy(high, high_i), q)
            dve.wait_ge(slot_used, p + 1)
            for m in range(w):
                node = node_1[:, ds(p * 2 + m, 1)]
                v_.tensor_scalar(low_hot[m], iota_128[:, :], low[:, m:m + 1], None, ALU.is_equal)
                v_.tensor_scalar(high_val[m][:, 0:NE * CT], iota_64[:, :], high[:, m:m + 1], node, ALU.is_equal, ALU.mult)
                ins = v_.tensor_scalar(high_val[m][:, NE * CT:2 * NE * CT], iota_64[:, :], high[:, m:m + 1],
                                       prb[:, m:m + 1], ALU.is_equal, ALU.mult)
            ins.then_inc(slot_hot, 1)

        main_phase(dve, gnn, kv_rows, kv_sums, mix, fin_rows, fin_norm, lambda q: route(q, q))

        dve.wait_ge(slot_used, NQ + 2)
        n_inv = [0]

        def chain(ins):
            n_inv[0] += 1
            ins.then_inc(inv_dve, 1)
            dve.wait_ge(inv_dve, n_inv[0])

        in_slot = inv_ps[:, 0:NE * CT]
        chain(v_.tensor_copy(slot_prb[:, :], inv_ps[:, NE * CT:2 * NE * CT]))
        chain(v_.tensor_scalar(inv_m[:, :], in_slot, 0.0, float(2 * N), ALU.is_equal, ALU.mult))
        chain(v_.tensor_scalar(inv_f[:, :], in_slot, -1.0, None, ALU.add))
        dve.wait_ge(route_cum, NQ + 2)
        chain(v_.tensor_copy(tokens[:, :], cum_ps[0:1, 1, :]))
        v_.tensor_tensor(inv_i[:, :], inv_f[:, :], inv_m[:, :], ALU.add).then_inc(inv_set, 1)
        dve.wait_ge(idx_next, NU // RING // 2 * 2 + 1)
        for k in range(2):
            chain(v_.memset(y_out[k], 0.0))

        def low_rows(e):
            for p in range(XG2):
                at = slice(p * 2 * P, (p + 1) * 2 * P)
                dve.wait_ge(xT_hi_set, e * XG2 + p + 1)
                v_.tensor_tensor(xT_lo[:, :, at], bank[4 + p][:, :].rearrange("p (c n) -> p c n", c=DC),
                                 xT_hi[:, :, at].bitcast(F32), ALU.subtract).then_inc(xT_lo_set, 1)

        dve.sem_inc(hid_lo_set, 2)
        dve.sem_inc(y_read, 2)
        dve.wait_ge(w1_hi_set, 1)
        v_.tensor_tensor(w1_lo[:, :, :], w1_raw, w1_hi[:, :, :].bitcast(F32), ALU.subtract).then_inc(w1_lo_set, 1)
        low_rows(0)

        def expert(e, k, more):
            count = filled(e, dve)

            def low_hidden(g):
                at = columns(g)
                for f in range(FC):
                    dve.wait_ge(hid_hi_set, e * UPS + g * FC + f + 1)
                    v_.tensor_tensor(hid_lo[:, f, at], hid_full[f % 2][:, 0:at.stop - at.start],
                                     hid_hi[:, f, at].bitcast(F32), ALU.subtract).then_inc(hid_lo_set, 1)
                    if g == 0 and f in (1, 3):
                        half = slice((f // 2) * (FC // 2), (f // 2 + 1) * (FC // 2))
                        dve.wait_ge(w2_hi_set, e + 1)
                        v_.tensor_tensor(w2_lo[:, half, :], w2_raw[:, half, :], w2_hi[:, half, :].bitcast(F32),
                                         ALU.subtract).then_inc(w2_lo_set, 1)

            def fix(c):
                t = e * CT + c
                w = min(P, CAP - c * P)
                m = [0]

                def step(ins):
                    m[0] += 1
                    ins.then_inc(y_dve, 1)
                    dve.wait_ge(y_dve, t * Y_STEPS + m[0])

                if c or not isinstance(e, int) or e > 0:
                    dve.wait_ge(y_fixed, t)
                dve.wait_ge(y_scaled, t + 1)
                apart(dve)
                y, zero, z = (b_[c % 2][0:w, :] for b_ in (y_sb, y_zero, y_out))
                fine, nan = y_fine[0:w, :], y_nan[0:w, :]
                v_.tensor_scalar(fine, zero, 0.0, None, ALU.is_equal)
                v_.tensor_tensor(nan, y, y, ALU.not_equal)
                if c >= 2 or not isinstance(e, int) or e > 0:
                    dve.wait_ge(y_st[c % 2], e * (8 * CT) + c // 2 * 16)
                    apart(dve)
                step(v_.tensor_scalar(z, y, 1e4, -1e4, ALU.min, ALU.max))
                apart(dve)
                step(v_.copy_predicated(z, fine, y))
                apart(dve)
                v_.copy_predicated(z, nan, zeros32[0:w, :]).then_inc(y_fixed, 1)

            def rows(g):
                t0, n = GROUPS[g]
                for c in range(t0, t0 + n + 1):
                    if c < t0 + n:
                        t = e * CT + c
                        w = min(P, CAP - c * P)
                        dve.wait_ge(down_ready, t + 1)
                        v_.tensor_tensor(y_sum[c % 2][0:w, :], bank[4 + c % 2][0:w, 0:D], b2_all[k][0:w, :], ALU.add
                                         ).then_inc(y_read, 1)
                    if c > t0:
                        fix(c - 1)

            for g in range(len(GROUPS)):
                if_filled(dve, count, g, lambda: low_hidden(g), ((hid_lo_set, e * UPS + (g * FC + 2), FC),))
            if more:
                low_rows(e + 1)
            dve.wait_ge(b2_in[k], (e // 2 + 1) * 16 if isinstance(e, int) else (e - k + 2) * 8)
            for g, (t0, n) in enumerate(GROUPS):
                if_filled(dve, count, g, lambda: rows(g), (
                    (y_read, e * CT + (t0 + 2), n), (y_dve, (e * CT + t0) * Y_STEPS, n * Y_STEPS),
                    (y_fixed, e * CT + t0, n)))

        each_expert(dve, expert)


_INS = ['x', 'src', 'dst', 'L0_gnn_W', 'L0_gnn_b', 'L0_mix_w_qkv', 'L0_mix_w_out', 'L0_mix_b_out',
        'L0_ffn_gate_w', 'L0_ffn_gate_b', 'L0_ffn_w1', 'L0_ffn_b1', 'L0_ffn_w2', 'L0_ffn_b2']


def kernel(**inputs):
    import numpy as _np
    import concourse.bacc as _bacc
    from concourse.bass_utils import run_bass_kernel_spmd as _run

    nc = _bacc.Bacc("TRN2", target_bir_lowering=False, num_devices=1)
    arrays, args = {}, []
    for name in _INS:
        a = _np.ascontiguousarray(inputs[name])
        arrays[f"in_{name}"] = a
        args.append(nc.dram_tensor(f"in_{name}", a.shape, mybir.dt.from_np(a.dtype), kind="ExternalInput").ap())
    args.append(nc.dram_tensor("out_0", (N, D), F32, kind="ExternalOutput").ap())
    build(nc, *args)
    r = _run(nc, [arrays], core_ids=[0])
    return r.results[0]["out_0"]
```
